# Optimizing a Trainium2 kernel written in Bass

```python
import numpy as np
import jax
import jax.numpy as jnp

def _softmax(x, axis=-1):
    return jax.nn.softmax(x, axis=axis)

def _gelu(x):
    return jax.nn.gelu(x, approximate=True)

def _silu(x):
    return jax.nn.silu(x)

def _sigmoid(x):
    return jax.nn.sigmoid(x)

def _layernorm(x, axis=-1, eps=1e-05):
    m = jnp.mean(x, axis=axis, keepdims=True)
    v = jnp.var(x, axis=axis, keepdims=True)
    return (x - m) / jnp.sqrt(v + eps)

def _scatter_add(tgt, idx, src, axis=0):
    return tgt.at[idx].add(src)

def _segment_sum(src, seg, n):
    return jax.ops.segment_sum(src, seg, n)
kernel_name = 'mk_xattn_ffn_d2_seqx_r4_46dfd6'

def setup_inputs(seed: int=0):
    np.random.seed(seed)
    _w = jnp.asarray

    def _rec_inputs():
        import jax
        import jax.numpy as jnp
        _rk = jax.random.key(seed)
        x = -0.000125 + 0.9999 * jax.random.normal(jax.random.fold_in(_rk, 1), (2, 1024, 256), jnp.float32)
        _lenS = 1024 - jax.random.randint(jax.random.fold_in(_rk, 7), (2,), 0, max(1, 1024 // 4) + 1, jnp.int32)
        _lenS2 = 77 - jax.random.randint(jax.random.fold_in(_rk, 8), (2,), 0, max(1, 77 // 4) + 1, jnp.int32)
        _ctx_768P = jax.random.normal(jax.random.fold_in(_rk, 11), (2, 16, 192), jnp.float32)
        _ctx_768c = jax.random.dirichlet(jax.random.fold_in(_rk, 511), 0.3 * jnp.ones((16,), jnp.float32), (2, 77))
        _ctx_768t = jnp.einsum('bsk,bkd->bsd', _ctx_768c, _ctx_768P)
        _ctx_768t = _ctx_768t * jax.lax.rsqrt(jnp.mean(jnp.square(_ctx_768t)) + 1e-12) * 0.953939
        ctx_768 = 0.00243539 + 0.99952 * (_ctx_768t + 0.3 * jax.random.normal(jax.random.fold_in(_rk, 611), (2, 77, 192), jnp.float32))
        return (x, ctx_768)
    x, ctx_768 = _rec_inputs()

    def _L0_xattn_setup():
        import jax, jax.numpy as jnp
        import numpy as np
        HEADS = 16
        DIM_HEAD = 64
        RANK = 32
        LORA_W = 1.0
        IPA_SCALE = 1.0
        IPA_TOKENS = 4
        SCALE = DIM_HEAD ** (-0.5)

        def _split_heads(t):
            b, n, _ = t.shape
            return t.reshape(b, n, HEADS, DIM_HEAD).transpose(0, 2, 1, 3)

        def _merge_heads(t):
            b, h, n, d = t.shape
            return t.transpose(0, 2, 1, 3).reshape(b, n, h * d)

        def _attention(q_in, k_in, v_in):
            q = _split_heads(q_in)
            k = _split_heads(k_in)
            v = _split_heads(v_in)
            s = jnp.einsum('bhid,bhjd->bhij', q, k) * SCALE
            p = jax.nn.softmax(s, axis=-1)
            o = jnp.einsum('bhij,bhjd->bhid', p, v)
            return _merge_heads(o)

        def _lora(t, down, up, alpha):
            return t @ down @ up * (LORA_W * alpha[0] / RANK)
        key = jax.random.key(seed)
        ks = jax.random.split(key, 20)
        B, N, QD, CD, ID = (8, 1024, 256, 192, HEADS * DIM_HEAD)
        CTX = 77 + IPA_TOKENS
        s = 0.02
        return {'x': jax.random.normal(ks[0], (B, N, QD), jnp.float32), 'context': jax.random.normal(ks[1], (B, CTX, CD), jnp.float32), 'Wq': jax.random.normal(ks[2], (QD, ID), jnp.float32) * s, 'Wk': jax.random.normal(ks[3], (CD, ID), jnp.float32) * s, 'Wv': jax.random.normal(ks[4], (CD, ID), jnp.float32) * s, 'Wo': jax.random.normal(ks[5], (ID, QD), jnp.float32) * s, 'bo': jnp.zeros((QD,), jnp.float32), 'q_down': jax.random.normal(ks[6], (QD, RANK), jnp.float32) * s, 'q_up': jax.random.normal(ks[7], (RANK, ID), jnp.float32) * s, 'q_alpha': jnp.ones((1,), jnp.float32) * RANK, 'k_down': jax.random.normal(ks[8], (CD, RANK), jnp.float32) * s, 'k_up': jax.random.normal(ks[9], (RANK, ID), jnp.float32) * s, 'k_alpha': jnp.ones((1,), jnp.float32) * RANK, 'v_down': jax.random.normal(ks[10], (CD, RANK), jnp.float32) * s, 'v_up': jax.random.normal(ks[11], (RANK, ID), jnp.float32) * s, 'v_alpha': jnp.ones((1,), jnp.float32) * RANK, 'o_down': jax.random.normal(ks[12], (ID, RANK), jnp.float32) * s, 'o_up': jax.random.normal(ks[13], (RANK, QD), jnp.float32) * s, 'o_alpha': jnp.ones((1,), jnp.float32) * RANK, 'Wk_ipa': jax.random.normal(ks[14], (CD, ID), jnp.float32) * s, 'Wv_ipa': jax.random.normal(ks[15], (CD, ID), jnp.float32) * s}
    _L0_xattn_all = _L0_xattn_setup()
    _L0_xattn_in = {k: v for k, v in _L0_xattn_all.items() if k in ('Wq', 'Wk', 'Wv', 'Wo', 'bo', 'q_down', 'q_up', 'q_alpha', 'k_down', 'k_up', 'k_alpha', 'v_down', 'v_up', 'v_alpha', 'o_down', 'o_up', 'o_alpha', 'Wk_ipa', 'Wv_ipa')}
    del _L0_xattn_all

    def _L0_ffn_setup():
        import jax, jax.numpy as jnp
        import numpy as np
        B, T, C = (2, 128, 256)
        I = 1024
        E = 8
        K = 2
        key = jax.random.key(seed)
        ks = jax.random.split(key, 8)
        s = 0.02
        return {'x': jax.random.normal(ks[0], (B, T, C), jnp.float32), 'Wr1': jax.random.normal(ks[1], (C, C // 4), jnp.float32) * s, 'br1': jnp.zeros((C // 4,), jnp.float32), 'Wr2': jax.random.normal(ks[2], (C // 4, E), jnp.float32) * s, 'br2': jnp.zeros((E,), jnp.float32), 'Ws1': jax.random.normal(ks[3], (C, I), jnp.float32) * s, 'bs1': jnp.zeros((I,), jnp.float32), 'Ws2': jax.random.normal(ks[4], (I, C), jnp.float32) * s, 'bs2': jnp.zeros((C,), jnp.float32), 'We1': jax.random.normal(ks[5], (E, C, I), jnp.float32) * s, 'be1': jnp.zeros((E, I), jnp.float32), 'We2': jax.random.normal(ks[6], (E, I, C), jnp.float32) * s, 'be2': jnp.zeros((E, C), jnp.float32)}
    _L0_ffn_all = _L0_ffn_setup()
    _L0_ffn_in = {k: v for k, v in _L0_ffn_all.items() if k in ('Wr1', 'br1', 'Wr2', 'br2', 'Ws1', 'bs1', 'Ws2', 'bs2', 'We1', 'be1', 'We2', 'be2')}
    del _L0_ffn_all

    def _L1_xattn_setup():
        import jax, jax.numpy as jnp
        import numpy as np
        import math
        N_HEADS = 8
        D_EMBED = 256
        D_CROSS = 192
        D_HEAD = D_EMBED // N_HEADS
        key = jax.random.key(seed)
        ks = jax.random.split(key, 10)
        B, S, SKV = (4, 768, 259)
        s_e = 1.0 / math.sqrt(D_EMBED)
        s_c = 1.0 / math.sqrt(D_CROSS)
        return {'x': jax.random.normal(ks[0], (B, S, D_EMBED), jnp.float32), 'y': jax.random.normal(ks[1], (B, SKV, D_CROSS), jnp.float32), 'Wq': jax.random.normal(ks[2], (D_EMBED, D_EMBED), jnp.float32) * s_e, 'bq': jnp.zeros((D_EMBED,), jnp.float32), 'Wk': jax.random.normal(ks[3], (D_EMBED, D_CROSS), jnp.float32) * s_c, 'bk': jnp.zeros((D_EMBED,), jnp.float32), 'Wv': jax.random.normal(ks[4], (D_EMBED, D_CROSS), jnp.float32) * s_c, 'bv': jnp.zeros((D_EMBED,), jnp.float32), 'Wo': jax.random.normal(ks[5], (D_EMBED, D_EMBED), jnp.float32) * s_e, 'bo': jnp.zeros((D_EMBED,), jnp.float32)}
    _L1_xattn_all = _L1_xattn_setup()
    _L1_xattn_in = {k: v for k, v in _L1_xattn_all.items() if k in ('Wq', 'bq', 'Wk', 'bk', 'Wv', 'bv', 'Wo', 'bo')}
    del _L1_xattn_all

    def _L1_ffn_setup():
        import jax, jax.numpy as jnp
        import numpy as np
        D, H, E, K = (256, 256, 8, 2)

        def _moe(x, router_w, w_in, b_in, w_out, b_out):
            B, S, Dm = x.shape
            T = B * S
            x2 = x.reshape(T, Dm)
            logits = x2 @ router_w
            probs = jax.nn.softmax(logits, axis=-1)
            top_p, top_e = jax.lax.top_k(probs, K)
            flat_e = top_e.reshape(-1)
            flat_p = top_p.reshape(-1)
            tok = jnp.repeat(jnp.arange(T), K)
            order = jnp.argsort(flat_e)
            se, sp, st = (flat_e[order], flat_p[order], tok[order])
            xd = x2[st]
            N = xd.shape[0]
            h = jnp.zeros((N, H), x.dtype)
            for e in range(E):
                m = (se == e)[:, None]
                h = h + jnp.where(m, jax.nn.gelu(xd @ w_in[e] + b_in[e]), 0.0)
            y = jnp.zeros((N, Dm), x.dtype)
            for e in range(E):
                m = (se == e)[:, None]
                y = y + jnp.where(m, h @ w_out[e] + b_out[e], 0.0)
            y = y * sp[:, None]
            out = jnp.zeros((T, Dm), x.dtype).at[st].add(y)
            return out.reshape(B, S, Dm)
        key = jax.random.key(seed)
        ks = jax.random.split(key, 5)
        s = lambda k, shape, scale: jax.random.normal(k, shape, dtype=jnp.float32) * scale
        return {'input_batch': s(ks[0], (2, 128, D), 1.0), 'router_w': s(ks[1], (D, E), D ** (-0.5)), 'w_in': s(ks[2], (E, D, H), D ** (-0.5)), 'b_in': jnp.zeros((E, H), jnp.float32), 'w_out': s(ks[3], (E, H, D), H ** (-0.5)), 'b_out': jnp.zeros((E, D), jnp.float32)}
    _L1_ffn_all = _L1_ffn_setup()
    _L1_ffn_in = {k: v for k, v in _L1_ffn_all.items() if k in ('router_w', 'w_in', 'b_in', 'w_out', 'b_out')}
    del _L1_ffn_all
    return {'x': x, 'ctx_768': ctx_768, 'L0_xattn_Wq': _L0_xattn_in['Wq'], 'L0_xattn_Wk': _L0_xattn_in['Wk'], 'L0_xattn_Wv': _L0_xattn_in['Wv'], 'L0_xattn_Wo': _L0_xattn_in['Wo'], 'L0_xattn_bo': _L0_xattn_in['bo'], 'L0_xattn_q_down': _L0_xattn_in['q_down'], 'L0_xattn_q_up': _L0_xattn_in['q_up'], 'L0_xattn_q_alpha': _L0_xattn_in['q_alpha'], 'L0_xattn_k_down': _L0_xattn_in['k_down'], 'L0_xattn_k_up': _L0_xattn_in['k_up'], 'L0_xattn_k_alpha': _L0_xattn_in['k_alpha'], 'L0_xattn_v_down': _L0_xattn_in['v_down'], 'L0_xattn_v_up': _L0_xattn_in['v_up'], 'L0_xattn_v_alpha': _L0_xattn_in['v_alpha'], 'L0_xattn_o_down': _L0_xattn_in['o_down'], 'L0_xattn_o_up': _L0_xattn_in['o_up'], 'L0_xattn_o_alpha': _L0_xattn_in['o_alpha'], 'L0_xattn_Wk_ipa': _L0_xattn_in['Wk_ipa'], 'L0_xattn_Wv_ipa': _L0_xattn_in['Wv_ipa'], 'L0_ffn_Wr1': _L0_ffn_in['Wr1'], 'L0_ffn_br1': _L0_ffn_in['br1'], 'L0_ffn_Wr2': _L0_ffn_in['Wr2'], 'L0_ffn_br2': _L0_ffn_in['br2'], 'L0_ffn_Ws1': _L0_ffn_in['Ws1'], 'L0_ffn_bs1': _L0_ffn_in['bs1'], 'L0_ffn_Ws2': _L0_ffn_in['Ws2'], 'L0_ffn_bs2': _L0_ffn_in['bs2'], 'L0_ffn_We1': _L0_ffn_in['We1'], 'L0_ffn_be1': _L0_ffn_in['be1'], 'L0_ffn_We2': _L0_ffn_in['We2'], 'L0_ffn_be2': _L0_ffn_in['be2'], 'L1_xattn_Wq': _L1_xattn_in['Wq'], 'L1_xattn_bq': _L1_xattn_in['bq'], 'L1_xattn_Wk': _L1_xattn_in['Wk'], 'L1_xattn_bk': _L1_xattn_in['bk'], 'L1_xattn_Wv': _L1_xattn_in['Wv'], 'L1_xattn_bv': _L1_xattn_in['bv'], 'L1_xattn_Wo': _L1_xattn_in['Wo'], 'L1_xattn_bo': _L1_xattn_in['bo'], 'L1_ffn_router_w': _L1_ffn_in['router_w'], 'L1_ffn_w_in': _L1_ffn_in['w_in'], 'L1_ffn_b_in': _L1_ffn_in['b_in'], 'L1_ffn_w_out': _L1_ffn_in['w_out'], 'L1_ffn_b_out': _L1_ffn_in['b_out']}

def reference(x, ctx_768, L0_xattn_Wq, L0_xattn_Wk, L0_xattn_Wv, L0_xattn_Wo, L0_xattn_bo, L0_xattn_q_down, L0_xattn_q_up, L0_xattn_q_alpha, L0_xattn_k_down, L0_xattn_k_up, L0_xattn_k_alpha, L0_xattn_v_down, L0_xattn_v_up, L0_xattn_v_alpha, L0_xattn_o_down, L0_xattn_o_up, L0_xattn_o_alpha, L0_xattn_Wk_ipa, L0_xattn_Wv_ipa, L0_ffn_Wr1, L0_ffn_br1, L0_ffn_Wr2, L0_ffn_br2, L0_ffn_Ws1, L0_ffn_bs1, L0_ffn_Ws2, L0_ffn_bs2, L0_ffn_We1, L0_ffn_be1, L0_ffn_We2, L0_ffn_be2, L1_xattn_Wq, L1_xattn_bq, L1_xattn_Wk, L1_xattn_bk, L1_xattn_Wv, L1_xattn_bv, L1_xattn_Wo, L1_xattn_bo, L1_ffn_router_w, L1_ffn_w_in, L1_ffn_b_in, L1_ffn_w_out, L1_ffn_b_out):
    import jax
    import jax.numpy as jnp

    def _L0_xattn_ref(x, context, Wq, Wk, Wv, Wo, bo, q_down, q_up, q_alpha, k_down, k_up, k_alpha, v_down, v_up, v_alpha, o_down, o_up, o_alpha, Wk_ipa, Wv_ipa):
        import jax, jax.numpy as jnp
        import numpy as np
        HEADS = 16
        DIM_HEAD = 64
        RANK = 32
        LORA_W = 1.0
        IPA_SCALE = 1.0
        IPA_TOKENS = 4
        SCALE = DIM_HEAD ** (-0.5)

        def _split_heads(t):
            b, n, _ = t.shape
            return t.reshape(b, n, HEADS, DIM_HEAD).transpose(0, 2, 1, 3)

        def _merge_heads(t):
            b, h, n, d = t.shape
            return t.transpose(0, 2, 1, 3).reshape(b, n, h * d)

        def _attention(q_in, k_in, v_in):
            q = _split_heads(q_in)
            k = _split_heads(k_in)
            v = _split_heads(v_in)
            s = jnp.einsum('bhid,bhjd->bhij', q, k) * SCALE
            p = jax.nn.softmax(s, axis=-1)
            o = jnp.einsum('bhij,bhjd->bhid', p, v)
            return _merge_heads(o)

        def _lora(t, down, up, alpha):
            return t @ down @ up * (LORA_W * alpha[0] / RANK)
        q_in = x @ Wq + _lora(x, q_down, q_up, q_alpha)
        end = context.shape[1] - IPA_TOKENS
        org_ctx = context[:, :end, :]
        ipa_ctx = context[:, end:, :]
        k_in = org_ctx @ Wk + _lora(org_ctx, k_down, k_up, k_alpha)
        v_in = org_ctx @ Wv + _lora(org_ctx, v_down, v_up, v_alpha)
        out = _attention(q_in, k_in, v_in)
        ipa_k = ipa_ctx @ Wk_ipa
        ipa_v = ipa_ctx @ Wv_ipa
        out_ipa = _attention(q_in, ipa_k, ipa_v)
        out = out + IPA_SCALE * out_ipa
        return out @ Wo + bo + _lora(out, o_down, o_up, o_alpha)

    def _L0_ffn_ref(x, Wr1, br1, Wr2, br2, Ws1, bs1, Ws2, bs2, We1, be1, We2, be2):
        import jax, jax.numpy as jnp
        import numpy as np
        B, T, C = (2, 128, 256)
        I = 1024
        E = 8
        K = 2
        Bb, Tt, Cc = x.shape
        xf = x.reshape(-1, Cc)
        logits = jax.nn.relu(xf @ Wr1 + br1) @ Wr2 + br2
        gates = jax.nn.softmax(logits, axis=-1)
        tg, ti = jax.lax.top_k(gates, K)
        tg = jax.nn.softmax(tg / K, axis=-1)
        out = jax.nn.silu(xf @ Ws1 + bs1) @ Ws2 + bs2
        for e in range(E):
            h = jax.nn.silu(xf @ We1[e] + be1[e]) @ We2[e] + be2[e]
            w = jnp.sum(tg * (ti == e), axis=-1)
            out = out + w[:, None] * h
        return out.reshape(Bb, Tt, Cc)

    def _L1_xattn_ref(x, y, Wq, bq, Wk, bk, Wv, bv, Wo, bo):
        import jax, jax.numpy as jnp
        import numpy as np
        import math
        N_HEADS = 8
        D_EMBED = 256
        D_CROSS = 192
        D_HEAD = D_EMBED // N_HEADS
        B, S, _ = x.shape
        SKV = y.shape[1]
        q = x @ Wq.T + bq
        k = y @ Wk.T + bk
        v = y @ Wv.T + bv
        q = q.reshape(B, S, N_HEADS, D_HEAD).transpose(0, 2, 1, 3)
        k = k.reshape(B, SKV, N_HEADS, D_HEAD).transpose(0, 2, 1, 3)
        v = v.reshape(B, SKV, N_HEADS, D_HEAD).transpose(0, 2, 1, 3)
        scores = jnp.einsum('bhqd,bhkd->bhqk', q, k) / math.sqrt(D_HEAD)
        attn = jax.nn.softmax(scores, axis=-1)
        out = jnp.einsum('bhqk,bhkd->bhqd', attn, v)
        out = out.transpose(0, 2, 1, 3).reshape(B, S, D_EMBED)
        return out @ Wo.T + bo

    def _L1_ffn_ref(input_batch, router_w, w_in, b_in, w_out, b_out):
        import jax, jax.numpy as jnp
        import numpy as np
        D, H, E, K = (256, 256, 8, 2)

        def _moe(x, router_w, w_in, b_in, w_out, b_out):
            B, S, Dm = x.shape
            T = B * S
            x2 = x.reshape(T, Dm)
            logits = x2 @ router_w
            probs = jax.nn.softmax(logits, axis=-1)
            top_p, top_e = jax.lax.top_k(probs, K)
            flat_e = top_e.reshape(-1)
            flat_p = top_p.reshape(-1)
            tok = jnp.repeat(jnp.arange(T), K)
            order = jnp.argsort(flat_e)
            se, sp, st = (flat_e[order], flat_p[order], tok[order])
            xd = x2[st]
            N = xd.shape[0]
            h = jnp.zeros((N, H), x.dtype)
            for e in range(E):
                m = (se == e)[:, None]
                h = h + jnp.where(m, jax.nn.gelu(xd @ w_in[e] + b_in[e]), 0.0)
            y = jnp.zeros((N, Dm), x.dtype)
            for e in range(E):
                m = (se == e)[:, None]
                y = y + jnp.where(m, h @ w_out[e] + b_out[e], 0.0)
            y = y * sp[:, None]
            out = jnp.zeros((T, Dm), x.dtype).at[st].add(y)
            return out.reshape(B, S, Dm)
        return _moe(input_batch, router_w, w_in, b_in, w_out, b_out)
    x = x + _L0_xattn_ref(_layernorm(x, axis=-1), ctx_768, L0_xattn_Wq, L0_xattn_Wk, L0_xattn_Wv, L0_xattn_Wo, L0_xattn_bo, L0_xattn_q_down, L0_xattn_q_up, L0_xattn_q_alpha, L0_xattn_k_down, L0_xattn_k_up, L0_xattn_k_alpha, L0_xattn_v_down, L0_xattn_v_up, L0_xattn_v_alpha, L0_xattn_o_down, L0_xattn_o_up, L0_xattn_o_alpha, L0_xattn_Wk_ipa, L0_xattn_Wv_ipa)
    x = x + _L0_ffn_ref(_layernorm(x, axis=-1), L0_ffn_Wr1, L0_ffn_br1, L0_ffn_Wr2, L0_ffn_br2, L0_ffn_Ws1, L0_ffn_bs1, L0_ffn_Ws2, L0_ffn_bs2, L0_ffn_We1, L0_ffn_be1, L0_ffn_We2, L0_ffn_be2)
    x = x + _L1_xattn_ref(_layernorm(x, axis=-1), ctx_768, L1_xattn_Wq, L1_xattn_bq, L1_xattn_Wk, L1_xattn_bk, L1_xattn_Wv, L1_xattn_bv, L1_xattn_Wo, L1_xattn_bo)
    x = x + _L1_ffn_ref(_layernorm(x, axis=-1), L1_ffn_router_w, L1_ffn_w_in, L1_ffn_b_in, L1_ffn_w_out, L1_ffn_b_out)
    return x

_drawn_inputs = setup_inputs


def setup_inputs(seed=0):
    import zlib

    import numpy as np

    out = dict(_drawn_inputs(seed))
    spreads = {'L0_xattn_bo': (0.0, 0.1),
     'L0_ffn_br1': (0.0, 0.273),
     'L0_ffn_br2': (0.0, 0.1),
     'L0_ffn_bs1': (0.0, 0.1),
     'L0_ffn_bs2': (0.0, 0.1),
     'L0_ffn_be1': (0.0, 0.269),
     'L0_ffn_be2': (0.0, 0.1),
     'L1_xattn_bq': (0.0, 0.292),
     'L1_xattn_bk': (0.0, 2.0),
     'L1_xattn_bv': (0.0, 0.1),
     'L1_xattn_bo': (0.0, 0.1),
     'L1_ffn_b_in': (0.0, 0.342),
     'L1_ffn_b_out': (0.0, 0.1)}
    factors = {'L0_xattn_Wq': 5.185,
     'L0_xattn_Wk': 7.91,
     'L0_xattn_q_down': 8.0,
     'L0_xattn_q_up': 8.0,
     'L0_xattn_k_down': 8.0,
     'L0_xattn_k_up': 8.0,
     'L0_xattn_v_down': 3.421,
     'L0_xattn_v_up': 4.026,
     'L0_xattn_Wk_ipa': 5.998}
    for name, (base, spread) in spreads.items():
        noise = np.random.default_rng([zlib.crc32(name.encode()), seed]).standard_normal(out[name].shape)
        drawn = base * np.exp(spread * noise) if base else spread * noise
        out[name] = jnp.asarray(drawn.astype(out[name].dtype))
    for name, factor in factors.items():
        out[name] = (out[name] * factor).astype(out[name].dtype)
    return out
```

```python
from contextlib import ExitStack

import concourse.bass as bass
from concourse import mybir

FP = mybir.dt.float32
FR = mybir.dt.float32r
I32 = mybir.dt.int32
ALU = mybir.AluOpType
ACT = mybir.ActivationFunctionType
AX = mybir.AxisListType



P = 128
NB, SEQ, D = 2, 1024, 256
TOK = NB * SEQ
NT = TOK // P
DK = D // P
KEYS, IPA, DC = 77, 4, 192
CP, CK = 96, 2
RANK = 32
E, TOPK = 8, 2
ST = 256
ROUTED = (TOK * TOPK + E * (ST - 1)) // ST
EPS = 1e-5

class Layer:

    def __init__(self, n, heads, dh, segments, lora, hid, shared, func):
        self.n, self.heads, self.dh, self.segments = n, heads, dh, segments
        self.lora, self.hid, self.shared, self.func = lora, hid, shared, func
        self.scale = dh ** -0.5
        self.hp = P // dh
        self.groups = heads // self.hp
        self.n_g = self.hp * KEYS
        self.cols = heads * KEYS
        self.chunks = -(-self.cols // P)
        self.pad = self.chunks * P
        self.c0 = [g * self.n_g // P for g in range(self.groups)]
        self.win = [P * (((g + 1) * self.n_g - 1) // P - self.c0[g] + 1) for g in range(self.groups)]
        self.m1 = hid // P
        self.sh_tiles = TOK // ST if shared else 0
        self.tiles = ROUTED + self.sh_tiles


LAYERS = [
    Layer(0, 16, 64, [(0, KEYS - IPA), (KEYS - IPA, KEYS)], True, 1024, True, ACT.Silu),
    Layer(1, 8, 32, [(0, KEYS)], False, 256, False, ACT.Gelu_apprx_tanh),
]


class Shared:
    pass


def wait(eng, sem, value):
    if not isinstance(value, int) or value > 0:
        eng.wait_ge(sem, value)


def one(ap, i):
    return ap[:, i:i + 1] if isinstance(i, int) else ap[:, bass.ds(i, 1)]


def product(nc, out, lhs, rhs, start, stop):
    (lh, ll), (rh, rl) = lhs, rhs
    nc.tensor.matmul(out, lh, rh, start=start, stop=False)
    nc.tensor.matmul(out, lh, rl, start=False, stop=False)
    return nc.tensor.matmul(out, ll, rh, start=False, stop=stop)


def prepare(nc, g, x, sem):
    s_x, s_c, s_st, s_z = sem("prep_x_loaded"), sem("prep_const"), sem("prep_stats"), sem("prep_xs_zero")
    s_zf = sem("prep_zero_tile")
    xs_flat = g.xs.rearrange("(a p) d -> p a d", p=P)
    na = xs_flat.shape[1]
    with nc.Block() as block:
        @block.sync
        def _(sp):
            sp.dma_start(g.X[:], x.rearrange("(t p) d -> p t d", p=P)).then_inc(s_x, 16)
            sp.wait_ge(s_zf, 1)
            for a in range(0, na, 2):
                sp.dma_start(xs_flat[:, a:a + 2, :], g.zero[:].rearrange("p (a d) -> p a d", a=2)).then_inc(s_z, 16)
            sp.wait_ge(s_z, 16 * (na // 2))

        @block.gpsimd
        def _(pool):
            nc.gpsimd.memset(g.zero[:], 0.0).then_inc(s_zf, 1)
            nc.gpsimd.memset(g.ident[:], 0.0).then_inc(s_c, 1)
            nc.gpsimd.memset(g.before[:], 1.0).then_inc(s_c, 1)
            nc.gpsimd.memset(g.ones[:], 1.0).then_inc(s_c, 1)
            pool.wait_ge(s_c, 3)
            nc.gpsimd.affine_select(out=g.ident[:], in_=g.ident[:], compare_op=ALU.not_equal, fill=1.0,
                                    base=0, pattern=[[-1, P]], channel_multiplier=1).then_inc(s_c, 1)
            nc.gpsimd.affine_select(out=g.before[:], in_=g.before[:], compare_op=ALU.is_gt, fill=0.0,
                                    base=0, pattern=[[1, P]], channel_multiplier=-1).then_inc(s_c, 1)
            nc.gpsimd.iota(g.iota_e[:], pattern=[[0, NT], [1, E]], base=0, channel_multiplier=0,
                           allow_small_or_imprecise_dtypes=True).then_inc(s_c, 1)
            nc.gpsimd.iota(g.iota_thr[:], pattern=[[0, E], [ST, TOK // ST]], base=0, channel_multiplier=0,
                           allow_small_or_imprecise_dtypes=True).then_inc(s_c, 1)
            nc.gpsimd.iota(g.iota_tile[:], pattern=[[1, g.iota_tile.shape[1]], [0, E]], base=0, channel_multiplier=0,
                           allow_small_or_imprecise_dtypes=True).then_inc(s_c, 1)
            pool.wait_ge(s_c, 8)

        @block.vector
        def _(dve):
            dve.wait_ge(s_c, 8)
            nc.vector.tensor_copy(g.ones_r[:], g.ones[0:1, :]).then_inc(s_st, 1)
            dve.wait_ge(s_x, 16)
            for t in range(NT):
                nc.vector.bn_stats(g.stats[:, t, :], g.X[:, t, :]).then_inc(s_st, 1)
            dve.wait_ge(s_st, 1 + NT)
            for t in range(NT):
                nc.vector.bn_aggr(g.mv[:, t, :], g.stats[:, t, :])


def inverse_deviation(nc, g, sem, tag):
    s_v, s_q, s_r = sem(tag + "_var_eps"), sem(tag + "_sqrt"), sem(tag + "_chain")
    var = g.mv[:, :, 1]
    with nc.Block() as block:
        @block.vector
        def _(dve):
            nc.vector.tensor_scalar(g.ve[:], var, EPS, None, ALU.add).then_inc(s_v, 1)
            dve.wait_ge(s_q, 1)
            nc.vector.reciprocal(g.rstd[:], g.sq[:]).then_inc(s_r, 1)
            dve.wait_ge(s_r, 1)
            nc.vector.tensor_tensor(g.sq[:], g.rstd[:], g.rstd[:], ALU.mult).then_inc(s_r, 1)
            dve.wait_ge(s_r, 2)
            nc.vector.tensor_tensor(g.sq[:], g.sq[:], g.ve[:], ALU.mult).then_inc(s_r, 1)
            dve.wait_ge(s_r, 3)
            nc.vector.tensor_scalar(g.sq[:], g.sq[:], -0.5, 1.5, ALU.mult, ALU.add).then_inc(s_r, 1)
            dve.wait_ge(s_r, 4)
            nc.vector.tensor_tensor(g.rstd[:], g.rstd[:], g.sq[:], ALU.mult).then_inc(s_r, 1)

        @block.scalar
        def _(act):
            act.wait_ge(s_v, 1)
            nc.scalar.activation(g.sq[:], g.ve[:], ACT.Sqrt).then_inc(s_q, 1)


def attention_setup(nc, g, L, w, sem):
    T = f"as{L.n}_"
    s_w, s_zero, s_al = sem(T + "weights"), sem(T + "zeroed"), sem(T + "alpha")
    s_lk, s_lk_sb = sem(T + "ctx_lora"), sem(T + "ctx_lora_copied")
    s_kv, s_bd = sem(T + "kv"), sem(T + "block_diagonal")
    s_u, s_u_sb = sem(T + "low_rank"), sem(T + "low_rank_copied")
    s_a, s_ahi, s_alo = sem(T + "a"), sem(T + "a_high"), sem(T + "a_low")
    s_b, s_bhi, s_blo = sem(T + "b"), sem(T + "b_high"), sem(T + "b_low")
    s_r = sem(T + "rows")
    G, n, hp, dh = L.groups, L.n_g, L.hp, L.dh
    HD = L.heads * dh
    org = KEYS - IPA
    with ExitStack() as ctx:
        sb = lambda name, shape, dt=FP: ctx.enter_context(nc.sbuf_tensor(T + name, shape, dt))
        pb = lambda name, shape: ctx.enter_context(nc.psum_tensor(T + name, shape, FP))
        c = sb("ctx", [CP, CK, NB, KEYS])
        wk, wv = sb("wk", [CP, CK, HD]), sb("wv", [CP, CK, HD])
        wq, wo = sb("wq", [P, G, D]), sb("wo", [P, G, D])
        bo = sb("bo", [1, D])
        loads = [(c, w["ctx"]), (wk, w["wk"]), (wv, w["wv"]), (wq, w["wq"]), (wo, w["wo"]), (bo, w["bo"])]
        if L.lora:
            wki, wvi = sb("wki", [CP, CK, HD]), sb("wvi", [CP, CK, HD])
            kd, vd = sb("kd", [CP, CK, RANK]), sb("vd", [CP, CK, RANK])
            ku, vu = sb("ku", [RANK, HD]), sb("vu", [RANK, HD])
            qu, qd = sb("qu", [P, G, RANK]), sb("qd", [RANK, D])
            od, ou = sb("od", [P, G, RANK]), sb("ou", [RANK, D])
            al = sb("al", [RANK, 4])
            loads += [(wki, w["wki"]), (wvi, w["wvi"]), (kd, w["kd"]), (vd, w["vd"]), (ku, w["ku"]), (vu, w["vu"]),
                      (qu, w["qu"]), (qd, w["qd"]), (od, w["od"]), (ou, w["ou"]),
                      (al, w["alphas"].to_broadcast([RANK, 4]))]
            low = sb("low", [RANK, 2, NB, org])
            u_sb = sb("u_sb", [RANK, 2, n])
            rt = sb("rt", [RANK, NB, L.pad])
        else:
            bq, bk, bv = sb("bq", [P, G]), sb("bk", [P, G]), sb("bv", [P, G])
            loads += [(bq, w["bq"]), (bk, w["bk"]), (bv, w["bv"])]
        kbd = sb("kbd", [P, G, NB, n])
        vbd = sb("vbd", [P, NB, sum(L.win)])
        ps_kv = pb("ps_kv", [P, 2, 2, 256])
        ps_u = pb("ps_u", [P, 2, 512])
        ps_a = pb("ps_a", [P, 2, 512])
        ps_b = pb("ps_b", [P, 2, 512])
        base = [sum(L.win[:gi]) for gi in range(G)]
        off = [base[gi] + gi * n - P * L.c0[gi] for gi in range(G)]
        b_items = [(b, ch) for b in range(NB) for ch in range(L.chunks)]

        with nc.Block() as block:
            @block.sync
            def _(sp):
                for dst, src in loads:
                    sp.dma_start(dst[:], src).then_inc(s_w, 16)

            n_u = NB * 2 if L.lora else NB

            @block.tensor
            def _(pe):
                pe.wait_ge(s_w, 16 * len(loads))
                if L.lora:
                    for i, down in enumerate((kd, vd)):
                        o = ps_u[0:RANK, i, 0:NB * org].rearrange("p (b j) -> p b j", b=NB)
                        for k in range(CK):
                            last = nc.tensor.matmul(o, down[:, k, :], c[:, k, :, 0:org], start=k == 0, stop=k == CK - 1)
                        last.then_inc(s_lk, 1)

                def keys_values(gi):
                    wait(pe, s_bd, gi - 1)
                    for i, (main, ipa, up) in enumerate(((wk, wki, ku), (wv, wvi, vu)) if L.lora else ((wk, 0, 0), (wv, 0, 0))):
                        o = ps_kv[:, gi % 2, i, 0:NB * KEYS].rearrange("p (b j) -> p b j", b=NB)
                        gs = slice(gi * P, gi * P + P)
                        m = org if L.lora else KEYS
                        for k in range(CK):
                            last = nc.tensor.matmul(o[:, :, 0:m], main[:, k, gs], c[:, k, :, 0:m], start=k == 0,
                                                    stop=not L.lora and k == CK - 1)
                        if L.lora:
                            if gi == 0 and i == 0:
                                pe.wait_ge(s_lk_sb, 2)
                            nc.tensor.matmul(o[:, :, 0:m], up[:, gs], low[:, i], start=False, stop=True)
                            for k in range(CK):
                                last = nc.tensor.matmul(o[:, :, m:], ipa[:, k, gs], c[:, k, :, m:], start=k == 0,
                                                        stop=k == CK - 1)
                    last.then_inc(s_kv, 1)

                keys_values(0)
                for gi in range(G):
                    if gi + 1 < G:
                        keys_values(gi + 1)
                    pe.wait_ge(s_bd, gi + 1)
                    for b in range(NB):
                        for r in range(n_u // NB):
                            u = gi * n_u + b * (n_u // NB) + r
                            wait(pe, s_u_sb, u - 1)
                            if L.lora:
                                if r == 0:
                                    last = nc.tensor.matmul(ps_u[0:RANK, u % 2, 0:n], qu[:, gi, :], kbd[:, gi, b, :], start=True, stop=True)
                                else:
                                    last = nc.tensor.matmul(ps_u[0:RANK, u % 2, 0:n], od[:, gi, :],
                                                            vbd[:, b, off[gi]:off[gi] + n], start=True, stop=True)
                            else:
                                last = nc.tensor.matmul(ps_u[0:1, u % 2, 0:n], bq[:, gi:gi + 1], kbd[:, gi, b, :], start=True, stop=True)
                            last.then_inc(s_u, 1)
                    for b in range(NB):
                        for k in range(DK):
                            a = (gi * NB + b) * DK + k
                            wait(pe, s_alo, a - 1)
                            last = nc.tensor.matmul(ps_a[:, a % 2, 0:n], wq[:, gi, k * P:(k + 1) * P], kbd[:, gi, b, :],
                                                    start=True, stop=not L.lora)
                            if L.lora:
                                if k == 0:
                                    pe.wait_ge(s_u_sb, gi * n_u + b * 2 + 1)
                                last = nc.tensor.matmul(ps_a[:, a % 2, 0:n], qd[:, k * P:(k + 1) * P], u_sb[:, b, :],
                                                        start=False, stop=True)
                            last.then_inc(s_a, 1)
                if L.lora:
                    pe.wait_ge(s_u_sb, G * n_u)
                for i, (b, ch) in enumerate(b_items):
                    wait(pe, s_blo, i - 1)
                    rows = min(P, L.cols - ch * P)
                    over = [gi for gi in range(G) if gi * n < (ch + 1) * P and (gi + 1) * n > ch * P]
                    for gi in over:
                        v0 = base[gi] + (ch - L.c0[gi]) * P
                        last = nc.tensor.matmul(ps_b[0:rows, i % 2, 0:D], vbd[:, b, v0:v0 + rows], wo[:, gi, :],
                                                start=gi == over[0], stop=not L.lora and gi == over[-1])
                    if L.lora:
                        last = nc.tensor.matmul(ps_b[0:rows, i % 2, 0:D], rt[:, b, ch * P:ch * P + rows], ou[:], start=False, stop=True)
                    last.then_inc(s_b, 1)

            @block.gpsimd
            def _(pool):
                nc.gpsimd.memset(kbd[:], 0.0).then_inc(s_zero, 1)
                nc.gpsimd.memset(g.Bh[L.n][:, :, L.chunks - 1, :].bitcast(FP), 0.0).then_inc(s_zero, 1)
                nc.gpsimd.memset(g.Bl[L.n][:, :, L.chunks - 1, :].bitcast(FP), 0.0).then_inc(s_zero, 1)

            @block.vector
            def _(dve):
                nc.vector.memset(vbd[:], 0.0).then_inc(s_zero, 1)
                dve.wait_ge(s_w, 16 * len(loads))
                if L.lora:
                    nc.vector.tensor_scalar(al[:], al[:], 1.0 / RANK, None, ALU.mult).then_inc(s_al, 1)
                nc.vector.tensor_copy(g.boh[:], bo[:]).then_inc(s_r, 1)
                dve.wait_ge(s_r, 1)
                nc.vector.tensor_tensor(g.bol[:], bo[:], g.boh[:], ALU.subtract)
                dve.wait_ge(s_zero, 4)

                def block_diagonal(gi):
                    dve.wait_ge(s_kv, gi + 1)
                    for hh in range(hp):
                        rows = slice(dh * hh, dh * (hh + 1))
                        for i in range(2):
                            src = ps_kv[rows, gi % 2, i, 0:NB * KEYS].rearrange("p (b j) -> p b j", b=NB)
                            at = hh * KEYS + (off[gi] if i else 0)
                            dst = vbd[rows, :, at:at + KEYS] if i else kbd[rows, gi, :, at:at + KEYS]
                            if L.lora:
                                last = nc.vector.tensor_copy(dst, src)
                            else:
                                last = nc.vector.tensor_scalar(dst, src, (bv if i else bk)[rows, gi:gi + 1], None, ALU.add)
                    last.then_inc(s_bd, 1)

                block_diagonal(0)
                for gi in range(G):
                    if gi + 1 < G:
                        block_diagonal(gi + 1)
                    if not L.lora:
                        for b in range(NB):
                            u = gi * n_u + b
                            dve.wait_ge(s_u, u + 1)
                            nc.vector.tensor_copy(g.rowh[:, b, gi * n:(gi + 1) * n], ps_u[0:1, u % 2, 0:n]).then_inc(s_r, 1)
                            dve.wait_ge(s_r, 2 + u)
                            nc.vector.tensor_tensor(g.rowl[:, b, gi * n:(gi + 1) * n], ps_u[0:1, u % 2, 0:n],
                                                    g.rowh[:, b, gi * n:(gi + 1) * n], ALU.subtract).then_inc(s_u_sb, 1)
                    for b in range(NB):
                        for k in range(DK):
                            a = (gi * NB + b) * DK + k
                            dve.wait_ge(s_ahi, a + 1)
                            cs = slice(gi * n, (gi + 1) * n)
                            nc.vector.tensor_tensor(g.Al[L.n][:, b, k, cs], ps_a[:, a % 2, 0:n],
                                                    g.Ah[L.n][:, b, k, cs], ALU.subtract).then_inc(s_alo, 1)
                for i, (b, ch) in enumerate(b_items):
                    rows = min(P, L.cols - ch * P)
                    dve.wait_ge(s_bhi, i + 1)
                    nc.vector.tensor_tensor(g.Bl[L.n][0:rows, b, ch, :], ps_b[0:rows, i % 2, 0:D],
                                            g.Bh[L.n][0:rows, b, ch, :], ALU.subtract).then_inc(s_blo, 1)

            @block.scalar
            def _(act):
                if L.lora:
                    act.wait_ge(s_al, 1)
                    for i in range(2):
                        act.wait_ge(s_lk, i + 1)
                        nc.scalar.activation(low[:, i], ps_u[0:RANK, i, 0:NB * org].rearrange("p (b j) -> p b j", b=NB),
                                             ACT.Copy, scale=al[:, 1 + i:2 + i]).then_inc(s_lk_sb, 1)
                act.wait_ge(s_zero, 4)
                for gi in range(G):
                    if L.lora:
                        for b in range(NB):
                            for r in range(2):
                                u = gi * n_u + b * 2 + r
                                act.wait_ge(s_u, u + 1)
                                if r == 0:
                                    wait(act, s_a, (gi * NB + b) * DK - 2)
                                    nc.scalar.activation(u_sb[:, b, :], ps_u[0:RANK, u % 2, 0:n], ACT.Copy,
                                                         scale=al[:, 0:1]).then_inc(s_u_sb, 1)
                                else:
                                    nc.scalar.activation(rt[:, b, gi * n:(gi + 1) * n], ps_u[0:RANK, u % 2, 0:n], ACT.Copy,
                                                         scale=al[:, 3:4]).then_inc(s_u_sb, 1)
                    for b in range(NB):
                        for k in range(DK):
                            a = (gi * NB + b) * DK + k
                            act.wait_ge(s_a, a + 1)
                            nc.scalar.copy(g.Ah[L.n][:, b, k, gi * n:(gi + 1) * n], ps_a[:, a % 2, 0:n]).then_inc(s_ahi, 1)
                for i, (b, ch) in enumerate(b_items):
                    rows = min(P, L.cols - ch * P)
                    act.wait_ge(s_b, i + 1)
                    nc.scalar.copy(g.Bh[L.n][0:rows, b, ch, :], ps_b[0:rows, i % 2, 0:D]).then_inc(s_bhi, 1)


def attention(nc, g, L, sem):
    T = f"at{L.n}_"
    s_xn, s_xt, s_xhi, s_xlo = sem(T + "xn"), sem(T + "x_transposed"), sem(T + "x_high"), sem(T + "x_low")
    s_s, s_mx, s_sub, s_exp = sem(T + "scores"), sem(T + "max"), sem(T + "shifted"), sem(T + "exp")
    s_sum, s_inv, s_pn = sem(T + "sum"), sem(T + "inverse"), sem(T + "probs")
    s_pt, s_phi, s_plo = sem(T + "probs_transposed"), sem(T + "probs_high"), sem(T + "probs_low")
    s_o, s_res, s_bn, s_pad, s_aggr = sem(T + "out"), sem(T + "residual"), sem(T + "bn"), sem(T + "pad"), sem(T + "aggr")
    H, NS, CH = L.heads, len(L.segments), L.chunks
    with ExitStack() as ctx:
        sb = lambda name, shape, dt=FP: ctx.enter_context(nc.sbuf_tensor(T + name, shape, dt))
        pb = lambda name, shape: ctx.enter_context(nc.psum_tensor(T + name, shape, FP))
        xn = sb("xn", [P, 2, D])
        xh, xl = sb("xh", [P, 2, DK, P], FR), sb("xl", [P, 2, DK, P], FR)
        sm = sb("sm", [P, L.cols])
        pr = sb("pr", [P, 2, L.pad])
        mx, su, inv = sb("mx", [P, H, NS]), sb("su", [P, H, NS]), sb("inv", [P, H, NS])
        ph, pl = sb("ph", [P, CH, P], FR), sb("pl", [P, CH, P], FR)
        ps_x = pb("ps_x", [P, 512])
        ps_s = pb("ps_s", [P, 512 * (-(-L.cols // 512))])
        ps_p = pb("ps_p", [P, 512 * (-(-L.pad // 512))])
        ps_o = pb("ps_o", [P, 512])
        scores = ps_s[:, 0:L.cols].rearrange("p (h j) -> p h j", h=H)
        shifted = sm[:, :].rearrange("p (h j) -> p h j", h=H)
        probs_t = ps_p[:, 0:L.pad].rearrange("p (c t) -> p c t", t=P)
        Ah, Al, Bh, Bl = g.Ah[L.n], g.Al[L.n], g.Bh[L.n], g.Bl[L.n]
        low_order = NT - 1

        def steps(eng, body, cuts):
            for lo, hi in cuts:
                if hi - lo < 4:
                    for t in range(lo, hi):
                        body(t, t % 2)
                else:
                    with eng.Fori(lo, hi - 1, 2) as i:
                        body(i, lo % 2)
                        body(i + 1, (lo + 1) % 2)

        with nc.Block() as block:
            @block.tensor
            def _(pe):
                def transpose_x(t, q):
                    wait(pe, s_xn, t + 1)
                    wait(pe, s_xlo, t)
                    for k in range(DK):
                        last = nc.tensor.transpose(ps_x[:, k * P:(k + 1) * P], xn[:, q, k * P:(k + 1) * P], g.ident[:])
                    last.then_inc(s_xt, 1)

                def make(b_s, b_o):
                    def step(t, q):
                        static = isinstance(t, int)
                        if not static or t + 1 < NT:
                            wait(pe, s_xlo, t + 2)
                            wait(pe, s_sub, t + 1)
                            for c0 in range(0, L.cols, 512):
                                c1 = min(c0 + 512, L.cols)
                                for k in range(DK):
                                    last = product(nc, ps_s[:, c0:c1], (xh[:, 1 - q, k, :], xl[:, 1 - q, k, :]),
                                                   (Ah[:, b_s, k, c0:c1], Al[:, b_s, k, c0:c1]), k == 0, L.lora and k == DK - 1)
                                if not L.lora:
                                    nc.tensor.matmul(ps_s[:, c0:c1], g.ones_r[:], g.rowh[:, b_s, c0:c1], start=False, stop=False)
                                    last = nc.tensor.matmul(ps_s[:, c0:c1], g.ones_r[:], g.rowl[:, b_s, c0:c1], start=False, stop=True)
                            last.then_inc(s_s, 1)
                        if not static or t >= 1:
                            wait(pe, s_plo, t)
                            wait(pe, s_res, t - 1)
                            nc.tensor.matmul(ps_o[:, 0:D], g.ones_r[:], g.boh[:], start=True, stop=False)
                            nc.tensor.matmul(ps_o[:, 0:D], g.ones_r[:], g.bol[:], start=False, stop=False)
                            for ch in range(CH):
                                last = product(nc, ps_o[:, 0:D], (ph[:, ch, :], pl[:, ch, :]),
                                               (Bh[:, b_o, ch, :], Bl[:, b_o, ch, :]), False, ch == CH - 1)
                            last.then_inc(s_o, 1)
                        if not static or t + 2 < NT:
                            transpose_x(t + 2, q)
                        if not static or 0 <= t < NT:
                            wait(pe, s_pn, t + 1)
                            wait(pe, s_plo, t)
                            for ch in range(CH):
                                last = nc.tensor.transpose(probs_t[:, ch, :], pr[:, q, ch * P:(ch + 1) * P], g.ident[:])
                            last.then_inc(s_pt, 1)
                    return step

                pe.wait_ge(s_pad, 1)
                transpose_x(0, 0)
                h = NT // NB
                steps(pe, make(0, 0), [(-1, 1), (1, 3), (3, h - 1)])
                steps(pe, make(1, 0), [(h - 1, h + 1)])
                steps(pe, make(1, 1), [(h + 1, NT - 3), (NT - 3, NT - 1), (NT - 1, NT + 1)])

            @block.vector
            def _(dve):
                def normalise(t, q):
                    if isinstance(t, int) and t < 2:
                        pass
                    else:
                        wait(dve, s_xt, t - 1)
                    nc.vector.tensor_scalar(xn[:, q:q + 1, :], one(g.X, t), one(g.mv[:, :, 0], t), one(g.rstd, t),
                                            ALU.subtract, ALU.mult).then_inc(s_xn, 1)

                def low_x(t, q):
                    wait(dve, s_xhi, t + 1)
                    nc.vector.tensor_tensor(xl[:, q], ps_x[:, 0:D].rearrange("p (k t) -> p k t", k=DK), xh[:, q],
                                            ALU.subtract).then_inc(s_xlo, 1)

                def step(t, q):
                    static = isinstance(t, int)
                    if not static or t + 2 < NT:
                        normalise(t + 2, q)
                    if not static or 0 <= t < NT:
                        wait(dve, s_exp, t + 1)
                        wait(dve, s_pn, t)
                        e = pr[:, q, 0:L.cols].rearrange("p (h j) -> p h j", h=H)
                        for i, (j0, j1) in enumerate(L.segments):
                            nc.vector.tensor_reduce(su[:, :, i:i + 1], e[:, :, j0:j1], AX.X, ALU.add).then_inc(s_sum, 1)
                        wait(dve, s_sum, NS * (t + 1))
                        nc.vector.reciprocal(inv[:], su[:]).then_inc(s_inv, 1)
                    if not static or t + 1 < NT:
                        wait(dve, s_s, t + 2)
                        for i, (j0, j1) in enumerate(L.segments):
                            nc.vector.tensor_reduce(mx[:, :, i:i + 1], scores[:, :, j0:j1], AX.X, ALU.max).then_inc(s_mx, 1)
                        wait(dve, s_mx, NS * (t + 2))
                        wait(dve, s_exp, t + 1)
                        for i, (j0, j1) in enumerate(L.segments):
                            last = nc.vector.tensor_tensor(shifted[:, :, j0:j1], scores[:, :, j0:j1],
                                                           mx[:, :, i:i + 1].to_broadcast([P, H, j1 - j0]), ALU.subtract)
                        last.then_inc(s_sub, 1)
                    if not static or t >= 1:
                        wait(dve, s_o, t)
                        x = one(g.X, t - 1)
                        nc.vector.tensor_tensor(x, x, ps_o[:, 0:D].rearrange("p (a d) -> p a d", a=1),
                                                ALU.add).then_inc(s_res, 1)
                        wait(dve, s_res, t)
                        nc.vector.bn_stats(one(g.stats, t - 1), one(g.X, t - 1)).then_inc(s_bn, 1)
                    if not static or t + 2 < NT:
                        low_x(t + 2, q)
                    if not static or 0 <= t < NT:
                        wait(dve, s_phi, t + 1)
                        nc.vector.tensor_tensor(pl[:], probs_t, ph[:], ALU.subtract).then_inc(s_plo, 1)

                nc.vector.memset(pr[:, :, L.cols:], 0.0).then_inc(s_pad, 1)
                normalise(0, 0)
                low_x(0, 0)
                steps(dve, step, [(-1, 1), (1, 3), (3, NT - 3), (NT - 3, NT - 1), (NT - 1, NT + 1)])
                dve.wait_ge(s_bn, NT)
                for t in range(NT):
                    nc.vector.bn_aggr(g.mv[:, t, :], g.stats[:, t, :]).then_inc(s_aggr, 1)

            @block.scalar
            def _(act):
                def high_x(t, q):
                    wait(act, s_xt, t + 1)
                    wait(act, s_s, t - 1)
                    nc.scalar.copy(xh[:, q], ps_x[:, 0:D].rearrange("p (k t) -> p k t", k=DK)).then_inc(s_xhi, 1)

                def step(t, q):
                    static = isinstance(t, int)
                    if not static or t + 1 < NT:
                        wait(act, s_sub, t + 2)
                        wait(act, s_pt, t)
                        nc.scalar.activation(pr[:, 1 - q, 0:L.cols], sm[:, :], ACT.Exp, scale=L.scale).then_inc(s_exp, 1)
                    if not static or t + 2 < NT:
                        high_x(t + 2, q)
                    if not static or 0 <= t < NT:
                        wait(act, s_pt, t + 1)
                        wait(act, s_o, t)
                        nc.scalar.copy(ph[:], probs_t).then_inc(s_phi, 1)

                nc.scalar.preload_act_table(ACT.Exp)
                high_x(0, 0)
                steps(act, step, [(-1, 1), (1, 3), (3, NT - 3), (NT - 3, NT - 1), (NT - 1, NT + 1)])

            @block.gpsimd
            def _(pool):
                def step(t, q):
                    wait(pool, s_inv, t + 1)
                    e = pr[:, q, 0:L.cols].rearrange("p (h j) -> p h j", h=H)
                    for i, (j0, j1) in enumerate(L.segments):
                        last = nc.gpsimd.tensor_tensor(e[:, :, j0:j1], e[:, :, j0:j1],
                                                       inv[:, :, i:i + 1].to_broadcast([P, H, j1 - j0]), ALU.mult)
                    last.then_inc(s_pn, 1)

                with pool.Fori(0, NT - 1, 2) as i:
                    step(i, 0)
                    step(i + 1, 1)


def allocate(nc, ctx):
    sb = lambda name, shape, dt=FP: ctx.enter_context(nc.sbuf_tensor(name, shape, dt))
    g = Shared()
    g.X = sb("X", [P, NT, D])
    g.stats, g.mv = sb("stats", [P, NT, 6]), sb("mean_var", [P, NT, 2])
    g.ve, g.sq, g.rstd = sb("var_eps", [P, NT]), sb("deviation", [P, NT]), sb("rstd", [P, NT])
    g.ident, g.before, g.ones = sb("ident", [P, P]), sb("before", [P, P]), sb("ones", [P, P])
    g.ones_r = sb("ones_r", [1, P], FR)
    g.iota_e, g.iota_thr = sb("iota_e", [P, NT, E]), sb("iota_thr", [P, E, TOK // ST])
    g.zero = sb("zero", [P, 2 * D])
    g.iota_tile = sb("iota_tile", [P, ROUTED, E])
    g.xs = nc.dram_tensor("slots_in", [max(L.tiles for L in LAYERS) * ST, D], FP, kind="Internal").ap()
    g.ys = nc.dram_tensor("slots_out", [max(L.tiles for L in LAYERS) * ST, D], FP, kind="Internal").ap()
    g.Ah, g.Al, g.Bh, g.Bl = {}, {}, {}, {}
    return g


def attention_operands(nc, ctx, g, L):
    sb = lambda name, shape: ctx.enter_context(nc.sbuf_tensor(f"{name}{L.n}", shape, FR))
    g.Ah[L.n], g.Al[L.n] = sb("A_high", [P, NB, DK, L.cols]), sb("A_low", [P, NB, DK, L.cols])
    g.Bh[L.n], g.Bl[L.n] = sb("B_high", [P, NB, L.chunks, D]), sb("B_low", [P, NB, L.chunks, D])
    g.boh, g.bol = sb("bo_high", [1, D]), sb("bo_low", [1, D])
    if not L.lora:
        g.rowh, g.rowl = sb("row_high", [1, NB, L.cols]), sb("row_low", [1, NB, L.cols])


def route(nc, g, m, L, w, sem):
    T = f"r{L.n}_"
    s_w, s_xn, s_t, s_xt = sem(T + "weights"), sem(T + "xn"), sem(T + "transposed"), [sem(f"{T}x_copied{k}") for k in range(DK)]
    s_r1, s_relu, s_lg = sem(T + "hidden"), sem(T + "relu"), sem(T + "logits")
    s_ch, s_ex, s_cnt, s_ct = sem(T + "chain"), sem(T + "exp"), sem(T + "counts"), sem(T + "counted")
    s_sc, s_sh, s_k = sem(T + "scattered"), sem(T + "shared_stored"), sem(T + "slots")
    CT, RH = 4, D // 4
    with ExitStack() as ctx:
        sb = lambda name, shape, dt=FP: ctx.enter_context(nc.sbuf_tensor(T + name, shape, dt))
        pb = lambda name, shape: ctx.enter_context(nc.psum_tensor(T + name, shape, FP))
        xt = sb("xt", [P, 2, DK, CT * P])
        if L.n == 0:
            r1, rb1, r2, rb2 = sb("r1", [P, DK, RH]), sb("rb1", [RH, 1]), sb("r2", [RH, E]), sb("rb2", [1, E])
            hid = sb("hid", [RH, 2, CT * P])
            loads = [(r1, w["r1"]), (rb1, w["rb1"]), (r2, w["r2"]), (rb2, w["rb2"])]
        else:
            r1 = sb("r", [P, DK, E])
            loads = [(r1, w["r"])]
        t8 = lambda name: sb(name, [P, NT, E])
        t1 = lambda name: sb(name, [P, NT, 1])
        sh, ex, pro, pro2, eq = t8("sh"), t8("ex"), t8("pro"), t8("pro2"), t8("eq")
        is1, is2, both, offs, slot, tmp = t8("is1"), t8("is2"), t8("both"), t8("offs"), t8("slot"), t8("tmp")
        far = t8("far")
        mx, sm, inv, p1, p2, i1, i2 = (t1(n) for n in ("mx", "sm", "inv", "p1", "p2", "i1", "i2"))
        ed, sf = t1("ed"), t1("sf")
        n_e, nt_e, ends, start = sb("n_e", [P, E, 1]), sb("nt_e", [P, E, 1]), sb("ends", [P, E, 1]), sb("start", [P, 1, E])
        over = sb("over", [P, E, TOK // ST])
        past, tile_e = sb("past", [1, ROUTED, E]), sb("tile_e", [1, ROUTED, 1])
        ps_x = pb("ps_x", [P, 2, DK, CT * P])
        ps_r = pb("ps_r", [RH, 2, CT * P])
        ps_l = pb("ps_l", [P, NT, E])
        ps_c = pb("ps_c", [P, 2, NT, E])
        chunks = NT // CT

        with nc.Block() as block:
            @block.sync
            def _(sp):
                for dst, src in loads:
                    sp.dma_start(dst[:], src).then_inc(s_w, 16)
                if L.shared:
                    sp.wait_ge(s_xn, NT)
                    sp.dma_start(g.xs[0:TOK, :].rearrange("(t p) d -> p t d", p=P), m.xn[:]).then_inc(s_sh, 16)
                    sp.wait_ge(s_sh, 16)

            @block.tensor
            def _(pe):
                def transpose(c):
                    pe.wait_ge(s_xn, CT * (c + 1))
                    for k in range(DK):
                        wait(pe, s_xt[k], c - 1)
                    for k in range(DK):
                        for a in range(CT):
                            last = nc.tensor.transpose(ps_x[:, c % 2, k, a * P:(a + 1) * P],
                                                       m.xn[:, c * CT + a, k * P:(k + 1) * P], g.ident[:])
                    last.then_inc(s_t, 1)

                transpose(0)
                pe.wait_ge(s_w, 16 * len(loads))
                for c in range(chunks):
                    if c + 1 < chunks:
                        transpose(c + 1)
                    for k in range(DK):
                        pe.wait_ge(s_xt[k], c + 1)
                    if L.n == 0:
                        for k in range(DK):
                            last = nc.tensor.matmul(ps_r[:, c % 2, :], r1[:, k, :], xt[:, c % 2, k, :], start=k == 0, stop=k == DK - 1)
                        last.then_inc(s_r1, 1)
                        pe.wait_ge(s_relu, c + 1)
                        for a in range(CT):
                            nc.tensor.matmul(ps_l[:, c * CT + a, :], hid[:, c % 2, a * P:(a + 1) * P], r2[:], start=True, stop=False)
                            last = nc.tensor.matmul(ps_l[:, c * CT + a, :], g.ones[0:1, :], rb2[:], start=False, stop=True)
                    else:
                        for a in range(CT):
                            for k in range(DK):
                                last = nc.tensor.matmul(ps_l[:, c * CT + a, :], xt[:, c % 2, k, a * P:(a + 1) * P], r1[:, k, :],
                                                        start=k == 0, stop=k == DK - 1)
                    last.then_inc(s_lg, 1)
                pe.wait_ge(s_cnt, 1)
                nc.tensor.matmul(ps_c[:, 0], g.before[:], both[:], start=True, stop=True)
                nc.tensor.matmul(ps_c[:, 1], g.ones[:], both[:], start=True, stop=True).then_inc(s_ct, 1)

            @block.scalar
            def _(act):
                nc.scalar.preload_act_table(ACT.Exp)
                for c in range(chunks):
                    act.wait_ge(s_t, c + 1)
                    wait(act, s_lg, c - 1)
                    nc.scalar.copy(xt[:, c % 2, 0, :], ps_x[:, c % 2, 0, :]).then_inc(s_xt[0], 1)
                    if L.n == 0:
                        act.wait_ge(s_r1, c + 1)
                        nc.scalar.activation(hid[:, c % 2, :], ps_r[:, c % 2, :], ACT.Relu, bias=rb1[:, 0:1]).then_inc(s_relu, 1)
                act.wait_ge(s_ch, 2)
                nc.scalar.activation(ex[:], sh[:], ACT.Exp).then_inc(s_ex, 1)
                if L.n == 0:
                    act.wait_ge(s_k, 1)
                    nc.scalar.activation(ed[:], sf[:], ACT.Exp, scale=1.0 / TOPK).then_inc(s_ex, 1)

            @block.vector
            def _(dve):
                done = [0]

                def link(ins):
                    done[0] += 1
                    ins.then_inc(s_ch, 1)
                    dve.wait_ge(s_ch, done[0])

                v = nc.vector
                for t in range(NT):
                    v.tensor_scalar(m.xn[:, t, :], g.X[:, t, :], g.mv[:, t, 0:1], g.rstd[:, t:t + 1],
                                    ALU.subtract, ALU.mult).then_inc(s_xn, 1)
                for c in range(chunks):
                    dve.wait_ge(s_t, c + 1)
                    wait(dve, s_lg, c - 1)
                    v.tensor_copy(xt[:, c % 2, 1, :], ps_x[:, c % 2, 1, :]).then_inc(s_xt[1], 1)
                dve.wait_ge(s_lg, chunks)
                e8 = lambda a: a[:].to_broadcast([P, NT, E])
                link(v.tensor_reduce(mx[:], ps_l[:], AX.X, ALU.max))
                link(v.tensor_tensor(sh[:], ps_l[:], e8(mx), ALU.subtract))
                dve.wait_ge(s_ex, 1)
                link(v.tensor_reduce(sm[:], ex[:], AX.X, ALU.add))
                link(v.reciprocal(inv[:], sm[:]))
                link(v.tensor_tensor(pro[:], ex[:], e8(inv), ALU.mult))
                link(v.tensor_scalar(far[:], g.iota_e[:], float(E), None, ALU.add))

                def choose(p, best, idx, is_it):
                    link(v.tensor_reduce(best[:], p[:], AX.X, ALU.max))
                    link(v.tensor_tensor(eq[:], p[:], e8(best), ALU.is_equal))
                    link(v.scalar_tensor_tensor(out=tmp[:], in0=eq[:], scalar=-float(E), in1=far[:], op0=ALU.mult, op1=ALU.add))
                    link(v.tensor_reduce(idx[:], tmp[:], AX.X, ALU.min))
                    link(v.tensor_tensor(is_it[:], g.iota_e[:], e8(idx), ALU.is_equal))

                choose(pro, p1, i1, is1)
                link(v.scalar_tensor_tensor(out=pro2[:], in0=is1[:], scalar=-4.0, in1=pro[:], op0=ALU.mult, op1=ALU.add))
                choose(pro2, p2, i2, is2)
                link(v.tensor_tensor(both[:], is1[:], is2[:], ALU.add))
                v.tensor_copy(offs[:, 0, :], both[:, 0, :]).then_inc(s_cnt, 1)
                if L.n == 0:
                    v.tensor_tensor(sf[:], p2[:], p1[:], ALU.subtract).then_inc(s_k, 1)
                    dve.wait_ge(s_ex, 2)
                    link(v.tensor_scalar(sf[:], ed[:], 1.0, None, ALU.add))
                    link(v.reciprocal(m.wt[:, 0, :], sf[:, :, 0]))
                    link(v.tensor_tensor(m.wt[:, 1, :], m.wt[:, 0, :], ed[:, :, 0], ALU.mult))
                else:
                    link(v.tensor_copy(m.wt[:, 0, :], p1[:, :, 0]))
                    link(v.tensor_copy(m.wt[:, 1, :], p2[:, :, 0]))
                dve.wait_ge(s_ct, 1)
                link(v.memset(offs[:, 0, :], 0.0))
                for t in range(1, NT):
                    link(v.tensor_tensor(offs[:, t, :], offs[:, t - 1, :], ps_c[:, 1, t - 1, :], ALU.add))
                link(v.tensor_tensor(n_e[:, :, 0], offs[:, NT - 1, :], ps_c[:, 1, NT - 1, :], ALU.add))
                link(v.tensor_tensor(over[:], n_e[:].to_broadcast([P, E, TOK // ST]), g.iota_thr[:], ALU.is_gt))
                link(v.tensor_reduce(nt_e[:], over[:], AX.X, ALU.add))
                link(v.tensor_copy(ends[:, 0, :], nt_e[:, 0, :]))
                for e in range(1, E):
                    link(v.tensor_tensor(ends[:, e, :], ends[:, e - 1, :], nt_e[:, e, :], ALU.add))
                link(v.tensor_tensor(start[:, 0, :], ends[:, :, 0], nt_e[:, :, 0], ALU.subtract))
                link(v.tensor_scalar(start[:], start[:], float(ST), float(L.sh_tiles * ST), ALU.mult, ALU.add))
                link(v.tensor_tensor(slot[:], ps_c[:, 0], offs[:], ALU.add))
                link(v.tensor_tensor(slot[:], slot[:], start[:].to_broadcast([P, NT, E]), ALU.add))
                for i, is_it in enumerate((is1, is2)):
                    link(v.tensor_tensor(tmp[:], slot[:], is_it[:], ALU.mult))
                    link(v.tensor_reduce(mx[:], tmp[:], AX.X, ALU.add))
                    v.tensor_copy(m.slots[:, i, :], mx[:, :, 0]).then_inc(s_k, 1)
                link(v.tensor_tensor(past[:], ends[0:1, :, :].rearrange("p e a -> p a e").to_broadcast([1, ROUTED, E]),
                                     g.iota_tile[0:1], ALU.is_le))
                link(v.tensor_reduce(tile_e[:], past[:], AX.X, ALU.add))
                link(v.tensor_scalar(tile_e[:], tile_e[:], float(E - 1), None, ALU.min))
                if L.sh_tiles:
                    link(v.memset(m.eid[:, 0:L.sh_tiles], E))
                link(v.tensor_copy(m.eid[:, L.sh_tiles:L.tiles], tile_e[:, :, 0]))

            @block.gpsimd
            def _(pool):
                pool.wait_ge(s_k, 2 + (L.n == 0))
                for t in range(NT):
                    for i in range(TOPK):
                        nc.gpsimd.indirect_dma_start(
                            out=g.xs, out_offset=bass.IndirectOffsetOnAxis(ap=m.slots[:, i, t:t + 1], axis=0),
                            in_=m.xn[:, t, :], in_offset=None).then_inc(s_sc, 16)
                pool.wait_ge(s_sc, 16 * NT * TOPK)


def experts(nc, g, m, L, w, sem):
    T = f"e{L.n}_"
    s_w1d, s_w2d, s_xl, s_bl = ([sem(f"{T}{n}_loaded{q}") for q in range(2)] for n in ("w1", "w2", "x", "b2"))
    s_st = [sem(f"{T}stored{q}") for q in range(2)]
    s_w1h, s_w1l, s_w2h, s_w2l = sem(T + "w1_high"), sem(T + "w1_low"), sem(T + "w2_high"), sem(T + "w2_low")
    s_tr, s_xh, s_xlo = sem(T + "x_transposed"), sem(T + "x_high"), sem(T + "x_low")
    s_m1, s_h, s_hh, s_hl = sem(T + "first"), sem(T + "hidden"), sem(T + "hidden_high"), sem(T + "hidden_low")
    s_m2, s_ev = sem(T + "second"), sem(T + "evacuated")
    M1, MP, J = L.m1, L.m1 // 2, L.tiles
    W1 = DK * L.hid
    slots_h = min(4, 2 * MP)
    with ExitStack() as ctx:
        sb = lambda name, shape, dt=FP: ctx.enter_context(nc.sbuf_tensor(T + name, shape, dt))
        pb = lambda name, shape: ctx.enter_context(nc.psum_tensor(T + name, shape, FP))
        w1s, w2s, b1s = sb("w1s", [P, 2, W1]), sb("w2s", [P, 2, W1]), sb("b1s", [P, 2, M1])
        w1h, w1l = sb("w1h", [P, 2, W1], FR), sb("w1l", [P, 2, W1], FR)
        w2h, w2l = sb("w2h", [P, 2, W1], FR), sb("w2l", [P, 2, W1], FR)
        xin = sb("xin", [P, 2, ST // P, D])
        xh, xl = sb("xh", [P, 2, DK, ST], FR), sb("xl", [P, 2, DK, ST], FR)
        hf = sb("hf", [P, M1, ST])
        hh, hl = sb("hh", [P, 2, M1, ST], FR), sb("hl", [P, 2, M1, ST], FR)
        b2s, yo = sb("b2s", [P, 2, 1, D]), sb("yo", [P, 2, ST // P, D])
        ps_x = pb("ps_x", [P, 2, DK, ST])
        ps_h = pb("ps_h", [P, 4, 2, ST])
        ps_o = pb("ps_o", [P, 2, ST // P, D])
        arrived = lambda j, q: 8 * j + (8 if q else 16)
        both = lambda value: 2 * value
        first = lambda a, q, k, i: a[:, q, k * L.hid + i * P:k * L.hid + (i + 1) * P]
        second = lambda a, q, i: a[:, q, i * D:(i + 1) * D]

        def steps(eng, body, lo, hi):
            mid = 3, J - 2
            for j in range(lo, mid[0]):
                body(j, j % 2)
            with eng.Fori(mid[0], mid[1] - 1, 2) as i:
                body(i, 1)
                body(i + 1, 0)
            for j in range(mid[1], hi):
                body(j, j % 2)

        with nc.Block() as block:
            @block.sync
            def _(sp):
                def expert(j):
                    return sp.value_load(m.eid[0:1, j:j + 1] if isinstance(j, int) else m.eid[0:1, bass.ds(j, 1)],
                                         min_val=0, max_val=w["w1"].shape[0] - 1)

                def of(a, e):
                    return w[a][bass.ds(e, 1)].rearrange("a p n -> p (a n)")

                def step(j, q):
                    static = isinstance(j, int)
                    if not static or j < J:
                        e = expert(j)
                        wait(sp, s_w1l, j - 1)
                        sp.dma_start(w1s[:, q, :], of("w1", e)).then_inc(s_w1d[q], 16)
                        wait(sp, s_tr, j - 1)
                        rows = g.xs.rearrange("(j a p) d -> j p a d", p=P, a=ST // P)
                        rows = rows[j] if static else rows[bass.ds(j, 1)].rearrange("j p a d -> p (j a) d")
                        sp.dma_start(xin[:, q], rows).then_inc(s_xl[q], 16)
                    if not static or j >= 1:
                        e = expert(j - 1)
                        wait(sp, s_w2l, j - 2)
                        sp.dma_start(w2s[:, 1 - q, :], of("w2", e)).then_inc(s_w2d[1 - q], 16)
                        wait(sp, s_ev, j - 2)
                        sp.dma_start(b1s[:, 1 - q, :], of("b1", e)).then_inc(s_bl[1 - q], 16)
                        sp.dma_start(b2s[:, 1 - q, 0, :], w["b2"][bass.ds(e, 1), :].to_broadcast([P, D])).then_inc(s_bl[1 - q], 16)
                steps(sp, step, 0, J + 1)

            @block.tensor
            def _(pe):
                def step(j, q):
                    static = isinstance(j, int)
                    if not static or j + 1 < J:
                        wait(pe, s_xl[1 - q], arrived(j + 1, 1 - q))
                        wait(pe, s_xlo, j)
                        for k in range(DK):
                            for a in range(ST // P):
                                last = nc.tensor.transpose(ps_x[:, 1 - q, k, a * P:(a + 1) * P],
                                                           xin[:, 1 - q, a, k * P:(k + 1) * P], g.ident[:])
                        last.then_inc(s_tr, 1)
                    if not static or 0 <= j < J:
                        wait(pe, s_w1l, j + 1)
                        wait(pe, s_xlo, j + 1)
                        for mp in range(MP):
                            wait(pe, s_h, j * MP + mp + 1 - slots_h)
                            for i in range(2):
                                o = ps_h[:, (q * MP + mp) % 4, i, :]
                                for k in range(DK):
                                    last = product(nc, o, (first(w1h, q, k, 2 * mp + i), first(w1l, q, k, 2 * mp + i)),
                                                   (xh[:, q, k, :], xl[:, q, k, :]), k == 0, k == DK - 1)
                            last.then_inc(s_m1, 1)
                    if not static or j >= 1:
                        wait(pe, s_hl, MP * j)
                        wait(pe, s_w2l, j)
                        wait(pe, s_ev, j - 2)
                        for a in range(ST // P):
                            o = ps_o[:, 1 - q, a, :]
                            for i in range(M1):
                                ts = slice(a * P, (a + 1) * P)
                                last = product(nc, o, (hh[:, 1 - q, i, ts], hl[:, 1 - q, i, ts]),
                                               (second(w2h, 1 - q, i), second(w2l, 1 - q, i)), i == 0, i == M1 - 1)
                        last.then_inc(s_m2, 1)
                steps(pe, step, -1, J + 1)

            @block.scalar
            def _(act):
                def step(j, q):
                    static = isinstance(j, int)
                    if not static or j + 1 < J:
                        wait(act, s_w1d[1 - q], arrived(j + 1, 1 - q))
                        wait(act, s_m1, MP * j)
                        nc.scalar.copy(w1h[:, 1 - q, :], w1s[:, 1 - q, :]).then_inc(s_w1h, 1)
                        wait(act, s_tr, j + 2)
                        nc.scalar.copy(xh[:, 1 - q], ps_x[:, 1 - q]).then_inc(s_xh, 1)
                    if not static or 0 <= j < J:
                        wait(act, s_bl[q], both(arrived(j, q)))
                        for mp in range(MP):
                            wait(act, s_m1, j * MP + mp + 1)
                            wait(act, s_hl, (j - 1) * MP + mp + 1)
                            for i in range(2):
                                c = 2 * mp + i
                                last = nc.scalar.activation(hf[:, 2 * mp + i, :], ps_h[:, (q * MP + mp) % 4, i, :], L.func,
                                                            bias=b1s[:, q, c:c + 1])
                            last.then_inc(s_h, 1)
                            wait(act, s_h, j * MP + mp + 1)
                            wait(act, s_m2, j - 1)
                            nc.scalar.copy(hh[:, q, 2 * mp:2 * mp + 2, :], hf[:, 2 * mp:2 * mp + 2, :]).then_inc(s_hh, 1)
                    if not static or j >= 2:
                        wait(act, s_ev, j - 1)
                        rows = g.ys.rearrange("(j a p) d -> j p a d", p=P, a=ST // P)
                        rows = rows[j - 2] if static else rows[bass.ds(j - 2, 1)].rearrange("j p a d -> p (j a) d")
                        act.dma_start(rows, yo[:, q]).then_inc(s_st[q], 16)
                nc.scalar.preload_act_table(L.func)
                steps(act, step, -1, J + 2)
                act.wait_ge(s_st[0], arrived(J - 1 - (J - 1) % 2, 0))
                act.wait_ge(s_st[1], arrived(J - 2 + (J - 1) % 2, 1))

            @block.vector
            def _(dve):
                def step(j, q):
                    static = isinstance(j, int)
                    if not static or j + 1 < J:
                        wait(dve, s_w1h, j + 2)
                        nc.vector.tensor_tensor(w1l[:, 1 - q, :], w1s[:, 1 - q, :], w1h[:, 1 - q, :], ALU.subtract).then_inc(s_w1l, 1)
                        wait(dve, s_xh, j + 2)
                        nc.vector.tensor_tensor(xl[:, 1 - q], ps_x[:, 1 - q], xh[:, 1 - q], ALU.subtract).then_inc(s_xlo, 1)
                    if not static or 0 <= j < J:
                        for mp in range(MP):
                            wait(dve, s_hh, j * MP + mp + 1)
                            nc.vector.tensor_tensor(hl[:, q, 2 * mp:2 * mp + 2, :], hf[:, 2 * mp:2 * mp + 2, :],
                                                    hh[:, q, 2 * mp:2 * mp + 2, :], ALU.subtract).then_inc(s_hl, 1)
                    if not static or 1 <= j <= J:
                        wait(dve, s_m2, j)
                        wait(dve, s_bl[1 - q], both(arrived(j - 1, 1 - q)))
                        if static:
                            n = j - 3
                            if n >= 0:
                                wait(dve, s_st[n % 2], arrived(n, n % 2))
                        else:
                            wait(dve, s_st[1 - q], arrived(j - 3, 1 - q))
                        nc.vector.tensor_tensor(yo[:, 1 - q], ps_o[:, 1 - q], b2s[:, 1 - q].to_broadcast([P, ST // P, D]),
                                                ALU.add).then_inc(s_ev, 1)
                    if not static or j + 1 < J:
                        wait(dve, s_m2, j)
                        wait(dve, s_w2d[1 - q], arrived(j + 1, 1 - q))
                        nc.vector.tensor_copy(w2h[:, 1 - q, :], w2s[:, 1 - q, :]).then_inc(s_w2h, 1)
                        wait(dve, s_w2h, j + 2)
                        nc.vector.tensor_tensor(w2l[:, 1 - q, :], w2s[:, 1 - q, :], w2h[:, 1 - q, :], ALU.subtract).then_inc(s_w2l, 1)
                steps(dve, step, -1, J + 1)


def combine(nc, g, m, L, sem, out):
    T = f"c{L.n}_"
    NBUF = 4
    s_g = [sem(f"{T}gathered{q}") for q in range(NBUF)]
    s_gs = [sem(f"{T}shared_loaded{q}") for q in range(NBUF)] if L.shared else None
    s_f, s_x, s_bn, s_out = sem(T + "used"), sem(T + "x"), sem(T + "bn"), sem(T + "stored")
    NY = TOPK + L.shared
    with ExitStack() as ctx:
        y = ctx.enter_context(nc.sbuf_tensor(T + "y", [P, NBUF, NY, D], FP))
        with nc.Block() as block:
            @block.gpsimd
            def _(pool):
                for t in range(NT):
                    wait(pool, s_f, t + 1 - NBUF)
                    for i in range(TOPK):
                        nc.gpsimd.indirect_dma_start(
                            out=y[:, t % NBUF, i, :], out_offset=None, in_=g.ys,
                            in_offset=bass.IndirectOffsetOnAxis(ap=m.slots[:, i, t:t + 1], axis=0)).then_inc(s_g[t % NBUF], 16)

            @block.sync
            def _(sp):
                for t in range(NT):
                    if L.shared:
                        wait(sp, s_f, t + 1 - NBUF)
                        sp.dma_start(y[:, t % NBUF, TOPK, :], g.ys[t * P:(t + 1) * P, :]).then_inc(s_gs[t % NBUF], 16)
                if out is not None:
                    for t in range(NT):
                        sp.wait_ge(s_f, t + 1)
                        sp.dma_start(out[t * P:(t + 1) * P, :], g.X[:, t, :]).then_inc(s_out, 16)
                    sp.wait_ge(s_out, 16 * NT)

            @block.vector
            def _(dve):
                for t in range(NT):
                    dve.wait_ge(s_g[t % NBUF], 16 * TOPK * (t // NBUF + 1))
                    if L.shared:
                        dve.wait_ge(s_gs[t % NBUF], 16 * (t // NBUF + 1))
                    x = g.X[:, t, :]
                    for i in range(NY):
                        if i < TOPK:
                            ins = nc.vector.scalar_tensor_tensor(out=x, in0=y[:, t % NBUF, i, :], scalar=m.wt[:, i, t:t + 1],
                                                                 in1=x, op0=ALU.mult, op1=ALU.add)
                        else:
                            ins = nc.vector.tensor_tensor(x, x, y[:, t % NBUF, i, :], ALU.add)
                        if i == NY - 1:
                            ins.then_inc(s_f, 1)
                            dve.wait_ge(s_f, t + 1)
                        else:
                            ins.then_inc(s_x, 1)
                            dve.wait_ge(s_x, t * (NY - 1) + i + 1)
                    if out is None:
                        nc.vector.bn_stats(g.stats[:, t, :], x).then_inc(s_bn, 1)
                if out is None:
                    dve.wait_ge(s_bn, NT)
                    for t in range(NT):
                        nc.vector.bn_aggr(g.mv[:, t, :], g.stats[:, t, :])


def mixture(nc, g, L, w, sem, out):
    with ExitStack() as ctx:
        sb = lambda name, shape, dt=FP: ctx.enter_context(nc.sbuf_tensor(f"m{L.n}_{name}", shape, dt))
        m = Shared()
        m.wt, m.slots = sb("weights", [P, TOPK, NT]), sb("slots", [P, TOPK, NT], I32)
        m.eid = sb("tile_expert", [1, L.tiles + 1], I32)
        with ExitStack() as ctx2:
            m.xn = ctx2.enter_context(nc.sbuf_tensor(f"m{L.n}_xn", [P, NT, D], FP))
            route(nc, g, m, L, w, sem)
        experts(nc, g, m, L, w, sem)
        combine(nc, g, m, L, sem, out)


def clear(nc, handles):
    with nc.Block() as block:
        @block.gpsimd
        def _(pool):
            for h in handles:
                pool.sem_clear(h)


def build(nc, t, out):
    with ExitStack() as ctx:
        handles = []

        def sem(name):
            handles.append(nc.alloc_semaphore(name=name))
            return handles[-1]

        g = allocate(nc, ctx)
        part = lambda p: {k[len(p):]: a for k, a in t.items() if k.startswith(p)}
        prepare(nc, g, t["x"], sem)
        for L in LAYERS:
            if L.n:
                clear(nc, handles)
                for h in handles:
                    nc.release_semaphore(h)
                handles.clear()
            inverse_deviation(nc, g, sem, f"a{L.n}")
            with ExitStack() as attn:
                attention_operands(nc, attn, g, L)
                attention_setup(nc, g, L, {**part(f"a{L.n}_"), "ctx": t["ctx"]}, sem)
                attention(nc, g, L, sem)
            inverse_deviation(nc, g, sem, f"m{L.n}")
            mixture(nc, g, L, part(f"m{L.n}_"), sem, out if L is LAYERS[-1] else None)


def host_layouts(inputs):
    import numpy as np
    c = np.ascontiguousarray
    f = {k: np.asarray(v) for k, v in inputs.items()}
    out = {"x": c(f["x"].reshape(TOK, D))}
    out["ctx"] = c(f["ctx_768"].transpose(2, 0, 1).reshape(CK, CP, NB, KEYS).transpose(1, 0, 2, 3))
    rows = lambda a, p: c(a.reshape(a.shape[0] // p, p, a.shape[1]).transpose(1, 0, 2))
    a0 = lambda k: f["L0_xattn_" + k]
    a1 = lambda k: f["L1_xattn_" + k]
    out.update({
        "a0_wk": rows(a0("Wk"), CP), "a0_wv": rows(a0("Wv"), CP),
        "a0_wki": rows(a0("Wk_ipa"), CP), "a0_wvi": rows(a0("Wv_ipa"), CP),
        "a0_wq": rows(a0("Wq").T, P), "a0_wo": rows(a0("Wo"), P), "a0_bo": c(a0("bo")[None, :]),
        "a0_kd": rows(a0("k_down"), CP), "a0_vd": rows(a0("v_down"), CP),
        "a0_ku": c(a0("k_up")), "a0_vu": c(a0("v_up")),
        "a0_qu": rows(a0("q_up").T, P), "a0_qd": c(a0("q_down").T),
        "a0_od": rows(a0("o_down"), P), "a0_ou": c(a0("o_up")),
        "a0_alphas": c(np.concatenate([a0(k + "_alpha") for k in "qkvo"])[None, :]),
        "a1_wk": rows(a1("Wk").T, CP), "a1_wv": rows(a1("Wv").T, CP),
        "a1_wq": rows(a1("Wq"), P), "a1_wo": rows(a1("Wo").T, P), "a1_bo": c(a1("bo")[None, :]),
        "a1_bq": c(a1("bq").reshape(-1, P).T), "a1_bk": c(a1("bk").reshape(-1, P).T), "a1_bv": c(a1("bv").reshape(-1, P).T),
    })

    def experts(p, w1, b1, w2, b2):
        n, _, hid = w1.shape
        out[p + "w1"] = c(w1.reshape(n, DK, P, hid).transpose(0, 2, 1, 3).reshape(n, P, -1))
        out[p + "b1"] = c(b1.reshape(n, hid // P, P).transpose(0, 2, 1))
        out[p + "w2"] = c(w2.reshape(n, hid // P, P, D).transpose(0, 2, 1, 3).reshape(n, P, -1))
        out[p + "b2"] = c(b2)

    m0 = lambda k: f["L0_ffn_" + k]
    m1 = lambda k: f["L1_ffn_" + k]
    with_shared = lambda e, s: np.concatenate([e, s[None]], axis=0)
    experts("m0_", *(with_shared(m0(e), m0(one)) for e, one in (("We1", "Ws1"), ("be1", "bs1"), ("We2", "Ws2"), ("be2", "bs2"))))
    experts("m1_", m1("w_in"), m1("b_in"), m1("w_out"), m1("b_out"))
    out.update({
        "m0_r1": rows(m0("Wr1"), P), "m0_rb1": c(m0("br1")[:, None]), "m0_r2": c(m0("Wr2")), "m0_rb2": c(m0("br2")[None, :]),
        "m1_r": rows(m1("router_w"), P),
    })
    return out


def kernel(**inputs):
    import concourse.bacc as _bacc
    from concourse.bass_utils import run_bass_kernel_spmd as _run

    nc = _bacc.Bacc("TRN2", target_bir_lowering=False, num_devices=1)
    arrays, aps = {}, {}
    for name, a in host_layouts(inputs).items():
        arrays[f"in_{name}"] = a
        aps[name] = nc.dram_tensor(f"in_{name}", a.shape, mybir.dt.from_np(a.dtype), kind="ExternalInput").ap()
    out = nc.dram_tensor("out", (TOK, D), FP, kind="ExternalOutput").ap()
    build(nc, aps, out)
    r = _run(nc, [arrays], core_ids=[0])
    return r.results[0]["out"].reshape(NB, SEQ, D)
```

```python
from contextlib import ExitStack

import concourse.bass as bass
from concourse import mybir

FP = mybir.dt.float32
FR = mybir.dt.float32r
I32 = mybir.dt.int32
ALU = mybir.AluOpType
ACT = mybir.ActivationFunctionType
AX = mybir.AxisListType



P = 128
NB, SEQ, D = 2, 1024, 256
TOK = NB * SEQ
NT = TOK // P
DK = D // P
KEYS, IPA, DC = 77, 4, 192
CP, CK = 96, 2
RANK = 32
E, TOPK = 8, 2
ST = 256
ROUTED = (TOK * TOPK + E * (ST - 1)) // ST
EPS = 1e-5
LOW = 32
SPLIT = LOW + 1

class Layer:

    def __init__(self, n, heads, dh, segments, lora, hid, shared, func):
        self.n, self.heads, self.dh, self.segments = n, heads, dh, segments
        self.lora, self.hid, self.shared, self.func = lora, hid, shared, func
        self.scale = dh ** -0.5
        self.hp = P // dh
        self.groups = heads // self.hp
        self.n_g = self.hp * KEYS
        self.cols = heads * KEYS
        self.chunks = -(-self.cols // P)
        self.pad = self.chunks * P
        banks = -(-self.cols // 512)
        self.banks, self.piece = (banks, self.cols // banks) if heads % banks == 0 else (1, 512)
        self.c0 = [g * self.n_g // P for g in range(self.groups)]
        self.win = [P * (((g + 1) * self.n_g - 1) // P - self.c0[g] + 1) for g in range(self.groups)]
        self.m1 = hid // P
        self.sh_tiles = TOK // ST if shared else 0
        self.tiles = ROUTED + self.sh_tiles


LAYERS = [
    Layer(0, 16, 64, [(0, KEYS - IPA), (KEYS - IPA, KEYS)], True, 1024, True, ACT.Silu),
    Layer(1, 8, 32, [(0, KEYS)], False, 256, False, ACT.Gelu_apprx_tanh),
]


class Shared:
    pass


def wait(eng, sem, value):
    if not isinstance(value, int) or value > 0:
        eng.wait_ge(sem, value)


def one(ap, i):
    return ap[:, i:i + 1] if isinstance(i, int) else ap[:, bass.ds(i, 1)]


def product(nc, out, lhs, rhs, start, stop):
    (lh, ll), (rh, rl) = lhs, rhs
    nc.tensor.matmul(out, lh, rh, start=start, stop=False)
    nc.tensor.matmul(out, lh, rl, start=False, stop=False)
    return nc.tensor.matmul(out, ll, rh, start=False, stop=stop)


class Prepare:

    def __init__(self, nc, g, x, sem):
        self.nc, self.g, self.x = nc, g, x
        self.s_x, self.s_c, self.s_st = sem("prep_x_loaded"), sem("prep_const"), sem("prep_stats")
        self.s_zf = sem("prep_zero_tile")

    def load(self, sp):
        sp.dma_start(self.g.X[:], self.x.rearrange("(t p) d -> p t d", p=P)).then_inc(self.s_x, 16)

    def zero_slots(self, sp):
        rows = self.g.xs.rearrange("(a p) d -> p a d", p=P)
        sp.wait_ge(self.s_zf, 1)
        for a in range(0, rows.shape[1], 2):
            sp.dma_start(rows[:, a:a + 2, :], self.g.zero[:].rearrange("p (a d) -> p a d", a=2)).then_inc(self.g.s_zeroed, 16)

    def constants(self, pool):
        g, gp = self.g, self.nc.gpsimd
        gp.memset(g.ident[:], 0.0).then_inc(self.s_c, 1)
        gp.memset(g.before[:], 1.0).then_inc(self.s_c, 1)
        gp.memset(g.ones[:], 1.0).then_inc(self.s_c, 1)
        pool.wait_ge(self.s_c, 3)
        gp.affine_select(out=g.ident[:], in_=g.ident[:], compare_op=ALU.not_equal, fill=1.0,
                         base=0, pattern=[[-1, P]], channel_multiplier=1).then_inc(self.s_c, 1)
        gp.affine_select(out=g.before[:], in_=g.before[:], compare_op=ALU.is_gt, fill=0.0,
                         base=0, pattern=[[1, P]], channel_multiplier=-1).then_inc(self.s_c, 1)
        gp.iota(g.iota_e[:], pattern=[[0, NT], [1, E]], base=0, channel_multiplier=0,
                allow_small_or_imprecise_dtypes=True).then_inc(self.s_c, 1)
        gp.iota(g.iota_thr[:], pattern=[[0, E], [ST, TOK // ST]], base=0, channel_multiplier=0,
                allow_small_or_imprecise_dtypes=True).then_inc(self.s_c, 1)
        gp.iota(g.iota_tile[:], pattern=[[1, ROUTED], [0, E]], base=0, channel_multiplier=0,
                allow_small_or_imprecise_dtypes=True).then_inc(self.s_c, 1)
        gp.memset(g.zero[:], 0.0).then_inc(self.s_zf, 1)

    def ones(self, dve):
        dve.wait_ge(self.s_c, 8)
        self.nc.vector.tensor_copy(self.g.ones_r[:], self.g.ones[0:SPLIT, :]).then_inc(self.s_st, 1)

    def tile_statistics(self, dve, t):
        if t == 0:
            dve.wait_ge(self.s_x, 16)
        self.nc.vector.bn_stats(self.g.stats[:, t, :], self.g.X[:, t, :]).then_inc(self.s_st, 1)

    def statistics(self, dve):
        g, v = self.g, self.nc.vector
        dve.wait_ge(self.s_st, 1 + NT)
        for t in range(NT):
            last = v.bn_aggr(g.mv[:, t, :], g.stats[:, t, :])
        last.then_inc(self.s_st, 1)
        dve.wait_ge(self.s_st, 2 + NT)


class InverseDeviation:

    def __init__(self, nc, g, sem, tag):
        self.nc, self.g = nc, g
        self.s_v, self.s_q, self.s_r = sem(tag + "_var_eps"), sem(tag + "_sqrt"), sem(tag + "_chain")

    def act(self, act):
        act.wait_ge(self.s_v, 1)
        self.nc.scalar.activation(self.g.sq[:], self.g.ve[:], ACT.Sqrt).then_inc(self.s_q, 1)

    def dve(self, dve):
        g, v, s_r = self.g, self.nc.vector, self.s_r
        v.tensor_scalar(g.ve[:], g.mv[:, :, 1], EPS, None, ALU.add).then_inc(self.s_v, 1)
        dve.wait_ge(self.s_q, 1)
        v.reciprocal(g.rstd[:], g.sq[:]).then_inc(s_r, 1)
        dve.wait_ge(s_r, 1)
        v.tensor_tensor(g.sq[:], g.rstd[:], g.rstd[:], ALU.mult).then_inc(s_r, 1)
        dve.wait_ge(s_r, 2)
        v.tensor_tensor(g.sq[:], g.sq[:], g.ve[:], ALU.mult).then_inc(s_r, 1)
        dve.wait_ge(s_r, 3)
        v.tensor_scalar(g.sq[:], g.sq[:], -0.5, 1.5, ALU.mult, ALU.add).then_inc(s_r, 1)
        dve.wait_ge(s_r, 4)
        v.tensor_tensor(g.rstd[:], g.rstd[:], g.sq[:], ALU.mult).then_inc(s_r, 1)
        dve.wait_ge(s_r, 5)


def attention_setup(nc, g, L, w, sem, prepare, before):
    T = f"as{L.n}_"
    s_wq, s_lq = sem(T + "wq_wo_loaded"), sem(T + "low_rank_loaded")
    deviation = InverseDeviation(nc, g, sem, T + "ln")
    s_w, s_wk, s_wv = sem(T + "context_loaded"), sem(T + "wk_loaded"), sem(T + "wv_loaded")
    s_zero, s_al = sem(T + "zeroed"), sem(T + "alpha")
    s_lk, s_lk_sb = sem(T + "ctx_lora"), sem(T + "ctx_lora_copied")
    s_kv, s_bd = sem(T + "kv"), sem(T + "block_diagonal")
    s_u, s_u_sb = sem(T + "low_rank"), sem(T + "low_rank_copied")
    s_a, s_ahi, s_alo = sem(T + "a"), sem(T + "a_high"), sem(T + "a_low")
    s_b, s_bhi, s_blo = sem(T + "b"), sem(T + "b_high"), sem(T + "b_low")
    s_r = sem(T + "rows")
    G, n, hp, dh = L.groups, L.n_g, L.hp, L.dh
    HD = L.heads * dh
    org = KEYS - IPA
    KA = min(DK, 512 // n)
    with ExitStack() as ctx:
        sb = lambda name, shape, dt=FP: ctx.enter_context(nc.sbuf_tensor(T + name, shape, dt))
        pb = lambda name, shape: ctx.enter_context(nc.psum_tensor(T + name, shape, FP))
        c = sb("ctx", [CP, CK, NB, KEYS])
        wk, wv = sb("wk", [CP, CK, HD]), sb("wv", [CP, CK, HD])
        wq, wo = sb("wq", [P, G, D]), sb("wo", [P, G, D])
        bo = sb("bo", [1, D])
        loads, loads_k, loads_v = [(c, w["ctx"])], [(wk, w["wk"])], [(wv, w["wv"])]
        loads_q, loads_lq = [(wq, w["wq"]), (wo, w["wo"]), (bo, w["bo"])], []
        if L.lora:
            wki, wvi = sb("wki", [CP, CK, HD]), sb("wvi", [CP, CK, HD])
            kd, vd = sb("kd", [CP, CK, RANK]), sb("vd", [CP, CK, RANK])
            ku, vu = sb("ku", [RANK, HD]), sb("vu", [RANK, HD])
            qu, qd = sb("qu", [RANK, HD]), sb("qd", [RANK, D])
            od, ou = sb("od", [RANK, HD]), sb("ou", [RANK, D])
            al = sb("al", [RANK, 4])
            loads = [(kd, w["kd"]), (vd, w["vd"]), (al, w["alphas"].to_broadcast([RANK, 4]))] + loads
            loads_k += [(ku, w["ku"]), (wki, w["wki"])]
            loads_v += [(vu, w["vu"]), (wvi, w["wvi"])]
            loads_lq = [(qu, w["qu"]), (qd, w["qd"]), (od, w["od"]), (ou, w["ou"])]
            low = sb("low", [RANK, 2, NB, org])
        else:
            bq, bk, bv = sb("bq", [P, G]), sb("bk", [P, G]), sb("bv", [P, G])
            loads_k.append((bk, w["bk"]))
            loads_v.append((bv, w["bv"]))
            loads_q += [(bq, w["bq"])]
        kbd = sb("kbd", [P, G, NB, n])
        vbd = sb("vbd", [P, NB, sum(L.win)])
        ps_kv = pb("ps_kv", [P, 2, 2, 256])
        ps_u = pb("ps_u", [P, 2, 512])
        ps_a = pb("ps_a", [P, 2, 512])
        ps_b = pb("ps_b", [P, 2, 2, D])
        half_a = lambda i: ps_a[:, i % 2, 0:KA * n].rearrange("p (k j) -> p k j", k=KA)
        base = [sum(L.win[:gi]) for gi in range(G)]
        off = [base[gi] + gi * n - P * L.c0[gi] for gi in range(G)]
        a_items = [(b, k) for b in range(NB) for k in range(0, DK, KA)]
        b_items = [(b, ch, min(2, L.chunks - ch)) for b in range(NB) for ch in range(0, L.chunks, 2)]

        with nc.Block() as block:
            @block.sync
            def _(sp):
                for group, loaded in ((loads, s_w), (loads_k, s_wk), (loads_v, s_wv), (loads_lq, s_lq), (loads_q, s_wq)):
                    for dst, src in group:
                        sp.dma_start(dst[:], src).then_inc(loaded, 16)
                if prepare:
                    prepare.load(sp)
                if prepare:
                    prepare.zero_slots(sp)
                if before:
                    before.sync(sp)

            n_u = 2

            @block.tensor
            def _(pe):
                pe.wait_ge(s_w, 16 * len(loads))
                if L.lora:
                    for i, down in enumerate((kd, vd)):
                        o = ps_u[0:RANK, i, 0:NB * org].rearrange("p (b j) -> p b j", b=NB)
                        for k in range(CK):
                            last = nc.tensor.matmul(o, down[:, k, :], c[:, k, :, 0:org], start=k == 0, stop=k == CK - 1)
                        last.then_inc(s_lk, 1)

                def keys_values(gi):
                    wait(pe, s_bd, gi - 1)
                    for i, (main, ipa, up) in enumerate(((wk, wki, ku), (wv, wvi, vu)) if L.lora else ((wk, 0, 0), (wv, 0, 0))):
                        o = ps_kv[:, gi % 2, i, 0:NB * KEYS].rearrange("p (b j) -> p b j", b=NB)
                        gs = slice(gi * P, gi * P + P)
                        m = org if L.lora else KEYS
                        if gi == 0:
                            pe.wait_ge((s_wk, s_wv)[i], 16 * len((loads_k, loads_v)[i]))
                        for k in range(CK):
                            last = nc.tensor.matmul(o[:, :, 0:m], main[:, k, gs], c[:, k, :, 0:m], start=k == 0,
                                                    stop=not L.lora and k == CK - 1)
                        if L.lora:
                            if gi == 0 and i == 0:
                                pe.wait_ge(s_lk_sb, 2)
                            nc.tensor.matmul(o[:, :, 0:m], up[:, gs], low[:, i], start=False, stop=True)
                            for k in range(CK):
                                last = nc.tensor.matmul(o[:, :, m:], ipa[:, k, gs], c[:, k, :, m:], start=k == 0,
                                                        stop=k == CK - 1)
                    last.then_inc(s_kv, 1)

                keys_values(0)
                keys_values(1)
                if L.lora:
                    pe.wait_ge(s_al, 2)
                for gi in range(G):
                    gs = slice(gi * P, gi * P + P)
                    if L.lora:
                        for r, (up, down) in enumerate(((qu, qd), (od, ou))):
                            wait(pe, s_u_sb, gi * n_u + r - 1)
                            nc.tensor.matmul(ps_u[:, r, 0:D], up[:, gs], down[:], start=True, stop=True).then_inc(s_u, 1)
                    if gi + 2 < G:
                        keys_values(gi + 2)
                    if gi == 0:
                        pe.wait_ge(s_wq, 16 * len(loads_q))
                    pe.wait_ge(s_bd, gi + 1)
                    if not L.lora:
                        for b in range(NB):
                            wait(pe, s_u_sb, gi * n_u + b - 1)
                            nc.tensor.matmul(ps_u[0:1, b, 0:n], bq[:, gi:gi + 1], kbd[:, gi, b, :], start=True,
                                             stop=True).then_inc(s_u, 1)
                    else:
                        pe.wait_ge(s_u_sb, gi * n_u + 2)
                    for j, (b, k0) in enumerate(a_items):
                        a = gi * len(a_items) + j
                        wait(pe, s_alo, a - 1)
                        for k in range(k0, k0 + KA):
                            last = nc.tensor.matmul(half_a(a)[:, k - k0, :], wq[:, gi, k * P:(k + 1) * P], kbd[:, gi, b, :],
                                                    start=True, stop=True)
                        last.then_inc(s_a, 1)
                for i, (b, ch0, nch) in enumerate(b_items):
                    wait(pe, s_blo, i - 1)
                    for ch in range(ch0, ch0 + nch):
                        over = [gi for gi in range(G) if gi * n < (ch + 1) * P and (gi + 1) * n > ch * P]
                        for gi in over:
                            v0 = base[gi] + (ch - L.c0[gi]) * P
                            last = nc.tensor.matmul(ps_b[:, i % 2, ch - ch0, :], vbd[:, b, v0:v0 + P], wo[:, gi, :],
                                                    start=gi == over[0], stop=gi == over[-1])
                    last.then_inc(s_b, 1)

            @block.gpsimd
            def _(pool):
                if prepare:
                    prepare.constants(pool)
                nc.gpsimd.memset(kbd[:], 0.0).then_inc(s_zero, 1)
                nc.gpsimd.memset(g.bo[:].bitcast(FP), 0.0).then_inc(s_zero, 1)
                if not L.lora:
                    nc.gpsimd.memset(g.row[:].bitcast(FP), 0.0).then_inc(s_zero, 1)
                if before:
                    before.gather(pool)

            @block.vector
            def _(dve):
                nc.vector.memset(vbd[:], 0.0).then_inc(s_zero, 1)
                if prepare:
                    prepare.ones(dve)
                if L.lora:
                    dve.wait_ge(s_w, 16 * len(loads))
                    nc.vector.tensor_scalar(al[:], al[:], 1.0 / RANK, None, ALU.mult).then_inc(s_al, 1)
                    dve.wait_ge(s_al, 1)
                    dve.wait_ge(s_lq, 16 * len(loads_lq))
                    nc.vector.tensor_scalar(qd[:], qd[:], al[:, 0:1], None, ALU.mult)
                    nc.vector.tensor_scalar(ou[:], ou[:], al[:, 3:4], None, ALU.mult).then_inc(s_al, 1)
                dve.wait_ge(s_zero, 3 + (not L.lora))

                def block_diagonal(gi):
                    dve.wait_ge(s_kv, gi + 1)
                    for hh in range(hp):
                        rows = slice(dh * hh, dh * (hh + 1))
                        for i in range(2):
                            src = ps_kv[rows, gi % 2, i, 0:NB * KEYS].rearrange("p (b j) -> p b j", b=NB)
                            at = hh * KEYS + (off[gi] if i else 0)
                            dst = vbd[rows, :, at:at + KEYS] if i else kbd[rows, gi, :, at:at + KEYS]
                            if L.lora:
                                last = nc.vector.tensor_copy(dst, src)
                            else:
                                last = nc.vector.tensor_scalar(dst, src, (bv if i else bk)[rows, gi:gi + 1], None, ALU.add)
                    last.then_inc(s_bd, 1)

                added = [0]

                def add_tile():
                    if added[0] < NT:
                        if before:
                            before.add(dve, added[0])
                        else:
                            prepare.tile_statistics(dve, added[0])
                        added[0] += 1

                if not L.lora:
                    dve.wait_ge(s_wk, 16 * len(loads_k))
                    dve.wait_ge(s_wv, 16 * len(loads_v))
                block_diagonal(0)
                block_diagonal(1)
                dve.wait_ge(s_wq, 16 * len(loads_q))
                nc.vector.tensor_copy(g.bo[0:1], bo[:]).then_inc(s_r, 1)
                dve.wait_ge(s_r, 1)
                nc.vector.tensor_tensor(g.bo[LOW:SPLIT], bo[:], g.bo[0:1], ALU.subtract)
                for gi in range(G):
                    if L.lora:
                        for r, dst in enumerate((wq, wo)):
                            dve.wait_ge(s_u, gi * n_u + r + 1)
                            nc.vector.tensor_tensor(dst[:, gi, :], dst[:, gi, :], ps_u[:, r, 0:D], ALU.add).then_inc(s_u_sb, 1)
                    if gi + 2 < G:
                        block_diagonal(gi + 2)
                    if not L.lora:
                        for b in range(NB):
                            u = gi * n_u + b
                            dve.wait_ge(s_u, u + 1)
                            nc.vector.tensor_copy(g.row[0:1, b, gi * n:(gi + 1) * n], ps_u[0:1, u % 2, 0:n]).then_inc(s_r, 1)
                            dve.wait_ge(s_r, 2 + u)
                            nc.vector.tensor_tensor(g.row[LOW:SPLIT, b, gi * n:(gi + 1) * n], ps_u[0:1, u % 2, 0:n],
                                                    g.row[0:1, b, gi * n:(gi + 1) * n], ALU.subtract).then_inc(s_u_sb, 1)
                    for j, (b, k0) in enumerate(a_items):
                        a = gi * len(a_items) + j
                        dve.wait_ge(s_ahi, a + 1)
                        at = (slice(None), b, slice(k0, k0 + KA), slice(gi * n, (gi + 1) * n))
                        nc.vector.tensor_tensor(g.Al[L.n][at], half_a(a), g.Ah[L.n][at], ALU.subtract).then_inc(s_alo, 1)
                        for _ in range(KA):
                            if before or gi > 0:
                                add_tile()
                    if prepare and gi == G - 2:
                        prepare.statistics(dve)
                        deviation.dve(dve)
                for i, (b, ch, nch) in enumerate(b_items):
                    dve.wait_ge(s_bhi, i + 1)
                    nc.vector.tensor_tensor(g.Bl[L.n][:, b, ch:ch + nch, :], ps_b[:, i % 2, 0:nch, :],
                                            g.Bh[L.n][:, b, ch:ch + nch, :], ALU.subtract).then_inc(s_blo, 1)
                    for _ in range(nch):
                        add_tile()
                if before:
                    before.statistics(dve)
                    deviation.dve(dve)

            @block.scalar
            def _(act):
                if L.lora:
                    act.wait_ge(s_al, 1)
                    for i in range(2):
                        act.wait_ge(s_lk, i + 1)
                        nc.scalar.activation(low[:, i], ps_u[0:RANK, i, 0:NB * org].rearrange("p (b j) -> p b j", b=NB),
                                             ACT.Copy, scale=al[:, 1 + i:2 + i]).then_inc(s_lk_sb, 1)
                for gi in range(G):
                    for j, (b, k0) in enumerate(a_items):
                        a = gi * len(a_items) + j
                        act.wait_ge(s_a, a + 1)
                        nc.scalar.copy(g.Ah[L.n][:, b, k0:k0 + KA, gi * n:(gi + 1) * n], half_a(a)).then_inc(s_ahi, 1)
                    if prepare and gi == G - 2:
                        deviation.act(act)
                for i, (b, ch, nch) in enumerate(b_items):
                    act.wait_ge(s_b, i + 1)
                    nc.scalar.copy(g.Bh[L.n][:, b, ch:ch + nch, :], ps_b[:, i % 2, 0:nch, :]).then_inc(s_bhi, 1)
                if before:
                    deviation.act(act)


def attention(nc, g, L, sem):
    T = f"at{L.n}_"
    s_xn, s_xt, s_xhi, s_xlo = sem(T + "xn"), sem(T + "x_transposed"), sem(T + "x_high"), sem(T + "x_low")
    s_s, s_mx, s_sub, s_exp = sem(T + "scores"), sem(T + "max"), sem(T + "shifted"), sem(T + "exp")
    s_sum, s_inv, s_pn = sem(T + "sum"), sem(T + "inverse"), sem(T + "probs")
    s_pt, s_phi, s_plo = sem(T + "probs_transposed"), sem(T + "probs_high"), sem(T + "probs_low")
    s_o, s_res, s_bn, s_pad, s_aggr = sem(T + "out"), sem(T + "residual"), sem(T + "bn"), sem(T + "pad"), sem(T + "aggr")
    H, NS, CH = L.heads, len(L.segments), L.chunks
    with ExitStack() as ctx:
        sb = lambda name, shape, dt=FP: ctx.enter_context(nc.sbuf_tensor(T + name, shape, dt))
        pb = lambda name, shape: ctx.enter_context(nc.psum_tensor(T + name, shape, FP))
        xn = sb("xn", [P, 2, D])
        xh, xl = sb("xh", [P, 2, DK, P], FR), sb("xl", [P, 2, DK, P], FR)
        sm = sb("sm", [P, L.cols])
        pr = sb("pr", [P, 2, L.pad])
        mx, su, inv = sb("mx", [P, H, NS]), sb("su", [P, H, NS]), sb("inv", [P, H, NS])
        ph, pl = sb("ph", [P, CH, P], FR), sb("pl", [P, CH, P], FR)
        ps_x = pb("ps_x", [P, 512])
        ps_s = pb("ps_s", [P, 512 * (-(-L.cols // 512))])
        ps_p = pb("ps_p", [P, 512 * (-(-L.pad // 512))])
        ps_o = pb("ps_o", [P, 512])
        NK, HB = L.banks, H // L.banks
        banked = ps_s[:].rearrange("p (b x) -> p b x", b=NK)[:, :, 0:L.cols // NK]
        scores = banked.rearrange("p b (h j) -> p b h j", j=KEYS)
        shifted = sm[:, :].rearrange("p (b h j) -> p b h j", b=NK, j=KEYS)
        maxima = mx[:].rearrange("p (b h) s -> p b h s", b=NK)
        probs_t = ps_p[:, 0:L.pad].rearrange("p (c t) -> p c t", t=P)
        Ah, Al, Bh, Bl = g.Ah[L.n], g.Al[L.n], g.Bh[L.n], g.Bl[L.n]
        parts = (slice(0, 4), slice(4, CH))

        def steps(eng, body, cuts):
            for lo, hi in cuts:
                if hi - lo < 4:
                    for t in range(lo, hi):
                        body(t, t % 2)
                else:
                    with eng.Fori(lo, hi - 1, 2) as i:
                        body(i, lo % 2)
                        body(i + 1, (lo + 1) % 2)

        with nc.Block() as block:
            @block.tensor
            def _(pe):
                def transpose_x(t, q):
                    wait(pe, s_xn, t + 1)
                    wait(pe, s_xlo, t)
                    for k in range(DK):
                        last = nc.tensor.transpose(ps_x[:, k * P:(k + 1) * P], xn[:, q, k * P:(k + 1) * P], g.ident[:])
                    last.then_inc(s_xt, 1)

                def make(b_s, b_o):
                    def step(t, q):
                        static = isinstance(t, int)
                        if not static or t + 1 < NT:
                            wait(pe, s_xlo, t + 2)
                            wait(pe, s_sub, t + 1)
                            for i, c0 in enumerate(range(0, L.cols, L.piece)):
                                c1 = min(c0 + L.piece, L.cols)
                                o = ps_s[:, 512 * i:512 * i + c1 - c0]
                                for k in range(DK):
                                    last = product(nc, o, (xh[:, 1 - q, k, :], xl[:, 1 - q, k, :]),
                                                   (Ah[:, b_s, k, c0:c1], Al[:, b_s, k, c0:c1]), k == 0, L.lora and k == DK - 1)
                                if not L.lora:
                                    last = nc.tensor.matmul(o, g.ones_r[:], g.row[:, b_s, c0:c1], start=False, stop=True)
                            last.then_inc(s_s, 1)
                        if not static or t + 2 < NT:
                            transpose_x(t + 2, q)
                        if not static or t >= 1:
                            wait(pe, s_res, t - 1)
                            nc.tensor.matmul(ps_o[:, 0:D], g.ones_r[:], g.bo[:], start=True, stop=False)
                            for ch in range(CH):
                                for i, cs in enumerate(parts):
                                    if ch == cs.start:
                                        wait(pe, s_plo, 2 * t + i - 1)
                                last = product(nc, ps_o[:, 0:D], (ph[:, ch, :], pl[:, ch, :]),
                                               (Bh[:, b_o, ch, :], Bl[:, b_o, ch, :]), False, ch == CH - 1)
                            last.then_inc(s_o, 1)
                        if not static or 0 <= t < NT:
                            wait(pe, s_pn, t + 1)
                            wait(pe, s_plo, 2 * t)
                            for ch in range(CH):
                                last = nc.tensor.transpose(probs_t[:, ch, :], pr[:, q, ch * P:(ch + 1) * P], g.ident[:])
                            last.then_inc(s_pt, 1)
                    return step

                pe.wait_ge(s_pad, 1)
                transpose_x(0, 0)
                h = NT // NB
                steps(pe, make(0, 0), [(-1, 1), (1, 3), (3, h - 1)])
                steps(pe, make(1, 0), [(h - 1, h + 1)])
                steps(pe, make(1, 1), [(h + 1, NT - 3), (NT - 3, NT - 1), (NT - 1, NT + 1)])

            @block.vector
            def _(dve):
                def normalise(t, q):
                    if isinstance(t, int) and t < 2:
                        pass
                    else:
                        wait(dve, s_xt, t - 1)
                    nc.vector.tensor_scalar(xn[:, q:q + 1, :], one(g.X, t), one(g.mv[:, :, 0], t), one(g.rstd, t),
                                            ALU.subtract, ALU.mult).then_inc(s_xn, 1)

                def low_x(t, q):
                    wait(dve, s_xhi, t + 1)
                    nc.vector.tensor_tensor(xl[:, q], ps_x[:, 0:D].rearrange("p (k t) -> p k t", k=DK), xh[:, q],
                                            ALU.subtract).then_inc(s_xlo, 1)

                def step(t, q):
                    static = isinstance(t, int)
                    if not static or t + 1 < NT:
                        wait(dve, s_s, t + 2)
                        for i, (j0, j1) in enumerate(L.segments):
                            nc.vector.tensor_reduce(maxima[:, :, :, i:i + 1], scores[:, :, :, j0:j1], AX.X, ALU.max).then_inc(s_mx, 1)
                        wait(dve, s_mx, NS * (t + 2))
                        wait(dve, s_exp, t + 1)
                        for i, (j0, j1) in enumerate(L.segments):
                            last = nc.vector.tensor_tensor(shifted[:, :, :, j0:j1], scores[:, :, :, j0:j1],
                                                           maxima[:, :, :, i:i + 1].to_broadcast([P, NK, HB, j1 - j0]), ALU.subtract)
                        last.then_inc(s_sub, 1)
                    if not static or t + 2 < NT:
                        low_x(t + 2, q)
                    if not static or t >= 1:
                        wait(dve, s_o, t)
                        x = one(g.X, t - 1)
                        nc.vector.tensor_tensor(x, x, ps_o[:, 0:D].rearrange("p (a d) -> p a d", a=1),
                                                ALU.add).then_inc(s_res, 1)
                        wait(dve, s_res, t)
                        nc.vector.bn_stats(one(g.stats, t - 1), one(g.X, t - 1)).then_inc(s_bn, 1)
                    if not static or t + 1 < NT:
                        wait(dve, s_exp, t + 2)
                        wait(dve, s_pn, t + 1)
                        e = pr[:, 1 - q, 0:L.cols].rearrange("p (h j) -> p h j", h=H)
                        for i, (j0, j1) in enumerate(L.segments):
                            nc.vector.tensor_reduce(su[:, :, i:i + 1], e[:, :, j0:j1], AX.X, ALU.add).then_inc(s_sum, 1)
                        wait(dve, s_sum, NS * (t + 2))
                        nc.vector.reciprocal(inv[:], su[:]).then_inc(s_inv, 1)
                    if not static or t + 3 < NT:
                        normalise(t + 3, 1 - q)
                    if not static or 0 <= t < NT:
                        for i, cs in enumerate(parts):
                            wait(dve, s_phi, 2 * t + i + 1)
                            nc.vector.tensor_tensor(pl[:, cs], probs_t[:, cs], ph[:, cs], ALU.subtract).then_inc(s_plo, 1)

                nc.vector.memset(pr[:, :, L.cols:], 0.0).then_inc(s_pad, 1)
                normalise(0, 0)
                normalise(1, 1)
                low_x(0, 0)
                steps(dve, step, [(-1, 1), (1, 3), (3, NT - 3), (NT - 3, NT - 1), (NT - 1, NT + 1)])
                dve.wait_ge(s_bn, NT)
                for t in range(NT):
                    nc.vector.bn_aggr(g.mv[:, t, :], g.stats[:, t, :]).then_inc(s_aggr, 1)

            @block.scalar
            def _(act):
                def high_x(t, q):
                    wait(act, s_xt, t + 1)
                    wait(act, s_s, t - 1)
                    nc.scalar.copy(xh[:, q], ps_x[:, 0:D].rearrange("p (k t) -> p k t", k=DK)).then_inc(s_xhi, 1)

                def step(t, q):
                    static = isinstance(t, int)
                    if not static or t + 2 < NT:
                        high_x(t + 2, q)
                    if not static or t + 1 < NT:
                        wait(act, s_sub, t + 2)
                        wait(act, s_pt, t)
                        nc.scalar.activation(pr[:, 1 - q, 0:L.cols], sm[:, :], ACT.Exp, scale=L.scale).then_inc(s_exp, 1)
                    if not static or 0 <= t < NT:
                        wait(act, s_pt, t + 1)
                        wait(act, s_o, t)
                        for cs in parts:
                            nc.scalar.copy(ph[:, cs], probs_t[:, cs]).then_inc(s_phi, 1)

                nc.scalar.preload_act_table(ACT.Exp)
                high_x(0, 0)
                steps(act, step, [(-1, 1), (1, 3), (3, NT - 3), (NT - 3, NT - 1), (NT - 1, NT + 1)])

            @block.gpsimd
            def _(pool):
                def step(t, q):
                    wait(pool, s_inv, t + 1)
                    e = pr[:, q, 0:L.cols].rearrange("p (h j) -> p h j", h=H)
                    for i, (j0, j1) in enumerate(L.segments):
                        last = nc.gpsimd.tensor_tensor(e[:, :, j0:j1], e[:, :, j0:j1],
                                                       inv[:, :, i:i + 1].to_broadcast([P, H, j1 - j0]), ALU.mult)
                    last.then_inc(s_pn, 1)

                with pool.Fori(0, NT - 1, 2) as i:
                    step(i, 0)
                    step(i + 1, 1)


def allocate(nc, ctx, sem):
    sb = lambda name, shape, dt=FP: ctx.enter_context(nc.sbuf_tensor(name, shape, dt))
    g = Shared()
    g.X = sb("X", [P, NT, D])
    g.stats, g.mv = sb("stats", [P, NT, 6]), sb("mean_var", [P, NT, 2])
    g.ve, g.sq, g.rstd = sb("var_eps", [P, NT]), sb("deviation", [P, NT]), sb("rstd", [P, NT])
    g.ident, g.before, g.ones = sb("ident", [P, P]), sb("before", [P, P]), sb("ones", [P, P])
    g.ones_r = sb("ones_r", [SPLIT, P], FR)
    g.iota_e, g.iota_thr = sb("iota_e", [P, NT, E]), sb("iota_thr", [P, E, TOK // ST])
    g.s_zeroed = sem("slots_zeroed")
    g.zero = sb("zero", [P, 2 * D])
    g.iota_tile = sb("iota_tile", [P, ROUTED, E])
    g.xs = nc.dram_tensor("slots_in", [ROUTED * ST, D], FP, kind="Internal").ap()
    g.ys = nc.dram_tensor("slots_out", [ROUTED * ST, D], FP, kind="Internal").ap()
    g.Ah, g.Al, g.Bh, g.Bl = {}, {}, {}, {}
    return g


def attention_operands(nc, ctx, g, L):
    sb = lambda name, shape: ctx.enter_context(nc.sbuf_tensor(f"{name}{L.n}", shape, FR))
    g.Ah[L.n], g.Al[L.n] = sb("A_high", [P, NB, DK, L.cols]), sb("A_low", [P, NB, DK, L.cols])
    g.Bh[L.n], g.Bl[L.n] = sb("B_high", [P, NB, L.chunks, D]), sb("B_low", [P, NB, L.chunks, D])
    g.bo = sb("bo", [SPLIT, D])
    if not L.lora:
        g.row = sb("row", [SPLIT, NB, L.cols])


def route(nc, g, m, L, w, sem):
    T = f"r{L.n}_"
    s_w, s_xn, s_t, s_xt = sem(T + "weights"), sem(T + "xn"), sem(T + "transposed"), [sem(f"{T}x_copied{k}") for k in range(DK)]
    s_r1, s_relu, s_lg = sem(T + "hidden"), sem(T + "relu"), sem(T + "logits")
    s_ch, s_ex, s_cnt, s_ct = sem(T + "chain"), sem(T + "exp"), sem(T + "counts"), sem(T + "counted")
    s_k = sem(T + "slots")
    deviation = InverseDeviation(nc, g, sem, T + "ln")
    CT, RH = 4, D // 4
    with ExitStack() as ctx:
        sb = lambda name, shape, dt=FP: ctx.enter_context(nc.sbuf_tensor(T + name, shape, dt))
        pb = lambda name, shape: ctx.enter_context(nc.psum_tensor(T + name, shape, FP))
        xt = sb("xt", [P, 2, DK, CT * P])
        if L.n == 0:
            r1, rb1, r2, rb2 = sb("r1", [P, DK, RH]), sb("rb1", [RH, 1]), sb("r2", [RH, E]), sb("rb2", [1, E])
            hid = sb("hid", [RH, 2, CT * P])
            loads = [(r1, w["r1"]), (rb1, w["rb1"]), (r2, w["r2"]), (rb2, w["rb2"])]
        else:
            r1 = sb("r", [P, DK, E])
            loads = [(r1, w["r"])]
        t8 = lambda name: sb(name, [P, NT, E])
        t1 = lambda name: sb(name, [P, NT, 1])
        sh, ex, pro, pro2, eq = t8("sh"), t8("ex"), t8("pro"), t8("pro2"), t8("eq")
        is1, is2, both, offs, slot, tmp = t8("is1"), t8("is2"), t8("both"), t8("offs"), t8("slot"), t8("tmp")
        far = t8("far")
        mx, sm, inv, p1, p2, i1, i2 = (t1(n) for n in ("mx", "sm", "inv", "p1", "p2", "i1", "i2"))
        ed, sf = t1("ed"), t1("sf")
        n_e, nt_e, ends, start = sb("n_e", [P, E, 1]), sb("nt_e", [P, E, 1]), sb("ends", [P, E, 1]), sb("start", [P, 1, E])
        over = sb("over", [P, E, TOK // ST])
        past, tile_e = sb("past", [1, ROUTED, E]), sb("tile_e", [1, ROUTED, 1])
        ps_x = pb("ps_x", [P, 2, DK, CT * P])
        ps_r = pb("ps_r", [RH, 2, CT * P])
        ps_l = pb("ps_l", [P, NT, E])
        ps_c = pb("ps_c", [P, 2, NT, E])
        chunks = NT // CT

        with nc.Block() as block:
            @block.sync
            def _(sp):
                for dst, src in loads:
                    sp.dma_start(dst[:], src).then_inc(s_w, 16)

            @block.tensor
            def _(pe):
                def transpose(c):
                    pe.wait_ge(s_xn, CT * (c + 1))
                    for k in range(DK):
                        wait(pe, s_xt[k], c - 1)
                    for k in range(DK):
                        for a in range(CT):
                            last = nc.tensor.transpose(ps_x[:, c % 2, k, a * P:(a + 1) * P],
                                                       m.xn[:, c * CT + a, k * P:(k + 1) * P], g.ident[:])
                    last.then_inc(s_t, 1)

                transpose(0)
                pe.wait_ge(s_w, 16 * len(loads))
                for c in range(chunks):
                    if c + 1 < chunks:
                        transpose(c + 1)
                    for k in range(DK):
                        pe.wait_ge(s_xt[k], c + 1)
                    if L.n == 0:
                        for k in range(DK):
                            last = nc.tensor.matmul(ps_r[:, c % 2, :], r1[:, k, :], xt[:, c % 2, k, :], start=k == 0, stop=k == DK - 1)
                        last.then_inc(s_r1, 1)
                        pe.wait_ge(s_relu, c + 1)
                        for a in range(CT):
                            nc.tensor.matmul(ps_l[:, c * CT + a, :], hid[:, c % 2, a * P:(a + 1) * P], r2[:], start=True, stop=False)
                            last = nc.tensor.matmul(ps_l[:, c * CT + a, :], g.ones[0:1, :], rb2[:], start=False, stop=True)
                    else:
                        for a in range(CT):
                            for k in range(DK):
                                last = nc.tensor.matmul(ps_l[:, c * CT + a, :], xt[:, c % 2, k, a * P:(a + 1) * P], r1[:, k, :],
                                                        start=k == 0, stop=k == DK - 1)
                    last.then_inc(s_lg, 1)
                pe.wait_ge(s_cnt, 1)
                nc.tensor.matmul(ps_c[:, 0], g.before[:], both[:], start=True, stop=True)
                nc.tensor.matmul(ps_c[:, 1], g.ones[:], both[:], start=True, stop=True).then_inc(s_ct, 1)

            @block.scalar
            def _(act):
                deviation.act(act)
                nc.scalar.preload_act_table(ACT.Exp)
                for c in range(chunks):
                    act.wait_ge(s_t, c + 1)
                    wait(act, s_lg, c - 1)
                    nc.scalar.copy(xt[:, c % 2, 0, :], ps_x[:, c % 2, 0, :]).then_inc(s_xt[0], 1)
                    if L.n == 0:
                        act.wait_ge(s_r1, c + 1)
                        nc.scalar.activation(hid[:, c % 2, :], ps_r[:, c % 2, :], ACT.Relu, bias=rb1[:, 0:1]).then_inc(s_relu, 1)
                act.wait_ge(s_ch, 2)
                nc.scalar.activation(ex[:], sh[:], ACT.Exp).then_inc(s_ex, 1)
                if L.n == 0:
                    act.wait_ge(s_k, 1)
                    nc.scalar.activation(ed[:], sf[:], ACT.Exp, scale=1.0 / TOPK).then_inc(s_ex, 1)

            @block.vector
            def _(dve):
                done = [0]

                def link(ins):
                    done[0] += 1
                    ins.then_inc(s_ch, 1)
                    dve.wait_ge(s_ch, done[0])

                v = nc.vector
                deviation.dve(dve)
                for t in range(NT):
                    v.tensor_scalar(m.xn[:, t, :], g.X[:, t, :], g.mv[:, t, 0:1], g.rstd[:, t:t + 1],
                                    ALU.subtract, ALU.mult).then_inc(s_xn, 1)
                for c in range(chunks):
                    dve.wait_ge(s_t, c + 1)
                    wait(dve, s_lg, c - 1)
                    v.tensor_copy(xt[:, c % 2, 1, :], ps_x[:, c % 2, 1, :]).then_inc(s_xt[1], 1)
                dve.wait_ge(s_lg, chunks)
                e8 = lambda a: a[:].to_broadcast([P, NT, E])
                link(v.tensor_reduce(mx[:], ps_l[:], AX.X, ALU.max))
                link(v.tensor_tensor(sh[:], ps_l[:], e8(mx), ALU.subtract))
                dve.wait_ge(s_ex, 1)
                link(v.tensor_reduce(sm[:], ex[:], AX.X, ALU.add))
                link(v.reciprocal(inv[:], sm[:]))
                link(v.tensor_tensor(pro[:], ex[:], e8(inv), ALU.mult))
                link(v.tensor_scalar(far[:], g.iota_e[:], float(E), None, ALU.add))

                def choose(p, best, idx, is_it):
                    link(v.tensor_reduce(best[:], p[:], AX.X, ALU.max))
                    link(v.tensor_tensor(eq[:], p[:], e8(best), ALU.is_equal))
                    link(v.scalar_tensor_tensor(out=tmp[:], in0=eq[:], scalar=-float(E), in1=far[:], op0=ALU.mult, op1=ALU.add))
                    link(v.tensor_reduce(idx[:], tmp[:], AX.X, ALU.min))
                    link(v.tensor_tensor(is_it[:], g.iota_e[:], e8(idx), ALU.is_equal))

                choose(pro, p1, i1, is1)
                link(v.scalar_tensor_tensor(out=pro2[:], in0=is1[:], scalar=-4.0, in1=pro[:], op0=ALU.mult, op1=ALU.add))
                choose(pro2, p2, i2, is2)
                link(v.tensor_tensor(both[:], is1[:], is2[:], ALU.add))
                v.tensor_copy(offs[:, 0, :], both[:, 0, :]).then_inc(s_cnt, 1)
                if L.n == 0:
                    v.tensor_tensor(sf[:], p2[:], p1[:], ALU.subtract).then_inc(s_k, 1)
                    dve.wait_ge(s_ex, 2)
                    link(v.tensor_scalar(sf[:], ed[:], 1.0, None, ALU.add))
                    link(v.reciprocal(m.wt[:, 0, :], sf[:, :, 0]))
                    link(v.tensor_tensor(m.wt[:, 1, :], m.wt[:, 0, :], ed[:, :, 0], ALU.mult))
                else:
                    link(v.tensor_copy(m.wt[:, 0, :], p1[:, :, 0]))
                    link(v.tensor_copy(m.wt[:, 1, :], p2[:, :, 0]))
                dve.wait_ge(s_ct, 1)
                link(v.memset(offs[:, 0, :], 0.0))
                for t in range(1, NT):
                    link(v.tensor_tensor(offs[:, t, :], offs[:, t - 1, :], ps_c[:, 1, t - 1, :], ALU.add))
                link(v.tensor_tensor(n_e[:, :, 0], offs[:, NT - 1, :], ps_c[:, 1, NT - 1, :], ALU.add))
                link(v.tensor_tensor(over[:], n_e[:].to_broadcast([P, E, TOK // ST]), g.iota_thr[:], ALU.is_gt))
                link(v.tensor_reduce(nt_e[:], over[:], AX.X, ALU.add))
                link(v.tensor_copy(ends[:, 0, :], nt_e[:, 0, :]))
                for e in range(1, E):
                    link(v.tensor_tensor(ends[:, e, :], ends[:, e - 1, :], nt_e[:, e, :], ALU.add))
                link(v.tensor_tensor(start[:, 0, :], ends[:, :, 0], nt_e[:, :, 0], ALU.subtract))
                link(v.tensor_scalar(start[:], start[:], float(ST), None, ALU.mult))
                link(v.tensor_tensor(slot[:], ps_c[:, 0], offs[:], ALU.add))
                link(v.tensor_tensor(slot[:], slot[:], start[:].to_broadcast([P, NT, E]), ALU.add))
                for i, is_it in enumerate((is1, is2)):
                    link(v.tensor_tensor(tmp[:], slot[:], is_it[:], ALU.mult))
                    link(v.tensor_reduce(mx[:], tmp[:], AX.X, ALU.add))
                    v.tensor_copy(m.slots[:, i, :], mx[:, :, 0]).then_inc(s_k, 1)
                link(v.tensor_tensor(past[:], ends[0:1, :, :].rearrange("p e a -> p a e").to_broadcast([1, ROUTED, E]),
                                     g.iota_tile[0:1], ALU.is_le))
                link(v.tensor_reduce(tile_e[:], past[:], AX.X, ALU.add))
                link(v.tensor_scalar(tile_e[:], tile_e[:], float(E - 1), None, ALU.min))
                if L.sh_tiles:
                    link(v.memset(m.eid[:, 0:L.sh_tiles], E))
                link(v.tensor_copy(m.eid[:, L.sh_tiles:L.tiles], tile_e[:, :, 0]))

            @block.gpsimd
            def _(pool):
                pool.wait_ge(s_k, 2 + (L.n == 0))


def scatter(nc, g, m, pool):
    pool.wait_ge(g.s_zeroed, 16 * ROUTED * ST // P // 2)
    for t in range(NT):
        for i in range(TOPK):
            nc.gpsimd.indirect_dma_start(
                out=g.xs, out_offset=bass.IndirectOffsetOnAxis(ap=m.slots[:, i, t:t + 1], axis=0),
                in_=m.xn[:, t, :], in_offset=None).then_inc(m.s_sc, 16)


def experts(nc, g, m, L, w, sem, idle):
    T = f"e{L.n}_"
    s_w1d, s_w2d, s_xl = ([sem(f"{T}{n}_loaded{q}") for q in range(2)] for n in ("w1", "w2", "x"))
    s_b1, s_b2 = sem(T + "b1_loaded"), sem(T + "b2_loaded")
    s_st = [sem(f"{T}stored{q}") for q in range(2)]
    s_w1h, s_w1l, s_w2h, s_w2l = sem(T + "w1_high"), sem(T + "w1_low"), sem(T + "w2_high"), sem(T + "w2_low")
    s_tr, s_xh, s_xlo = sem(T + "x_transposed"), sem(T + "x_high"), sem(T + "x_low")
    s_m1, s_h, s_hh, s_hl = sem(T + "first"), sem(T + "hidden"), sem(T + "hidden_high"), sem(T + "hidden_low")
    s_m2, s_ev, s_sx = sem(T + "second"), sem(T + "evacuated"), sem(T + "shared_added")
    M1, J = L.m1, L.tiles
    MG = 2 if M1 > 2 else 1
    MP = M1 // MG
    W1 = DK * L.hid
    NE = w["w1"].shape[0]
    slots_h = min(4, 2 * MP)
    with ExitStack() as ctx:
        sb = lambda name, shape, dt=FP: ctx.enter_context(nc.sbuf_tensor(T + name, shape, dt))
        pb = lambda name, shape: ctx.enter_context(nc.psum_tensor(T + name, shape, FP))
        w1s, w2s = sb("w1s", [P, 2, W1]), sb("w2s", [P, 2, W1])
        w1h, w1l = sb("w1h", [P, 2, W1], FR), sb("w1l", [P, 2, W1], FR)
        w2h, w2l = sb("w2h", [P, 2, W1], FR), sb("w2l", [P, 2, W1], FR)
        xin = sb("xin", [P, 2, ST // P, D])
        xh, xl = sb("xh", [P, 2, DK, ST], FR), sb("xl", [P, 2, DK, ST], FR)
        hf = sb("hf", [P, M1, ST])
        hh, hl = sb("hh", [P, 2, M1, ST], FR), sb("hl", [P, 2, M1, ST], FR)
        b1s, b2s = sb("b1s", [P, NE, M1]), sb("b2s", [P, NE, D])
        yo = sb("yo", [P, 2, ST // P, D])
        ps_x = pb("ps_x", [P, 2, DK, ST])
        ps_h = pb("ps_h", [P, 4, 2, ST])
        ps_o = pb("ps_o", [P, 2, ST // P, D])
        arrived = lambda j, q: 8 * j + (8 if q else 16)
        first = lambda a, q, k, i: a[:, q, k * L.hid + i * P:k * L.hid + (i + 1) * P]
        second = lambda a, q, i: a[:, q, i * D:(i + 1) * D]

        S = L.sh_tiles
        ROWS = ST // P

        def steps(eng, body, lo, hi, cuts=(3, J - 2)):
            for j in range(lo, cuts[0]):
                body(j, j % 2)
            for c0, c1 in zip(cuts, cuts[1:]):
                if c1 - c0 < 4:
                    for j in range(c0, c1):
                        body(j, j % 2)
                else:
                    with eng.Fori(c0, c1 - 1, 2) as i:
                        body(i, c0 % 2)
                        body(i + 1, 1 - c0 % 2)
            for j in range(cuts[-1], hi):
                body(j, j % 2)

        def expert(eng, j):
            return eng.value_load(one(m.eid[0:1, :], j), min_val=0, max_val=NE - 1)

        def low_w1(eng, unit, j, q):
            wait(eng, s_w1h, j + 1)
            unit.tensor_tensor(w1l[:, q, :], w1s[:, q, :], w1h[:, q, :], ALU.subtract).then_inc(s_w1l, 1)

        def low_w2(eng, unit, j, q):
            wait(eng, s_w2h, j + 1)
            unit.tensor_tensor(w2l[:, q, :], w2s[:, q, :], w2h[:, q, :], ALU.subtract).then_inc(s_w2l, 1)

        with nc.Block() as block:
            @block.gpsimd
            def _(pool):
                scatter(nc, g, m, pool)
                for h in idle:
                    pool.sem_clear(h)
                if not L.shared:
                    def step(j, q):
                        static = isinstance(j, int)
                        if not static or j + 1 < J:
                            wait(pool, s_m1, MP * j)
                            low_w1(pool, nc.gpsimd, j + 1, 1 - q)
                            wait(pool, s_m2, j)
                            low_w2(pool, nc.gpsimd, j + 1, 1 - q)
                    steps(pool, step, -1, J)

            @block.sync
            def _(sp):
                def of(a, e):
                    return w[a][bass.ds(e, 1)].rearrange("a p n -> p (a n)")

                def make(shared):
                    def step(j, q):
                        static = isinstance(j, int)
                        if not static or j < J:
                            e = expert(sp, j)
                            wait(sp, s_w1l, j - 1)
                            sp.dma_start(w1s[:, q, :], of("w1", e)).then_inc(s_w1d[q], 16)
                            wait(sp, s_tr, j - 1)
                            if shared:
                                t = j * ROWS
                                rows = m.xn[:, t:t + ROWS, :] if static else m.xn[:, bass.ds(t, ROWS), :]
                            else:
                                if static and j == S:
                                    sp.wait_ge(m.s_sc, 16 * NT * TOPK)
                                rows = g.xs.rearrange("(j a p) d -> j p a d", p=P, a=ROWS)
                                rows = rows[j - S] if static else rows[bass.ds(j - S, 1)].rearrange("j p a d -> p (j a) d")
                            sp.dma_start(xin[:, q], rows).then_inc(s_xl[q], 16)
                        if not static or 1 <= j <= J:
                            e = expert(sp, j - 1)
                            wait(sp, s_w2l, j - 2)
                            sp.dma_start(w2s[:, 1 - q, :], of("w2", e)).then_inc(s_w2d[1 - q], 16)
                    return step

                make(S > 0)(0, 0)
                sp.dma_start(b1s[:], w["b1"].rearrange("e p m -> p e m")).then_inc(s_b1, 16)
                sp.dma_start(b2s[:], w["b2"].rearrange("(a e) d -> a e d", a=1).to_broadcast([P, NE, D])).then_inc(s_b2, 16)
                if L.shared:
                    steps(sp, make(True), 1, S, (3, S - 1))
                    steps(sp, make(False), S, J + 1, (S + 1, J - 2))
                else:
                    steps(sp, make(False), 1, J + 1)

            @block.tensor
            def _(pe):
                def step(j, q):
                    static = isinstance(j, int)
                    if not static or j + 1 < J:
                        wait(pe, s_xl[1 - q], arrived(j + 1, 1 - q))
                        wait(pe, s_xlo, j)
                        for k in range(DK):
                            for a in range(ST // P):
                                last = nc.tensor.transpose(ps_x[:, 1 - q, k, a * P:(a + 1) * P],
                                                           xin[:, 1 - q, a, k * P:(k + 1) * P], g.ident[:])
                        last.then_inc(s_tr, 1)
                    if not static or 0 <= j < J:
                        wait(pe, s_w1l, j + 1)
                        wait(pe, s_xlo, j + 1)
                        for mp in range(MP):
                            wait(pe, s_h, j * MP + mp + 1 - slots_h)
                            for i in range(MG):
                                o = ps_h[:, (q * MP + mp) % 4, i, :]
                                for k in range(DK):
                                    last = product(nc, o, (first(w1h, q, k, MG * mp + i), first(w1l, q, k, MG * mp + i)),
                                                   (xh[:, q, k, :], xl[:, q, k, :]), k == 0, k == DK - 1)
                            last.then_inc(s_m1, 1)
                    if not static or j >= 1:
                        wait(pe, s_hl, MP * j)
                        wait(pe, s_w2l, j)
                        wait(pe, s_ev, j - 2)
                        for a in range(ST // P):
                            o = ps_o[:, 1 - q, a, :]
                            for i in range(M1):
                                ts = slice(a * P, (a + 1) * P)
                                last = product(nc, o, (hh[:, 1 - q, i, ts], hl[:, 1 - q, i, ts]),
                                               (second(w2h, 1 - q, i), second(w2l, 1 - q, i)), i == 0, i == M1 - 1)
                        last.then_inc(s_m2, 1)
                steps(pe, step, -1, J + 1)

            @block.scalar
            def _(act):
                def make(shared):
                    def step(j, q):
                        static = isinstance(j, int)
                        if not static or j + 1 < J:
                            wait(act, s_w1d[1 - q], arrived(j + 1, 1 - q))
                            wait(act, s_m1, MP * j)
                            nc.scalar.copy(w1h[:, 1 - q, :], w1s[:, 1 - q, :]).then_inc(s_w1h, 1)
                            wait(act, s_tr, j + 2)
                            nc.scalar.copy(xh[:, 1 - q], ps_x[:, 1 - q]).then_inc(s_xh, 1)
                        if not static or 0 <= j < J:
                            e = expert(act, j)
                            for mp in range(MP):
                                wait(act, s_m1, j * MP + mp + 1)
                                wait(act, s_hl, (j - 1) * MP + mp + 1)
                                for i in range(MG):
                                    c = MG * mp + i
                                    last = nc.scalar.activation(hf[:, c, :], ps_h[:, (q * MP + mp) % 4, i, :], L.func,
                                                                bias=b1s[:, bass.ds(e, 1), c:c + 1])
                                last.then_inc(s_h, 1)
                                wait(act, s_h, j * MP + mp + 1)
                                wait(act, s_m2, j - 1)
                                nc.scalar.copy(hh[:, q, MG * mp:MG * (mp + 1), :], hf[:, MG * mp:MG * (mp + 1), :]).then_inc(s_hh, 1)
                        if not shared and (not static or j - 2 >= S):
                            wait(act, s_ev, j - 1)
                            rows = g.ys.rearrange("(j a p) d -> j p a d", p=P, a=ROWS)
                            n = j - 2 - S
                            rows = rows[n] if static else rows[bass.ds(n, 1)].rearrange("j p a d -> p (j a) d")
                            act.dma_start(rows, yo[:, q]).then_inc(s_st[q], 16)
                    return step

                nc.scalar.preload_act_table(L.func)
                act.wait_ge(s_b1, 16)
                if L.shared:
                    steps(act, make(True), -1, S + 1, (3, S + 1))
                    steps(act, make(False), S + 1, J + 2, (S + 3, J - 2))
                else:
                    steps(act, make(False), -1, J + 2)
                for n in (ROUTED - 2, ROUTED - 1):
                    act.wait_ge(s_st[n % 2], arrived(n, n % 2))

            @block.vector
            def _(dve):
                def make(shared):
                    def step(j, q):
                        static = isinstance(j, int)
                        if not static or j + 1 < J:
                            if L.shared:
                                low_w1(dve, nc.vector, j + 1, 1 - q)
                            wait(dve, s_xh, j + 2)
                            nc.vector.tensor_tensor(xl[:, 1 - q], ps_x[:, 1 - q], xh[:, 1 - q], ALU.subtract).then_inc(s_xlo, 1)
                        if not static or 0 <= j < J:
                            for mp in range(MP):
                                wait(dve, s_hh, j * MP + mp + 1)
                                nc.vector.tensor_tensor(hl[:, q, MG * mp:MG * (mp + 1), :], hf[:, MG * mp:MG * (mp + 1), :],
                                                        hh[:, q, MG * mp:MG * (mp + 1), :], ALU.subtract).then_inc(s_hl, 1)
                        if not static or 1 <= j <= J:
                            wait(dve, s_m2, j)
                            e = expert(dve, j - 1)
                            n = j - 3 - S
                            if not static or n >= 0:
                                if not shared:
                                    wait(dve, s_st[1 - q], arrived(n, 1 - q))
                            nc.vector.tensor_tensor(yo[:, 1 - q], ps_o[:, 1 - q], b2s[:, bass.ds(e, 1), :].to_broadcast([P, ST // P, D]),
                                                    ALU.add).then_inc(s_ev, 1)
                            if shared:
                                wait(dve, s_ev, j)
                                t = (j - 1) * ROWS
                                x = g.X[:, t:t + ROWS, :] if static else g.X[:, bass.ds(t, ROWS), :]
                                nc.vector.tensor_tensor(x, x, yo[:, 1 - q], ALU.add).then_inc(s_sx, 1)
                        if not static or j + 1 < J:
                            wait(dve, s_m2, j)
                            wait(dve, s_w2d[1 - q], arrived(j + 1, 1 - q))
                            nc.vector.tensor_copy(w2h[:, 1 - q, :], w2s[:, 1 - q, :]).then_inc(s_w2h, 1)
                            if L.shared:
                                low_w2(dve, nc.vector, j + 1, 1 - q)
                    return step

                dve.wait_ge(s_b2, 16)
                if L.shared:
                    steps(dve, make(True), -1, S + 1, (3, S + 1))
                    steps(dve, make(False), S + 1, J + 1, (S + 3, J - 2))
                else:
                    steps(dve, make(False), -1, J + 1)


class Combine:

    NBUF = 4

    def __init__(self, nc, ctx, g, m, L, sem, out):
        self.nc, self.g, self.m, self.L, self.out = nc, g, m, L, out
        T = f"c{L.n}_"
        self.s_g = [sem(f"{T}gathered{q}") for q in range(self.NBUF)]
        self.s_f, self.s_x, self.s_bn, self.s_out = sem(T + "used"), sem(T + "x"), sem(T + "bn"), sem(T + "stored")
        self.y = ctx.enter_context(nc.sbuf_tensor(T + "y", [P, self.NBUF, TOPK, D], FP))

    def gather(self, pool):
        for t in range(NT):
            wait(pool, self.s_f, t + 1 - self.NBUF)
            for i in range(TOPK):
                self.nc.gpsimd.indirect_dma_start(
                    out=self.y[:, t % self.NBUF, i, :], out_offset=None, in_=self.g.ys,
                    in_offset=bass.IndirectOffsetOnAxis(ap=self.m.slots[:, i, t:t + 1], axis=0)).then_inc(self.s_g[t % self.NBUF], 16)

    def sync(self, sp):
        if self.out is not None:
            for t in range(NT):
                sp.wait_ge(self.s_f, t + 1)
                sp.dma_start(self.out[t * P:(t + 1) * P, :], self.g.X[:, t, :]).then_inc(self.s_out, 16)
            sp.wait_ge(self.s_out, 16 * NT)

    def add(self, dve, t):
        v, q = self.nc.vector, t % self.NBUF
        dve.wait_ge(self.s_g[q], 16 * TOPK * (t // self.NBUF + 1))
        x = self.g.X[:, t, :]
        for i in range(TOPK):
            done, n = (self.s_f, t + 1) if i == TOPK - 1 else (self.s_x, t + 1)
            v.scalar_tensor_tensor(out=x, in0=self.y[:, q, i, :], scalar=self.m.wt[:, i, t:t + 1],
                                   in1=x, op0=ALU.mult, op1=ALU.add).then_inc(done, 1)
            dve.wait_ge(done, n)
        if self.out is None:
            v.bn_stats(self.g.stats[:, t, :], x).then_inc(self.s_bn, 1)

    def statistics(self, dve):
        dve.wait_ge(self.s_bn, NT)
        for t in range(NT):
            last = self.nc.vector.bn_aggr(self.g.mv[:, t, :], self.g.stats[:, t, :])
        last.then_inc(self.s_bn, 1)
        dve.wait_ge(self.s_bn, NT + 1)


def mixture(nc, g, m, L, w, sem, handles):
    with ExitStack() as ctx:
        m.xn = ctx.enter_context(nc.sbuf_tensor(f"m{L.n}_xn", [P, NT, D], FP))
        route(nc, g, m, L, w, sem)
        idle = [h for h in handles if h is not g.s_zeroed] if L.n == 0 else []
        m.s_sc = sem(f"m{L.n}_scattered")
        experts(nc, g, m, L, w, sem, idle)
        for h in idle:
            nc.release_semaphore(h)


def build(nc, t, out):
    with ExitStack() as ctx:
        handles = []

        def sem(name):
            handles.append(nc.alloc_semaphore(name=name))
            return handles[-1]

        g = allocate(nc, ctx, sem)
        ms = []
        for L in LAYERS:
            sb = lambda name, shape, dt=FP: ctx.enter_context(nc.sbuf_tensor(f"m{L.n}_{name}", shape, dt))
            m = Shared()
            m.wt, m.slots = sb("weights", [P, TOPK, NT]), sb("slots", [P, TOPK, NT], I32)
            m.eid = sb("tile_expert", [1, L.tiles + 1], I32)
            ms.append(m)
        part = lambda p: {k[len(p):]: a for k, a in t.items() if k.startswith(p)}
        for L, m in zip(LAYERS, ms):
            with ExitStack() as attn:
                attention_operands(nc, attn, g, L)
                with ExitStack() as extra:
                    prepare = Prepare(nc, g, t["x"], sem) if L.n == 0 else None
                    before = Combine(nc, extra, g, ms[L.n - 1], LAYERS[L.n - 1], sem, None) if L.n else None
                    attention_setup(nc, g, L, {**part(f"a{L.n}_"), "ctx": t["ctx"]}, sem, prepare, before)
                attention(nc, g, L, sem)
            mixture(nc, g, m, L, part(f"m{L.n}_"), sem, handles)
        with ExitStack() as last:
            final = Combine(nc, last, g, ms[-1], LAYERS[-1], sem, out)
            with nc.Block() as block:
                @block.gpsimd
                def _(pool):
                    final.gather(pool)

                @block.sync
                def _(sp):
                    final.sync(sp)

                @block.vector
                def _(dve):
                    for t in range(NT):
                        final.add(dve, t)


def host_layouts(inputs):
    import numpy as np
    c = np.ascontiguousarray
    f = {k: np.asarray(v) for k, v in inputs.items()}
    out = {"x": c(f["x"].reshape(TOK, D))}
    out["ctx"] = c(f["ctx_768"].transpose(2, 0, 1).reshape(CK, CP, NB, KEYS).transpose(1, 0, 2, 3))
    rows = lambda a, p: c(a.reshape(a.shape[0] // p, p, a.shape[1]).transpose(1, 0, 2))
    a0 = lambda k: f["L0_xattn_" + k]
    a1 = lambda k: f["L1_xattn_" + k]
    out.update({
        "a0_wk": rows(a0("Wk"), CP), "a0_wv": rows(a0("Wv"), CP),
        "a0_wki": rows(a0("Wk_ipa"), CP), "a0_wvi": rows(a0("Wv_ipa"), CP),
        "a0_wq": rows(a0("Wq").T, P), "a0_wo": rows(a0("Wo"), P), "a0_bo": c(a0("bo")[None, :]),
        "a0_kd": rows(a0("k_down"), CP), "a0_vd": rows(a0("v_down"), CP),
        "a0_ku": c(a0("k_up")), "a0_vu": c(a0("v_up")),
        "a0_qu": c(a0("q_up")), "a0_qd": c(a0("q_down").T),
        "a0_od": c(a0("o_down").T), "a0_ou": c(a0("o_up")),
        "a0_alphas": c(np.concatenate([a0(k + "_alpha") for k in "qkvo"])[None, :]),
        "a1_wk": rows(a1("Wk").T, CP), "a1_wv": rows(a1("Wv").T, CP),
        "a1_wq": rows(a1("Wq"), P), "a1_wo": rows(a1("Wo").T, P), "a1_bo": c(a1("bo")[None, :]),
        "a1_bq": c(a1("bq").reshape(-1, P).T), "a1_bk": c(a1("bk").reshape(-1, P).T), "a1_bv": c(a1("bv").reshape(-1, P).T),
    })

    def experts(p, w1, b1, w2, b2):
        n, _, hid = w1.shape
        out[p + "w1"] = c(w1.reshape(n, DK, P, hid).transpose(0, 2, 1, 3).reshape(n, P, -1))
        out[p + "b1"] = c(b1.reshape(n, hid // P, P).transpose(0, 2, 1))
        out[p + "w2"] = c(w2.reshape(n, hid // P, P, D).transpose(0, 2, 1, 3).reshape(n, P, -1))
        out[p + "b2"] = c(b2)

    m0 = lambda k: f["L0_ffn_" + k]
    m1 = lambda k: f["L1_ffn_" + k]
    with_shared = lambda e, s: np.concatenate([e, s[None]], axis=0)
    experts("m0_", *(with_shared(m0(e), m0(one)) for e, one in (("We1", "Ws1"), ("be1", "bs1"), ("We2", "Ws2"), ("be2", "bs2"))))
    experts("m1_", m1("w_in"), m1("b_in"), m1("w_out"), m1("b_out"))
    out.update({
        "m0_r1": rows(m0("Wr1"), P), "m0_rb1": c(m0("br1")[:, None]), "m0_r2": c(m0("Wr2")), "m0_rb2": c(m0("br2")[None, :]),
        "m1_r": rows(m1("router_w"), P),
    })
    return out


def kernel(**inputs):
    import concourse.bacc as _bacc
    from concourse.bass_utils import run_bass_kernel_spmd as _run

    nc = _bacc.Bacc("TRN2", target_bir_lowering=False, num_devices=1)
    arrays, aps = {}, {}
    for name, a in host_layouts(inputs).items():
        arrays[f"in_{name}"] = a
        aps[name] = nc.dram_tensor(f"in_{name}", a.shape, mybir.dt.from_np(a.dtype), kind="ExternalInput").ap()
    out = nc.dram_tensor("out", (TOK, D), FP, kind="ExternalOutput").ap()
    build(nc, aps, out)
    r = _run(nc, [arrays], core_ids=[0])
    return r.results[0]["out"].reshape(NB, SEQ, D)
```

```python
from contextlib import ExitStack

import concourse.bass as bass
from concourse import mybir

FP = mybir.dt.float32
FR = mybir.dt.float32r
I32 = mybir.dt.int32
ALU = mybir.AluOpType
ACT = mybir.ActivationFunctionType
AX = mybir.AxisListType



P = 128
NB, SEQ, D = 2, 1024, 256
TOK = NB * SEQ
NT = TOK // P
DK = D // P
KEYS, IPA, DC = 77, 4, 192
CP, CK = 96, 2
RANK = 32
E, TOPK = 8, 2
ST = 256
ROUTED = (TOK * TOPK + E * (ST - 1)) // ST
EPS = 1e-5
LOW = 32
SPLIT = LOW + 1

class Layer:

    def __init__(self, n, heads, dh, segments, lora, hid, shared, func):
        self.n, self.heads, self.dh, self.segments = n, heads, dh, segments
        self.lora, self.hid, self.shared, self.func = lora, hid, shared, func
        self.scale = dh ** -0.5
        self.hp = P // dh
        self.groups = heads // self.hp
        self.n_g = self.hp * KEYS
        self.cols = heads * KEYS
        self.chunks = -(-self.cols // P)
        self.pad = self.chunks * P
        banks = -(-self.cols // 512)
        self.banks, self.piece = (banks, self.cols // banks) if heads % banks == 0 else (1, 512)
        self.c0 = [g * self.n_g // P for g in range(self.groups)]
        self.win = [P * (((g + 1) * self.n_g - 1) // P - self.c0[g] + 1) for g in range(self.groups)]
        self.m1 = hid // P
        self.sh_tiles = TOK // ST if shared else 0
        self.tiles = ROUTED + self.sh_tiles


LAYERS = [
    Layer(0, 16, 64, [(0, KEYS - IPA), (KEYS - IPA, KEYS)], True, 1024, True, ACT.Silu),
    Layer(1, 8, 32, [(0, KEYS)], False, 256, False, ACT.Gelu_apprx_tanh),
]


class Shared:
    pass


def wait(eng, sem, value):
    if not isinstance(value, int) or value > 0:
        eng.wait_ge(sem, value)


def one(ap, i):
    return ap[:, i:i + 1] if isinstance(i, int) else ap[:, bass.ds(i, 1)]


def product(nc, out, lhs, rhs, start, stop):
    (lh, ll), (rh, rl) = lhs, rhs
    nc.tensor.matmul(out, lh, rh, start=start, stop=False)
    nc.tensor.matmul(out, lh, rl, start=False, stop=False)
    return nc.tensor.matmul(out, ll, rh, start=False, stop=stop)


class Prepare:

    def __init__(self, nc, g, x, sem):
        self.nc, self.g, self.x = nc, g, x
        self.s_x, self.s_c, self.s_st = sem("prep_x_loaded"), sem("prep_const"), sem("prep_stats")
        self.s_zf = sem("prep_zero_tile")

    def load(self, sp):
        sp.dma_start(self.g.X[:], self.x.rearrange("(t p) d -> p t d", p=P)).then_inc(self.s_x, 16)

    def zero_slots(self, sp):
        rows = self.g.xs.rearrange("(a p) d -> p a d", p=P)
        sp.wait_ge(self.s_zf, 1)
        for a in range(0, rows.shape[1], 2):
            sp.dma_start(rows[:, a:a + 2, :], self.g.zero[:].rearrange("p (a d) -> p a d", a=2)).then_inc(self.g.s_zeroed, 16)

    def constants(self, pool):
        g, gp = self.g, self.nc.gpsimd
        gp.memset(g.ident[:], 0.0).then_inc(self.s_c, 1)
        gp.memset(g.before[:], 1.0).then_inc(self.s_c, 1)
        gp.memset(g.ones[:], 1.0).then_inc(self.s_c, 1)
        pool.wait_ge(self.s_c, 3)
        gp.affine_select(out=g.ident[:], in_=g.ident[:], compare_op=ALU.not_equal, fill=1.0,
                         base=0, pattern=[[-1, P]], channel_multiplier=1).then_inc(self.s_c, 1)
        gp.affine_select(out=g.before[:], in_=g.before[:], compare_op=ALU.is_gt, fill=0.0,
                         base=0, pattern=[[1, P]], channel_multiplier=-1).then_inc(self.s_c, 1)
        gp.iota(g.iota_e[:], pattern=[[0, NT], [1, E]], base=0, channel_multiplier=0,
                allow_small_or_imprecise_dtypes=True).then_inc(self.s_c, 1)
        gp.iota(g.iota_thr[:], pattern=[[0, E], [ST, TOK // ST]], base=0, channel_multiplier=0,
                allow_small_or_imprecise_dtypes=True).then_inc(self.s_c, 1)
        gp.iota(g.iota_tile[:], pattern=[[1, ROUTED], [0, E]], base=0, channel_multiplier=0,
                allow_small_or_imprecise_dtypes=True).then_inc(self.s_c, 1)
        gp.memset(g.zero[:], 0.0).then_inc(self.s_zf, 1)

    def ones(self, dve):
        dve.wait_ge(self.s_c, 8)
        self.nc.vector.tensor_copy(self.g.ones_r[:], self.g.ones[0:SPLIT, :]).then_inc(self.s_st, 1)

    def tile_statistics(self, dve, t):
        if t == 0:
            dve.wait_ge(self.s_x, 16)
        self.nc.vector.bn_stats(self.g.stats[:, t, :], self.g.X[:, t, :]).then_inc(self.s_st, 1)

    def statistics(self, dve):
        g, v = self.g, self.nc.vector
        dve.wait_ge(self.s_st, 1 + NT)
        for t in range(NT):
            last = v.bn_aggr(g.mv[:, t, :], g.stats[:, t, :])
        last.then_inc(self.s_st, 1)
        dve.wait_ge(self.s_st, 2 + NT)


class InverseDeviation:

    def __init__(self, nc, g, sem, tag):
        self.nc, self.g = nc, g
        self.s_v, self.s_q, self.s_r = sem(tag + "_var_eps"), sem(tag + "_sqrt"), sem(tag + "_chain")

    def act(self, act):
        act.wait_ge(self.s_v, 1)
        self.nc.scalar.activation(self.g.sq[:], self.g.ve[:], ACT.Sqrt).then_inc(self.s_q, 1)

    def dve(self, dve):
        g, v, s_r = self.g, self.nc.vector, self.s_r
        v.tensor_scalar(g.ve[:], g.mv[:, :, 1], EPS, None, ALU.add).then_inc(self.s_v, 1)
        dve.wait_ge(self.s_q, 1)
        v.reciprocal(g.rstd[:], g.sq[:]).then_inc(s_r, 1)
        dve.wait_ge(s_r, 1)
        v.tensor_tensor(g.sq[:], g.rstd[:], g.rstd[:], ALU.mult).then_inc(s_r, 1)
        dve.wait_ge(s_r, 2)
        v.tensor_tensor(g.sq[:], g.sq[:], g.ve[:], ALU.mult).then_inc(s_r, 1)
        dve.wait_ge(s_r, 3)
        v.tensor_scalar(g.sq[:], g.sq[:], -0.5, 1.5, ALU.mult, ALU.add).then_inc(s_r, 1)
        dve.wait_ge(s_r, 4)
        v.tensor_tensor(g.rstd[:], g.rstd[:], g.sq[:], ALU.mult).then_inc(s_r, 1)
        dve.wait_ge(s_r, 5)


def attention_setup(nc, g, L, w, sem, prepare, before):
    T = f"as{L.n}_"
    s_wq, s_lq = sem(T + "wq_wo_loaded"), sem(T + "low_rank_loaded")
    deviation = InverseDeviation(nc, g, sem, T + "ln")
    s_w, s_wk, s_wv = sem(T + "context_loaded"), sem(T + "wk_loaded"), sem(T + "wv_loaded")
    s_mask = sem(T + "context_masked")
    s_zero, s_al = sem(T + "zeroed"), sem(T + "alpha")
    s_lk, s_lk_sb = sem(T + "ctx_lora"), sem(T + "ctx_lora_copied")
    s_kv, s_bd = sem(T + "kv"), sem(T + "block_diagonal")
    s_u, s_u_sb = sem(T + "low_rank"), sem(T + "low_rank_copied")
    s_a, s_ahi, s_alo = sem(T + "a"), sem(T + "a_high"), sem(T + "a_low")
    s_b, s_bhi, s_blo = sem(T + "b"), sem(T + "b_high"), sem(T + "b_low")
    s_r = sem(T + "rows")
    G, n, hp, dh = L.groups, L.n_g, L.hp, L.dh
    HD = L.heads * dh
    org = KEYS - IPA
    KA = min(DK, 512 // n)
    with ExitStack() as ctx:
        sb = lambda name, shape, dt=FP: ctx.enter_context(nc.sbuf_tensor(T + name, shape, dt))
        pb = lambda name, shape: ctx.enter_context(nc.psum_tensor(T + name, shape, FP))
        c = sb("ctx", [CP, CK, NB, KEYS])
        wk, wv = sb("wk", [CP, CK, HD]), sb("wv", [CP, CK, HD])
        wq, wo = sb("wq", [P, G, D]), sb("wo", [P, G, D])
        bo = sb("bo", [1, D])
        loads, loads_k, loads_v = [(c, w["ctx"])], [(wk, w["wk"])], [(wv, w["wv"])]
        loads_q, loads_lq = [(wq, w["wq"]), (wo, w["wo"]), (bo, w["bo"])], []
        if L.lora:
            ci = sb("ctx_ipa", [CP, CK, NB, KEYS])
            loads.append((ci, w["ctx"]))
            wki, wvi = sb("wki", [CP, CK, HD]), sb("wvi", [CP, CK, HD])
            kd, vd = sb("kd", [CP, CK, RANK]), sb("vd", [CP, CK, RANK])
            ku, vu = sb("ku", [RANK, HD]), sb("vu", [RANK, HD])
            qu, qd = sb("qu", [RANK, HD]), sb("qd", [RANK, D])
            od, ou = sb("od", [RANK, HD]), sb("ou", [RANK, D])
            al = sb("al", [RANK, 4])
            loads = [(kd, w["kd"]), (vd, w["vd"]), (al, w["alphas"].to_broadcast([RANK, 4]))] + loads
            loads_k += [(ku, w["ku"]), (wki, w["wki"])]
            loads_v += [(vu, w["vu"]), (wvi, w["wvi"])]
            loads_lq = [(qu, w["qu"]), (qd, w["qd"]), (od, w["od"]), (ou, w["ou"])]
            low = sb("low", [RANK, 2, NB, KEYS])
        else:
            bq, bk, bv = sb("bq", [P, G]), sb("bk", [P, G]), sb("bv", [P, G])
            loads_k.append((bk, w["bk"]))
            loads_v.append((bv, w["bv"]))
            loads_q += [(bq, w["bq"])]
        kbd = sb("kbd", [P, G, NB, n])
        vbd = sb("vbd", [P, NB, sum(L.win)])
        ps_kv = pb("ps_kv", [P, 2, 2, 256])
        ps_u = pb("ps_u", [P, 2, 512])
        ps_a = pb("ps_a", [P, 2, 512])
        ps_b = pb("ps_b", [P, 2, 2, D])
        half_a = lambda i: ps_a[:, i % 2, 0:KA * n].rearrange("p (k j) -> p k j", k=KA)
        base = [sum(L.win[:gi]) for gi in range(G)]
        off = [base[gi] + gi * n - P * L.c0[gi] for gi in range(G)]
        a_items = [(b, k) for b in range(NB) for k in range(0, DK, KA)]
        b_items = [(b, ch, min(2, L.chunks - ch)) for b in range(NB) for ch in range(0, L.chunks, 2)]

        with nc.Block() as block:
            @block.sync
            def _(sp):
                for group, loaded in ((loads, s_w), (loads_k, s_wk), (loads_v, s_wv), (loads_lq, s_lq), (loads_q, s_wq)):
                    for dst, src in group:
                        sp.dma_start(dst[:], src).then_inc(loaded, 16)
                if prepare:
                    prepare.load(sp)
                if prepare:
                    prepare.zero_slots(sp)
                if before:
                    before.sync(sp)

            n_u = 2

            @block.tensor
            def _(pe):
                pe.wait_ge(s_w, 16 * len(loads))
                if L.lora:
                    pe.wait_ge(s_mask, 2)
                    for i, down in enumerate((kd, vd)):
                        for k in range(CK):
                            last = nc.tensor.matmul(ps_u[0:RANK, i, 0:NB * KEYS], down[:, k, :], c[:, k], start=k == 0, stop=k == CK - 1)
                        last.then_inc(s_lk, 1)

                def keys_values(gi):
                    wait(pe, s_bd, gi - 1)
                    for i, (main, ipa, up) in enumerate(((wk, wki, ku), (wv, wvi, vu)) if L.lora else ((wk, 0, 0), (wv, 0, 0))):
                        gs = slice(gi * P, gi * P + P)
                        if gi == 0:
                            pe.wait_ge((s_wk, s_wv)[i], 16 * len((loads_k, loads_v)[i]))
                        parts = [(main[:, k, gs], c[:, k]) for k in range(CK)]
                        if L.lora:
                            parts += [(ipa[:, k, gs], ci[:, k]) for k in range(CK)]
                            parts.append((up[:, gs], low[:, i]))
                        for lhs, rhs in parts:
                            if rhs is parts[-1][1] and L.lora and gi == 0 and i == 0:
                                pe.wait_ge(s_lk_sb, 2)
                            last = nc.tensor.matmul(ps_kv[:, gi % 2, i, 0:NB * KEYS], lhs, rhs, start=rhs is parts[0][1],
                                                    stop=rhs is parts[-1][1])
                    last.then_inc(s_kv, 1)

                keys_values(0)
                keys_values(1)
                if L.lora:
                    pe.wait_ge(s_al, 2)
                for gi in range(G):
                    gs = slice(gi * P, gi * P + P)
                    if L.lora:
                        for r, (up, down) in enumerate(((qu, qd), (od, ou))):
                            wait(pe, s_u_sb, gi * n_u + r - 1)
                            nc.tensor.matmul(ps_u[:, r, 0:D], up[:, gs], down[:], start=True, stop=True).then_inc(s_u, 1)
                    if gi + 2 < G:
                        keys_values(gi + 2)
                    if gi == 0:
                        pe.wait_ge(s_wq, 16 * len(loads_q))
                    pe.wait_ge(s_bd, gi + 1)
                    if not L.lora:
                        for b in range(NB):
                            wait(pe, s_u_sb, gi * n_u + b - 1)
                            nc.tensor.matmul(ps_u[0:1, b, 0:n], bq[:, gi:gi + 1], kbd[:, gi, b, :], start=True,
                                             stop=True).then_inc(s_u, 1)
                    else:
                        pe.wait_ge(s_u_sb, gi * n_u + 2)
                    for j, (b, k0) in enumerate(a_items):
                        a = gi * len(a_items) + j
                        wait(pe, s_alo, a - 1)
                        for k in range(k0, k0 + KA):
                            last = nc.tensor.matmul(half_a(a)[:, k - k0, :], wq[:, gi, k * P:(k + 1) * P], kbd[:, gi, b, :],
                                                    start=True, stop=True)
                        last.then_inc(s_a, 1)
                for i, (b, ch0, nch) in enumerate(b_items):
                    wait(pe, s_blo, i - 1)
                    for ch in range(ch0, ch0 + nch):
                        over = [gi for gi in range(G) if gi * n < (ch + 1) * P and (gi + 1) * n > ch * P]
                        for gi in over:
                            v0 = base[gi] + (ch - L.c0[gi]) * P
                            last = nc.tensor.matmul(ps_b[:, i % 2, ch - ch0, :], vbd[:, b, v0:v0 + P], wo[:, gi, :],
                                                    start=gi == over[0], stop=gi == over[-1])
                    last.then_inc(s_b, 1)

            @block.gpsimd
            def _(pool):
                if prepare:
                    prepare.constants(pool)
                if L.lora:
                    nc.gpsimd.memset(kbd[:], 0.0).then_inc(s_zero, 1)
                    nc.gpsimd.memset(g.bo[:].bitcast(FP), 0.0).then_inc(s_zero, 1)
                if before:
                    before.gather(pool)

            @block.vector
            def _(dve):
                if not L.lora:
                    for zeros in (kbd[:], vbd[:], g.bo[:].bitcast(FP), g.row[:].bitcast(FP)):
                        nc.vector.memset(zeros, 0.0).then_inc(s_zero, 1)
                if L.lora:
                    dve.wait_ge(s_w, 16 * len(loads))
                    nc.vector.memset(c[:, :, :, org:], 0.0).then_inc(s_mask, 1)
                    nc.vector.memset(ci[:, :, :, 0:org], 0.0).then_inc(s_mask, 1)
                    nc.vector.tensor_scalar(al[:], al[:], 1.0 / RANK, None, ALU.mult).then_inc(s_al, 1)
                    nc.vector.memset(vbd[:], 0.0).then_inc(s_zero, 1)
                    prepare.ones(dve)
                    dve.wait_ge(s_al, 1)
                    dve.wait_ge(s_lq, 16 * len(loads_lq))
                    nc.vector.tensor_scalar(qd[:], qd[:], al[:, 0:1], None, ALU.mult)
                    nc.vector.tensor_scalar(ou[:], ou[:], al[:, 3:4], None, ALU.mult).then_inc(s_al, 1)
                dve.wait_ge(s_zero, 3 + (not L.lora))

                def block_diagonal(gi):
                    dve.wait_ge(s_kv, gi + 1)
                    for hh in range(hp):
                        rows = slice(dh * hh, dh * (hh + 1))
                        for i in range(2):
                            src = ps_kv[rows, gi % 2, i, 0:NB * KEYS].rearrange("p (b j) -> p b j", b=NB)
                            at = hh * KEYS + (off[gi] if i else 0)
                            dst = vbd[rows, :, at:at + KEYS] if i else kbd[rows, gi, :, at:at + KEYS]
                            if L.lora:
                                last = nc.vector.tensor_copy(dst, src)
                            else:
                                last = nc.vector.tensor_scalar(dst, src, (bv if i else bk)[rows, gi:gi + 1], None, ALU.add)
                    last.then_inc(s_bd, 1)

                added = [0]

                def add_tile():
                    if added[0] < NT:
                        if before:
                            before.add(dve, added[0])
                        else:
                            prepare.tile_statistics(dve, added[0])
                        added[0] += 1

                if not L.lora:
                    dve.wait_ge(s_wk, 16 * len(loads_k))
                    dve.wait_ge(s_wv, 16 * len(loads_v))
                block_diagonal(0)
                block_diagonal(1)
                dve.wait_ge(s_wq, 16 * len(loads_q))
                nc.vector.tensor_copy(g.bo[0:1], bo[:]).then_inc(s_r, 1)
                dve.wait_ge(s_r, 1)
                nc.vector.tensor_tensor(g.bo[LOW:SPLIT], bo[:], g.bo[0:1], ALU.subtract)
                for gi in range(G):
                    if L.lora:
                        for r, dst in enumerate((wq, wo)):
                            dve.wait_ge(s_u, gi * n_u + r + 1)
                            nc.vector.tensor_tensor(dst[:, gi, :], dst[:, gi, :], ps_u[:, r, 0:D], ALU.add).then_inc(s_u_sb, 1)
                    if gi + 2 < G:
                        block_diagonal(gi + 2)
                    if not L.lora:
                        for b in range(NB):
                            u = gi * n_u + b
                            dve.wait_ge(s_u, u + 1)
                            nc.vector.tensor_copy(g.row[0:1, b, gi * n:(gi + 1) * n], ps_u[0:1, u % 2, 0:n]).then_inc(s_r, 1)
                            dve.wait_ge(s_r, 2 + u)
                            nc.vector.tensor_tensor(g.row[LOW:SPLIT, b, gi * n:(gi + 1) * n], ps_u[0:1, u % 2, 0:n],
                                                    g.row[0:1, b, gi * n:(gi + 1) * n], ALU.subtract).then_inc(s_u_sb, 1)
                    for j, (b, k0) in enumerate(a_items):
                        a = gi * len(a_items) + j
                        dve.wait_ge(s_ahi, a + 1)
                        at = (slice(None), b, slice(k0, k0 + KA), slice(gi * n, (gi + 1) * n))
                        nc.vector.tensor_tensor(g.Al[L.n][at], half_a(a), g.Ah[L.n][at], ALU.subtract).then_inc(s_alo, 1)
                        for _ in range(KA):
                            if before or gi > 0:
                                add_tile()
                    if prepare and gi == G - 2:
                        prepare.statistics(dve)
                        deviation.dve(dve)
                for i, (b, ch, nch) in enumerate(b_items):
                    dve.wait_ge(s_bhi, i + 1)
                    nc.vector.tensor_tensor(g.Bl[L.n][:, b, ch:ch + nch, :], ps_b[:, i % 2, 0:nch, :],
                                            g.Bh[L.n][:, b, ch:ch + nch, :], ALU.subtract).then_inc(s_blo, 1)
                    for _ in range(nch):
                        add_tile()
                if before:
                    before.statistics(dve)
                    deviation.dve(dve)

            @block.scalar
            def _(act):
                if L.lora:
                    act.wait_ge(s_al, 1)
                    for i in range(2):
                        act.wait_ge(s_lk, i + 1)
                        nc.scalar.activation(low[:, i], ps_u[0:RANK, i, 0:NB * KEYS].rearrange("p (b j) -> p b j", b=NB),
                                             ACT.Copy, scale=al[:, 1 + i:2 + i]).then_inc(s_lk_sb, 1)
                for gi in range(G):
                    for j, (b, k0) in enumerate(a_items):
                        a = gi * len(a_items) + j
                        act.wait_ge(s_a, a + 1)
                        nc.scalar.copy(g.Ah[L.n][:, b, k0:k0 + KA, gi * n:(gi + 1) * n], half_a(a)).then_inc(s_ahi, 1)
                    if prepare and gi == G - 2:
                        deviation.act(act)
                for i, (b, ch, nch) in enumerate(b_items):
                    act.wait_ge(s_b, i + 1)
                    nc.scalar.copy(g.Bh[L.n][:, b, ch:ch + nch, :], ps_b[:, i % 2, 0:nch, :]).then_inc(s_bhi, 1)
                if before:
                    deviation.act(act)


def attention(nc, g, L, sem):
    T = f"at{L.n}_"
    s_xn, s_xt, s_xhi, s_xlo = sem(T + "xn"), sem(T + "x_transposed"), sem(T + "x_high"), sem(T + "x_low")
    s_s, s_mx, s_sub, s_exp = sem(T + "scores"), sem(T + "max"), sem(T + "shifted"), sem(T + "exp")
    s_sum, s_inv, s_pn = sem(T + "sum"), sem(T + "inverse"), sem(T + "probs")
    s_pt, s_phi, s_plo = sem(T + "probs_transposed"), sem(T + "probs_high"), sem(T + "probs_low")
    s_o, s_res, s_bn, s_pad, s_aggr = sem(T + "out"), sem(T + "residual"), sem(T + "bn"), sem(T + "pad"), sem(T + "aggr")
    H, NS, CH = L.heads, len(L.segments), L.chunks
    with ExitStack() as ctx:
        sb = lambda name, shape, dt=FP: ctx.enter_context(nc.sbuf_tensor(T + name, shape, dt))
        pb = lambda name, shape: ctx.enter_context(nc.psum_tensor(T + name, shape, FP))
        xn = sb("xn", [P, 2, D])
        xh, xl = sb("xh", [P, 2, DK, P], FR), sb("xl", [P, 2, DK, P], FR)
        sm = sb("sm", [P, L.cols])
        pr = sb("pr", [P, 2, L.pad])
        mx, su, inv = sb("mx", [P, H, NS]), sb("su", [P, H, NS]), sb("inv", [P, H, NS])
        ph, pl = sb("ph", [P, CH, P], FR), sb("pl", [P, CH, P], FR)
        ps_x = pb("ps_x", [P, 512])
        ps_s = pb("ps_s", [P, 512 * (-(-L.cols // 512))])
        ps_p = pb("ps_p", [P, 512 * (-(-L.pad // 512))])
        ps_o = pb("ps_o", [P, 512])
        NK, HB = L.banks, H // L.banks
        banked = ps_s[:].rearrange("p (b x) -> p b x", b=NK)[:, :, 0:L.cols // NK]
        scores = banked.rearrange("p b (h j) -> p b h j", j=KEYS)
        shifted = sm[:, :].rearrange("p (b h j) -> p b h j", b=NK, j=KEYS)
        maxima = mx[:].rearrange("p (b h) s -> p b h s", b=NK)
        probs_t = ps_p[:, 0:L.pad].rearrange("p (c t) -> p c t", t=P)
        Ah, Al, Bh, Bl = g.Ah[L.n], g.Al[L.n], g.Bh[L.n], g.Bl[L.n]
        parts = (slice(0, 4), slice(4, CH))

        def steps(eng, body, cuts):
            for lo, hi in cuts:
                if hi - lo < 4:
                    for t in range(lo, hi):
                        body(t, t % 2)
                else:
                    with eng.Fori(lo, hi - 1, 2) as i:
                        body(i, lo % 2)
                        body(i + 1, (lo + 1) % 2)

        with nc.Block() as block:
            @block.tensor
            def _(pe):
                def transpose_x(t, q):
                    wait(pe, s_xn, t + 1)
                    wait(pe, s_xlo, t)
                    for k in range(DK):
                        last = nc.tensor.transpose(ps_x[:, k * P:(k + 1) * P], xn[:, q, k * P:(k + 1) * P], g.ident[:])
                    last.then_inc(s_xt, 1)

                def make(b_s, b_o):
                    def step(t, q):
                        static = isinstance(t, int)
                        if not static or t + 1 < NT:
                            wait(pe, s_xlo, t + 2)
                            wait(pe, s_sub, t + 1)
                            for i, c0 in enumerate(range(0, L.cols, L.piece)):
                                c1 = min(c0 + L.piece, L.cols)
                                o = ps_s[:, 512 * i:512 * i + c1 - c0]
                                for k in range(DK):
                                    last = product(nc, o, (xh[:, 1 - q, k, :], xl[:, 1 - q, k, :]),
                                                   (Ah[:, b_s, k, c0:c1], Al[:, b_s, k, c0:c1]), k == 0, L.lora and k == DK - 1)
                                if not L.lora:
                                    last = nc.tensor.matmul(o, g.ones_r[:], g.row[:, b_s, c0:c1], start=False, stop=True)
                            last.then_inc(s_s, 1)
                        if not static or t + 2 < NT:
                            transpose_x(t + 2, q)
                        if not static or t >= 1:
                            wait(pe, s_res, t - 1)
                            nc.tensor.matmul(ps_o[:, 0:D], g.ones_r[:], g.bo[:], start=True, stop=False)
                            for ch in range(CH):
                                for i, cs in enumerate(parts):
                                    if ch == cs.start:
                                        wait(pe, s_plo, 2 * t + i - 1)
                                last = product(nc, ps_o[:, 0:D], (ph[:, ch, :], pl[:, ch, :]),
                                               (Bh[:, b_o, ch, :], Bl[:, b_o, ch, :]), False, ch == CH - 1)
                            last.then_inc(s_o, 1)
                        if not static or 0 <= t < NT:
                            wait(pe, s_pn, t + 1)
                            wait(pe, s_plo, 2 * t)
                            for ch in range(CH):
                                last = nc.tensor.transpose(probs_t[:, ch, :], pr[:, q, ch * P:(ch + 1) * P], g.ident[:])
                            last.then_inc(s_pt, 1)
                    return step

                pe.wait_ge(s_pad, 1)
                transpose_x(0, 0)
                h = NT // NB
                steps(pe, make(0, 0), [(-1, 1), (1, 3), (3, h - 1)])
                steps(pe, make(1, 0), [(h - 1, h + 1)])
                steps(pe, make(1, 1), [(h + 1, NT - 3), (NT - 3, NT - 1), (NT - 1, NT + 1)])

            @block.vector
            def _(dve):
                def normalise(t, q):
                    if isinstance(t, int) and t < 2:
                        pass
                    else:
                        wait(dve, s_xt, t - 1)
                    nc.vector.tensor_scalar(xn[:, q:q + 1, :], one(g.X, t), one(g.mv[:, :, 0], t), one(g.rstd, t),
                                            ALU.subtract, ALU.mult).then_inc(s_xn, 1)

                def low_x(t, q):
                    wait(dve, s_xhi, t + 1)
                    nc.vector.tensor_tensor(xl[:, q], ps_x[:, 0:D].rearrange("p (k t) -> p k t", k=DK), xh[:, q],
                                            ALU.subtract).then_inc(s_xlo, 1)

                def step(t, q):
                    static = isinstance(t, int)
                    if not static or t + 1 < NT:
                        wait(dve, s_s, t + 2)
                        for i, (j0, j1) in enumerate(L.segments):
                            nc.vector.tensor_reduce(maxima[:, :, :, i:i + 1], scores[:, :, :, j0:j1], AX.X, ALU.max).then_inc(s_mx, 1)
                        wait(dve, s_mx, NS * (t + 2))
                        wait(dve, s_exp, t + 1)
                        for i, (j0, j1) in enumerate(L.segments):
                            last = nc.vector.tensor_tensor(shifted[:, :, :, j0:j1], scores[:, :, :, j0:j1],
                                                           maxima[:, :, :, i:i + 1].to_broadcast([P, NK, HB, j1 - j0]), ALU.subtract)
                        last.then_inc(s_sub, 1)
                    if not static or t + 2 < NT:
                        low_x(t + 2, q)
                    if not static or t >= 1:
                        wait(dve, s_o, t)
                        x = one(g.X, t - 1)
                        nc.vector.tensor_tensor(x, x, ps_o[:, 0:D].rearrange("p (a d) -> p a d", a=1),
                                                ALU.add).then_inc(s_res, 1)
                        wait(dve, s_res, t)
                        nc.vector.bn_stats(one(g.stats, t - 1), one(g.X, t - 1)).then_inc(s_bn, 1)
                    if not static or t + 1 < NT:
                        wait(dve, s_exp, t + 2)
                        wait(dve, s_pn, t + 1)
                        e = pr[:, 1 - q, 0:L.cols].rearrange("p (h j) -> p h j", h=H)
                        for i, (j0, j1) in enumerate(L.segments):
                            nc.vector.tensor_reduce(su[:, :, i:i + 1], e[:, :, j0:j1], AX.X, ALU.add).then_inc(s_sum, 1)
                        wait(dve, s_sum, NS * (t + 2))
                        nc.vector.reciprocal(inv[:], su[:]).then_inc(s_inv, 1)
                    if not static or t + 3 < NT:
                        normalise(t + 3, 1 - q)
                    if not static or 0 <= t < NT:
                        for i, cs in enumerate(parts):
                            wait(dve, s_phi, 2 * t + i + 1)
                            nc.vector.tensor_tensor(pl[:, cs], probs_t[:, cs], ph[:, cs], ALU.subtract).then_inc(s_plo, 1)

                nc.vector.memset(pr[:, :, L.cols:], 0.0).then_inc(s_pad, 1)
                normalise(0, 0)
                normalise(1, 1)
                low_x(0, 0)
                steps(dve, step, [(-1, 1), (1, 3), (3, NT - 3), (NT - 3, NT - 1), (NT - 1, NT + 1)])
                dve.wait_ge(s_bn, NT)
                for t in range(NT):
                    nc.vector.bn_aggr(g.mv[:, t, :], g.stats[:, t, :]).then_inc(s_aggr, 1)

            @block.scalar
            def _(act):
                def high_x(t, q):
                    wait(act, s_xt, t + 1)
                    wait(act, s_s, t - 1)
                    nc.scalar.copy(xh[:, q], ps_x[:, 0:D].rearrange("p (k t) -> p k t", k=DK)).then_inc(s_xhi, 1)

                def step(t, q):
                    static = isinstance(t, int)
                    if not static or t + 2 < NT:
                        high_x(t + 2, q)
                    if not static or t + 1 < NT:
                        wait(act, s_sub, t + 2)
                        wait(act, s_pt, t)
                        nc.scalar.activation(pr[:, 1 - q, 0:L.cols], sm[:, :], ACT.Exp, scale=L.scale).then_inc(s_exp, 1)
                    if not static or 0 <= t < NT:
                        wait(act, s_pt, t + 1)
                        wait(act, s_o, t)
                        for cs in parts:
                            nc.scalar.copy(ph[:, cs], probs_t[:, cs]).then_inc(s_phi, 1)

                nc.scalar.preload_act_table(ACT.Exp)
                high_x(0, 0)
                steps(act, step, [(-1, 1), (1, 3), (3, NT - 3), (NT - 3, NT - 1), (NT - 1, NT + 1)])

            @block.gpsimd
            def _(pool):
                def step(t, q):
                    wait(pool, s_inv, t + 1)
                    e = pr[:, q, 0:L.cols].rearrange("p (h j) -> p h j", h=H)
                    for i, (j0, j1) in enumerate(L.segments):
                        last = nc.gpsimd.tensor_tensor(e[:, :, j0:j1], e[:, :, j0:j1],
                                                       inv[:, :, i:i + 1].to_broadcast([P, H, j1 - j0]), ALU.mult)
                    last.then_inc(s_pn, 1)

                with pool.Fori(0, NT - 1, 2) as i:
                    step(i, 0)
                    step(i + 1, 1)


def allocate(nc, ctx, sem):
    sb = lambda name, shape, dt=FP: ctx.enter_context(nc.sbuf_tensor(name, shape, dt))
    g = Shared()
    g.X = sb("X", [P, NT, D])
    g.stats, g.mv = sb("stats", [P, NT, 6]), sb("mean_var", [P, NT, 2])
    g.ve, g.sq, g.rstd = sb("var_eps", [P, NT]), sb("deviation", [P, NT]), sb("rstd", [P, NT])
    g.ident, g.before, g.ones = sb("ident", [P, P]), sb("before", [P, P]), sb("ones", [P, P])
    g.ones_r = sb("ones_r", [SPLIT, P], FR)
    g.iota_e, g.iota_thr = sb("iota_e", [P, NT, E]), sb("iota_thr", [P, E, TOK // ST])
    g.s_zeroed = sem("slots_zeroed")
    g.zero = sb("zero", [P, 2 * D])
    g.iota_tile = sb("iota_tile", [P, ROUTED, E])
    g.xs = nc.dram_tensor("slots_in", [ROUTED * ST, D], FP, kind="Internal").ap()
    g.ys = nc.dram_tensor("slots_out", [ROUTED * ST, D], FP, kind="Internal").ap()
    g.Ah, g.Al, g.Bh, g.Bl = {}, {}, {}, {}
    return g


def attention_operands(nc, ctx, g, L):
    sb = lambda name, shape: ctx.enter_context(nc.sbuf_tensor(f"{name}{L.n}", shape, FR))
    g.Ah[L.n], g.Al[L.n] = sb("A_high", [P, NB, DK, L.cols]), sb("A_low", [P, NB, DK, L.cols])
    g.Bh[L.n], g.Bl[L.n] = sb("B_high", [P, NB, L.chunks, D]), sb("B_low", [P, NB, L.chunks, D])
    g.bo = sb("bo", [SPLIT, D])
    if not L.lora:
        g.row = sb("row", [SPLIT, NB, L.cols])


class Chain:

    def __init__(self, nc, sem, T):
        self.nc, self.sem, self.done = nc, sem(T + "chain"), 0

    def link(self, dve, ins):
        self.done += 1
        ins.then_inc(self.sem, 1)
        dve.wait_ge(self.sem, self.done)

    def prefix(self, dve, bufs, n):
        v, src, to, d = self.nc.vector, bufs[0], 1, 1
        while d < n:
            dst = bufs[to]
            self.link(dve, v.tensor_copy(dst[:, 0:d, :], src[:, 0:d, :]))
            self.link(dve, v.tensor_tensor(dst[:, d:n, :], src[:, d:n, :], src[:, 0:n - d, :], ALU.add))
            src, to, d = dst, 3 - to, 2 * d
        return src


def top_two(nc, g, dve, chain, b):
    v = nc.vector
    e8 = lambda a: a[:].to_broadcast([P, NT, E])
    link = lambda ins: chain.link(dve, ins)
    dve.wait_ge(b.s_ex, 1)
    link(v.tensor_reduce(b.sm[:], b.ex[:], AX.X, ALU.add))
    link(v.reciprocal(b.inv[:], b.sm[:]))
    link(v.tensor_tensor(b.pro[:], b.ex[:], e8(b.inv), ALU.mult))
    link(v.tensor_scalar(b.far[:], g.iota_e[:], float(E), None, ALU.add))

    def choose(p, best, idx, is_it):
        link(v.tensor_reduce(best[:], p[:], AX.X, ALU.max))
        link(v.tensor_tensor(b.eq[:], p[:], e8(best), ALU.is_equal))
        link(v.scalar_tensor_tensor(out=b.tmp[:], in0=b.eq[:], scalar=-float(E), in1=b.far[:], op0=ALU.mult, op1=ALU.add))
        link(v.tensor_reduce(idx[:], b.tmp[:], AX.X, ALU.min))
        link(v.tensor_tensor(is_it[:], g.iota_e[:], e8(idx), ALU.is_equal))

    choose(b.pro, b.p1, b.i1, b.is1)
    link(v.scalar_tensor_tensor(out=b.pro2[:], in0=b.is1[:], scalar=-4.0, in1=b.pro[:], op0=ALU.mult, op1=ALU.add))
    choose(b.pro2, b.p2, b.i2, b.is2)


class Dense:

    CT = 4

    def __init__(self, nc, ctx, g, L, w, sem):
        self.nc, self.g, self.L, self.w, self.sem = nc, g, L, w, sem
        T = self.T = "d_"
        sb = lambda name, shape, dt=FP: ctx.enter_context(nc.sbuf_tensor(T + name, shape, dt))
        self.NC, self.NE, self.W = NT // self.CT, E, DK * L.hid
        C = self.CT * P
        self.xh, self.xl = sb("xh", [P, DK, TOK], FR), sb("xl", [P, DK, TOK], FR)
        self.w1s, self.w2s = sb("w1s", [P, 2, self.W]), sb("w2s", [P, 2, self.W])
        self.w1h, self.w1l = sb("w1h", [P, 2, self.W], FR), sb("w1l", [P, 2, self.W], FR)
        self.w2h, self.w2l = sb("w2h", [P, 2, self.W], FR), sb("w2l", [P, 2, self.W], FR)
        self.b1s, self.b2s = sb("b1s", [P, 2, L.m1]), sb("b2s", [P, E, D])
        self.ex, self.wt = sb("ex", [P, NT, E]), sb("wt", [P, NT, E])
        self.s_w1d, self.s_w2d = ([sem(f"{T}{n}_loaded{q}") for q in range(2)] for n in ("w1", "w2"))
        self.s_w1h, self.s_w1l, self.s_w2h, self.s_w2l = (sem(T + n) for n in ("w1_high", "w1_low", "w2_high", "w2_low"))
        self.s_b1d, self.s_h = [sem(f"{T}b1_loaded{q}") for q in range(2)], sem(T + "hidden")
        self.s_b, self.s_ex = sem(T + "b2_loaded"), sem(T + "exp")

    def load(self, sp, e):
        q = e % 2
        wait(sp, self.s_w1l, e - 1)
        sp.dma_start(self.w1s[:, q, :], self.w["w1"][e]).then_inc(self.s_w1d[q], 16)
        wait(sp, self.s_w2l, e - 1)
        sp.dma_start(self.w2s[:, q, :], self.w["w2"][e]).then_inc(self.s_w2d[q], 16)
        wait(sp, self.s_h, self.L.m1 * self.NC * (e - 1))
        sp.dma_start(self.b1s[:, q, :], self.w["b1"][e]).then_inc(self.s_b1d[q], 16)

    def high_w1(self, act, e, q):
        act.wait_ge(self.s_w1d[q], 8 * e + (8 if q else 16))
        self.nc.scalar.copy(self.w1h[:, q, :], self.w1s[:, q, :]).then_inc(self.s_w1h, 1)

    def high_w2(self, act, e, q):
        act.wait_ge(self.s_w2d[q], 8 * e + (8 if q else 16))
        self.nc.scalar.copy(self.w2h[:, q, :], self.w2s[:, q, :]).then_inc(self.s_w2h, 1)

    def low_w1(self, dve, e, q):
        dve.wait_ge(self.s_w1h, e + 1)
        self.nc.vector.tensor_tensor(self.w1l[:, q, :], self.w1s[:, q, :], self.w1h[:, q, :],
                                     ALU.subtract).then_inc(self.s_w1l, 1)

    def low_w2(self, dve, e, q):
        dve.wait_ge(self.s_w2h, e + 1)
        self.nc.vector.tensor_tensor(self.w2l[:, q, :], self.w2s[:, q, :], self.w2h[:, q, :],
                                     ALU.subtract).then_inc(self.s_w2l, 1)

    def prepare(self):
        nc, g, sem, T, CT, NC = self.nc, self.g, self.sem, self.T, self.CT, self.NC
        C = CT * P
        xh, xl, ex = self.xh, self.xl, self.ex
        deviation = InverseDeviation(nc, g, sem, T + "ln")
        s_w, s_rh, s_rl = sem(T + "router_loaded"), sem(T + "router_high"), sem(T + "router_low")
        s_xn, s_t = sem(T + "xn"), sem(T + "transposed")
        s_xh, s_xl = sem(T + "x_high"), sem(T + "x_low")
        s_r, s_rc, s_lg, s_mx, s_sh = (sem(T + n) for n in ("logits_t", "logits_t_copied", "logits", "max", "shifted"))
        with ExitStack() as ctx:
            sb = lambda name, shape, dt=FP: ctx.enter_context(nc.sbuf_tensor(T + name, shape, dt))
            pb = lambda name, shape: ctx.enter_context(nc.psum_tensor(T + name, shape, FP))
            xn = sb("xn", [P, NT, D])
            rt, rh, rl = sb("router", [P, DK, E]), sb("router_h", [P, DK, E], FR), sb("router_l", [P, DK, E], FR)
            lt, mx, sh = sb("logits_t", [E, 2, C]), sb("mx", [P, NT, 1]), sb("sh", [P, NT, E])
            ps_x = pb("ps_x", [P, 2, DK, C])
            ps_r, ps_l = pb("ps_r", [E, 2, C]), pb("ps_l", [P, NT, E])
            with nc.Block() as block:
                @block.sync
                def _(sp):
                    sp.dma_start(rt[:], self.w["r"]).then_inc(s_w, 16)
                    for e in range(2):
                        self.load(sp, e)
                    sp.dma_start(self.b2s[:], self.w["b2"].rearrange("(a e) d -> a e d", a=1).to_broadcast([P, E, D])
                                 ).then_inc(self.s_b, 16)

                @block.tensor
                def _(pe):
                    def transpose(c):
                        pe.wait_ge(s_xn, CT * (c + 1))
                        wait(pe, s_xl, c - 1)
                        for k in range(DK):
                            for a in range(CT):
                                last = nc.tensor.transpose(ps_x[:, c % 2, k, a * P:(a + 1) * P],
                                                           xn[:, c * CT + a, k * P:(k + 1) * P], g.ident[:])
                        last.then_inc(s_t, 1)

                    def tokens_first(c):
                        pe.wait_ge(s_rc, c + 1)
                        for a in range(CT):
                            last = nc.tensor.transpose(ps_l[:, c * CT + a, :], lt[:, c % 2, a * P:(a + 1) * P], g.ident[0:E, 0:E])
                        last.then_inc(s_lg, 1)

                    transpose(0)
                    pe.wait_ge(s_rl, 1)
                    for c in range(NC):
                        if c + 1 < NC:
                            transpose(c + 1)
                        pe.wait_ge(s_xl, c + 1)
                        for k in range(DK):
                            cs = slice(c * C, (c + 1) * C)
                            last = product(nc, ps_r[:, c % 2, :], (rh[:, k, :], rl[:, k, :]), (xh[:, k, cs], xl[:, k, cs]),
                                           k == 0, k == DK - 1)
                        last.then_inc(s_r, 1)
                        if c >= 1:
                            tokens_first(c - 1)
                    tokens_first(NC - 1)

                @block.scalar
                def _(act):
                    deviation.act(act)
                    nc.scalar.preload_act_table(ACT.Exp)
                    act.wait_ge(s_w, 16)
                    nc.scalar.copy(rh[:], rt[:]).then_inc(s_rh, 1)
                    for c in range(NC + 1):
                        if c < NC:
                            act.wait_ge(s_t, c + 1)
                            nc.scalar.copy(xh[:, :, c * C:(c + 1) * C], ps_x[:, c % 2]).then_inc(s_xh, 1)
                        if c == NC - 2:
                            self.high_w1(act, 0, 0)
                            self.high_w2(act, 0, 0)
                        if c >= 1:
                            act.wait_ge(s_r, c)
                            wait(act, s_lg, c - 2)
                            nc.scalar.copy(lt[:, 1 - c % 2, :], ps_r[:, 1 - c % 2, :]).then_inc(s_rc, 1)
                    act.wait_ge(s_sh, 1)
                    nc.scalar.activation(ex[:], sh[:], ACT.Exp).then_inc(self.s_ex, 1)

                @block.vector
                def _(dve):
                    v = nc.vector
                    deviation.dve(dve)

                    def normalise(c):
                        for t in range(c * CT, (c + 1) * CT):
                            v.tensor_scalar(xn[:, t, :], g.X[:, t, :], g.mv[:, t, 0:1], g.rstd[:, t:t + 1],
                                            ALU.subtract, ALU.mult).then_inc(s_xn, 1)

                    normalise(0)
                    dve.wait_ge(s_rh, 1)
                    v.tensor_tensor(rl[:], rt[:], rh[:], ALU.subtract).then_inc(s_rl, 1)
                    normalise(1)
                    for c in range(NC):
                        dve.wait_ge(s_xh, c + 1)
                        cs = slice(c * C, (c + 1) * C)
                        v.tensor_tensor(xl[:, :, cs], ps_x[:, c % 2], xh[:, :, cs], ALU.subtract).then_inc(s_xl, 1)
                        if c + 2 < NC:
                            normalise(c + 2)
                        if c == NC - 2:
                            self.low_w1(dve, 0, 0)
                            self.low_w2(dve, 0, 0)
                    dve.wait_ge(s_lg, NC)
                    v.tensor_reduce(mx[:], ps_l[:], AX.X, ALU.max).then_inc(s_mx, 1)
                    dve.wait_ge(s_mx, 1)
                    v.tensor_tensor(sh[:], ps_l[:], mx[:].to_broadcast([P, NT, E]), ALU.subtract).then_inc(s_sh, 1)

    def run(self, out):
        nc, g, L, sem, T, CT, NC = self.nc, self.g, self.L, self.sem, self.T, self.CT, self.NC
        C, M1 = CT * P, L.m1
        PAIR = 2 * NC
        xh, xl, wt, b2s = self.xh, self.xl, self.wt, self.b2s
        s_m1, s_hh, s_hl, s_m2 = (sem(T + n) for n in ("first", "hidden_high", "hidden_low", "second"))
        s_h = self.s_h
        s_x, s_wt, s_fin, s_out = (sem(T + n) for n in ("added", "weights", "finished", "stored"))
        chain = Chain(nc, sem, T)
        s_acc, s_term = sem(T + "bias_sum"), sem(T + "bias_term")
        with ExitStack() as ctx:
            sb = lambda name, shape, dt=FP: ctx.enter_context(nc.sbuf_tensor(T + name, shape, dt))
            pb = lambda name, shape: ctx.enter_context(nc.psum_tensor(T + name, shape, FP))
            hf, hh, hl = sb("hf", [P, 2, M1, C]), sb("hh", [P, 2, M1, C], FR), sb("hl", [P, 2, M1, C], FR)
            acc, term = sb("acc", [P, NT, D]), sb("term", [P, NT, D])
            t8, t1 = (lambda n: sb(n, [P, NT, E])), (lambda n: sb(n, [P, NT, 1]))
            self.pro, self.pro2, self.eq, self.tmp, self.far, self.is1, self.is2 = (
                t8(n) for n in ("pro", "pro2", "eq", "tmp", "far", "is1", "is2"))
            self.sm, self.inv, self.p1, self.p2, self.i1, self.i2 = (t1(n) for n in ("sm", "inv", "p1", "p2", "i1", "i2"))
            ps_h, ps_o = pb("ps_h", [P, 2, M1, C]), pb("ps_o", [P, 2, CT, D])

            def steps(eng, body):
                for r in range(PAIR):
                    body(0, r)
                with eng.Fori(1, E // 2 - 1) as i:
                    for r in range(PAIR):
                        body(i, r)
                for r in range(PAIR + 1):
                    body(E // 2 - 1, r)

            with nc.Block() as block:
                @block.sync
                def _(sp):
                    for e in range(2, E):
                        self.load(sp, e)
                    for t in range(NT):
                        sp.wait_ge(s_fin, t + 1)
                        sp.dma_start(out[t * P:(t + 1) * P, :], g.X[:, t, :]).then_inc(s_out, 16)
                    sp.wait_ge(s_out, 16 * NT)

                @block.tensor
                def _(pe):
                    def body(i, r):
                        S = lambda d: PAIR * i + r + d
                        q, half = r % 2, r // NC % 2
                        first_pair = isinstance(i, int) and i == 0
                        if r < PAIR:
                            if r % NC == 0:
                                pe.wait_ge(self.s_w1l, 2 * i + half + 1)
                            cs = slice(r % NC * C, (r % NC + 1) * C)
                            for m in range(M1):
                                if not first_pair or r >= 2:
                                    pe.wait_ge(s_h, M1 * PAIR * i + M1 * (r - 2) + m + 1)
                                for k in range(DK):
                                    ws = slice(k * L.hid + m * P, k * L.hid + (m + 1) * P)
                                    last = product(nc, ps_h[:, q, m, :], (self.w1h[:, half, ws], self.w1l[:, half, ws]),
                                                   (xh[:, k, cs], xl[:, k, cs]), k == 0, k == DK - 1)
                                last.then_inc(s_m1, 1)
                        if not first_pair or r >= 1:
                            half = (r - 1) // NC % 2
                            if (r - 1) % NC == 0:
                                pe.wait_ge(self.s_w2l, 2 * i + half + 1)
                            pe.wait_ge(s_hl, M1 * PAIR * i + M1 * r)
                            for a in range(CT):
                                if a % 2 == 0 and (not first_pair or r >= 3):
                                    pe.wait_ge(s_x, CT * PAIR * i + CT * (r - 3) + a + 2)
                                for m in range(M1):
                                    ts, ds = slice(a * P, (a + 1) * P), slice(m * D, (m + 1) * D)
                                    last = product(nc, ps_o[:, 1 - q, a, :], (hh[:, 1 - q, m, ts], hl[:, 1 - q, m, ts]),
                                                   (self.w2h[:, half, ds], self.w2l[:, half, ds]), m == 0, m == M1 - 1)
                                if a % 2 == 1:
                                    last.then_inc(s_m2, 1)
                    steps(pe, body)

                @block.scalar
                def _(act):
                    def body(i, r):
                        q = r % 2
                        first_pair, last_pair = (isinstance(i, int) and i == n for n in (0, E // 2 - 1))
                        if r == PAIR:
                            return
                        if r % NC == 0:
                            act.wait_ge(self.s_b1d[r // NC], 16 * i + 16)
                        for m in range(M1):
                            act.wait_ge(s_m1, M1 * PAIR * i + M1 * r + m + 1)
                            if not first_pair or r >= 2:
                                act.wait_ge(s_hl, M1 * PAIR * i + M1 * (r - 2) + m + 1)
                            nc.scalar.activation(hf[:, q, m, :], ps_h[:, q, m, :], L.func,
                                                 bias=self.b1s[:, r // NC, m:m + 1]).then_inc(s_h, 1)
                            act.wait_ge(s_h, M1 * PAIR * i + M1 * r + m + 1)
                            if not first_pair or r >= 2:
                                act.wait_ge(s_m2, 2 * PAIR * i + 2 * (r - 1))
                            nc.scalar.copy(hh[:, q, m, :], hf[:, q, m, :]).then_inc(s_hh, 1)
                        half = 1 - r // NC
                        if not (last_pair and r >= NC):
                            if r % NC == 1:
                                if not first_pair or r >= NC:
                                    act.wait_ge(s_m1, M1 * PAIR * i + M1 * (r - 1))
                                self.high_w1(act, 2 * i + r // NC + 1, half)
                            if r % NC == 2:
                                if not first_pair or r >= NC:
                                    act.wait_ge(s_m2, 2 * PAIR * i + 2 * (r - 2))
                                self.high_w2(act, 2 * i + r // NC + 1, half)
                    nc.scalar.preload_act_table(L.func)
                    steps(act, body)

                @block.vector
                def _(dve):
                    v = nc.vector
                    top_two(nc, g, dve, chain, self)
                    chain.link(dve, v.tensor_tensor(self.is1[:], self.is1[:], self.is2[:], ALU.add))
                    v.tensor_tensor(wt[:], self.pro[:], self.is1[:], ALU.mult).then_inc(s_wt, 1)
                    dve.wait_ge(s_wt, 1)

                    def body(i, r):
                        q = r % 2
                        first_pair, last_pair = (isinstance(i, int) and i == n for n in (0, E // 2 - 1))
                        if r < PAIR:
                            if not first_pair or r >= 2:
                                dve.wait_ge(s_m2, 2 * PAIR * i + 2 * (r - 1))
                            for m in range(M1):
                                dve.wait_ge(s_hh, M1 * PAIR * i + M1 * r + m + 1)
                                v.tensor_tensor(hl[:, q, m, :], hf[:, q, m, :], hh[:, q, m, :], ALU.subtract).then_inc(s_hl, 1)
                        if not first_pair or r >= 1:
                            e, n = 2 * i + (r - 1) // NC, (r - 1) % NC
                            if not first_pair or r >= NC + 1:
                                dve.wait_ge(s_x, CT * PAIR * i + CT * (r - NC))
                            for a in range(CT):
                                t = n * CT + a
                                if a % 2 == 0:
                                    dve.wait_ge(s_m2, 2 * PAIR * i + 2 * (r - 1) + a // 2 + 1)
                                weight = wt[:, t, e:e + 1] if isinstance(i, int) else wt[:, t, bass.ds(e, 1)]
                                v.scalar_tensor_tensor(out=g.X[:, t, :], in0=ps_o[:, 1 - q, a, :], scalar=weight,
                                                       in1=g.X[:, t, :], op0=ALU.mult, op1=ALU.add).then_inc(s_x, 1)
                            if last_pair and r >= NC + 1:
                                if n == 0:
                                    dve.wait_ge(s_acc, E - 1)
                                for a in range(CT):
                                    t = n * CT + a
                                    dve.wait_ge(s_x, CT * PAIR * i + CT * (r - 1) + a + 1)
                                    v.tensor_tensor(g.X[:, t, :], g.X[:, t, :], acc[:, t, :], ALU.add).then_inc(s_fin, 1)
                        if r < PAIR and not (last_pair and r >= NC):
                            half = 1 - r // NC
                            if r % NC == 1:
                                self.low_w1(dve, 2 * i + r // NC + 1, half)
                            if r % NC == 2:
                                self.low_w2(dve, 2 * i + r // NC + 1, half)
                    steps(dve, body)

                @block.gpsimd
                def _(pool):
                    shape = [P, NT, D]
                    pool.wait_ge(self.s_b, 16)
                    pool.wait_ge(s_wt, 1)
                    for e in range(E):
                        if e >= 2:
                            pool.wait_ge(s_acc, e - 1)
                        nc.gpsimd.tensor_tensor((term if e else acc)[:], b2s[:, e:e + 1, :].to_broadcast(shape),
                                                wt[:, :, e:e + 1].to_broadcast(shape), ALU.mult).then_inc(s_term, 1)
                        if e:
                            pool.wait_ge(s_term, e + 1)
                            nc.gpsimd.tensor_tensor(acc[:], acc[:], term[:], ALU.add).then_inc(s_acc, 1)


class Route:

    def __init__(self, nc, ctx, g, m, L, w, sem):
        self.nc, self.g, self.m, self.L, self.w, self.sem = nc, g, m, L, w, sem
        T = self.T = f"r{L.n}_"
        sb = lambda name, shape, dt=FP: ctx.enter_context(nc.sbuf_tensor(T + name, shape, dt))
        t8 = lambda name: sb(name, [P, NT, E])
        t1 = lambda name: sb(name, [P, NT, 1])
        self.ex, self.pro, self.pro2, self.eq, self.tmp, self.far = (t8(n) for n in ("ex", "pro", "pro2", "eq", "tmp", "far"))
        self.is1, self.is2, self.both, self.slot = (t8(n) for n in ("is1", "is2", "both", "slot"))
        self.mx, self.sm, self.inv, self.p1, self.p2, self.i1, self.i2, self.ed, self.sf = (
            t1(n) for n in ("mx", "sm", "inv", "p1", "p2", "i1", "i2", "ed", "sf"))
        self.n_e, self.nt_e, self.ends_a, self.ends_b = (sb(n, [P, E, 1]) for n in ("n_e", "nt_e", "ends_a", "ends_b"))
        self.start, self.over = sb("start", [P, 1, E]), sb("over", [P, E, TOK // ST])
        self.past, self.tile_e = sb("past", [1, ROUTED, E]), sb("tile_e", [1, ROUTED, 1])
        self.chain = Chain(nc, sem, T)
        self.s_ex, self.s_cnt, self.s_ct = sem(T + "exp"), sem(T + "choices"), sem(T + "counted")
        self.s_sf, self.s_ed, self.s_num = sem(T + "gate_difference"), sem(T + "gate_exp"), sem(T + "numbered")
        self.s_k, self.s_eid = sem(T + "slots"), sem(T + "tile_experts")

    def logits(self):
        nc, g, m, L, w, sem, T = self.nc, self.g, self.m, self.L, self.w, self.sem, self.T
        s_w, s_xn, s_t, s_xt = sem(T + "weights"), sem(T + "xn"), sem(T + "transposed"), [sem(f"{T}x_copied{k}") for k in range(DK)]
        s_r1, s_relu, s_lg = sem(T + "hidden"), sem(T + "relu"), sem(T + "logits")
        deviation = InverseDeviation(nc, g, sem, T + "ln")
        CT, RH = 4, D // 4
        with ExitStack() as ctx:
            sb = lambda name, shape, dt=FP: ctx.enter_context(nc.sbuf_tensor(T + name, shape, dt))
            pb = lambda name, shape: ctx.enter_context(nc.psum_tensor(T + name, shape, FP))
            xt = sb("xt", [P, 2, DK, CT * P])
            r1, rb1, r2, rb2 = sb("r1", [P, DK, RH]), sb("rb1", [RH, 1]), sb("r2", [RH, E]), sb("rb2", [1, E])
            loads = [(r1, w["r1"]), (rb1, w["rb1"]), (r2, w["r2"]), (rb2, w["rb2"])]
            hid, sh = sb("hid", [RH, 2, CT * P]), sb("sh", [P, NT, E])
            ps_x = pb("ps_x", [P, 2, DK, CT * P])
            ps_r = pb("ps_r", [RH, 2, CT * P])
            ps_l = pb("ps_l", [P, NT, E])
            chunks = NT // CT

            with nc.Block() as block:
                @block.sync
                def _(sp):
                    for dst, src in loads:
                        sp.dma_start(dst[:], src).then_inc(s_w, 16)

                @block.tensor
                def _(pe):
                    def transpose(c):
                        pe.wait_ge(s_xn, CT * (c + 1))
                        for k in range(DK):
                            wait(pe, s_xt[k], c - 1)
                        for k in range(DK):
                            for a in range(CT):
                                last = nc.tensor.transpose(ps_x[:, c % 2, k, a * P:(a + 1) * P],
                                                           m.xn[:, c * CT + a, k * P:(k + 1) * P], g.ident[:])
                        last.then_inc(s_t, 1)

                    def second(c):
                        pe.wait_ge(s_relu, c + 1)
                        for a in range(CT):
                            ts = slice(a * P, (a + 1) * P)
                            nc.tensor.matmul(ps_l[:, c * CT + a, :], hid[:, c % 2, ts], r2[:], start=True, stop=False)
                            last = nc.tensor.matmul(ps_l[:, c * CT + a, :], g.ones[0:1, :], rb2[:], start=False, stop=True)
                        last.then_inc(s_lg, 1)

                    transpose(0)
                    pe.wait_ge(s_w, 16 * len(loads))
                    for c in range(chunks):
                        if c + 1 < chunks:
                            transpose(c + 1)
                        for k in range(DK):
                            pe.wait_ge(s_xt[k], c + 1)
                        for k in range(DK):
                            last = nc.tensor.matmul(ps_r[:, c % 2, :], r1[:, k, :], xt[:, c % 2, k, :], start=k == 0, stop=k == DK - 1)
                        last.then_inc(s_r1, 1)
                        if c >= 1:
                            second(c - 1)
                    second(chunks - 1)

                @block.scalar
                def _(act):
                    deviation.act(act)
                    nc.scalar.preload_act_table(ACT.Exp)
                    for c in range(chunks + 1):
                        if c < chunks:
                            act.wait_ge(s_t, c + 1)
                            wait(act, s_r1, c - 1)
                            nc.scalar.copy(xt[:, c % 2, 0, :], ps_x[:, c % 2, 0, :]).then_inc(s_xt[0], 1)
                        if c >= 1:
                            act.wait_ge(s_r1, c)
                            wait(act, s_lg, c - 2)
                            nc.scalar.activation(hid[:, 1 - c % 2, :], ps_r[:, 1 - c % 2, :], ACT.Relu, bias=rb1[:, 0:1]).then_inc(s_relu, 1)
                    act.wait_ge(self.chain.sem, 2)
                    nc.scalar.activation(self.ex[:], sh[:], ACT.Exp).then_inc(self.s_ex, 1)

                @block.vector
                def _(dve):
                    v = nc.vector
                    deviation.dve(dve)

                    def normalise(c):
                        for t in range(c * CT, (c + 1) * CT):
                            v.tensor_scalar(m.xn[:, t, :], g.X[:, t, :], g.mv[:, t, 0:1], g.rstd[:, t:t + 1],
                                            ALU.subtract, ALU.mult).then_inc(s_xn, 1)

                    normalise(0)
                    normalise(1)
                    for c in range(chunks):
                        dve.wait_ge(s_t, c + 1)
                        wait(dve, s_r1, c - 1)
                        v.tensor_copy(xt[:, c % 2, 1, :], ps_x[:, c % 2, 1, :]).then_inc(s_xt[1], 1)
                        if c + 2 < chunks:
                            normalise(c + 2)
                    v.memset(m.eid[:, 0:L.sh_tiles], E)
                    dve.wait_ge(s_lg, chunks)
                    link = self.chain.link
                    link(dve, v.tensor_reduce(self.mx[:], ps_l[:], AX.X, ALU.max))
                    link(dve, v.tensor_tensor(sh[:], ps_l[:], self.mx[:].to_broadcast([P, NT, E]), ALU.subtract))

    def choose(self, dve):
        v, g, link = self.nc.vector, self.g, self.chain.link
        top_two(self.nc, g, dve, self.chain, self)
        link(dve, v.tensor_tensor(self.both[:], self.is1[:], self.is2[:], ALU.add))
        v.tensor_tensor(self.sf[:], self.p2[:], self.p1[:], ALU.subtract).then_inc(self.s_sf, 1)

    def gate(self, act):
        act.wait_ge(self.s_sf, 1)
        self.nc.scalar.activation(self.ed[:], self.sf[:], ACT.Exp, scale=1.0 / TOPK).then_inc(self.s_ed, 1)

    def count(self, pe, ps_c):
        pe.wait_ge(self.s_sf, 1)
        self.nc.tensor.matmul(ps_c[:, 0], self.g.before[:], self.both[:], start=True, stop=True)
        self.nc.tensor.matmul(ps_c[:, 1], self.g.ones[:], self.both[:], start=True, stop=True).then_inc(self.s_ct, 1)

    def number(self, dve, ps_c):
        v, g, m, c = self.nc.vector, self.g, self.m, self.chain
        link = c.link
        dve.wait_ge(self.s_ed, 1)
        link(dve, v.tensor_scalar(self.sf[:], self.ed[:], 1.0, None, ALU.add))
        link(dve, v.reciprocal(m.wt[:, 0, :], self.sf[:, :, 0]))
        link(dve, v.tensor_tensor(m.wt[:, 1, :], m.wt[:, 0, :], self.ed[:, :, 0], ALU.mult))
        dve.wait_ge(self.s_ct, 1)
        run = (self.pro2, self.eq, self.tmp)
        link(dve, v.memset(run[0][:, 0, :], 0.0))
        link(dve, v.tensor_copy(run[0][:, 1:NT, :], ps_c[:, 1, 0:NT - 1, :]))
        offs = c.prefix(dve, run, NT)
        link(dve, v.tensor_tensor(self.n_e[:, :, 0], offs[:, NT - 1, :], ps_c[:, 1, NT - 1, :], ALU.add))
        link(dve, v.tensor_tensor(self.slot[:], ps_c[:, 0], offs[:], ALU.add))
        link(dve, v.tensor_tensor(self.over[:], self.n_e[:].to_broadcast([P, E, TOK // ST]), g.iota_thr[:], ALU.is_gt))
        v.tensor_reduce(self.nt_e[:], self.over[:], AX.X, ALU.add).then_inc(self.s_num, 1)

    def slots(self, dve):
        v, g, m, L, c = self.nc.vector, self.g, self.m, self.L, self.chain
        link, nt_e, start, past, tile_e = c.link, self.nt_e, self.start, self.past, self.tile_e
        dve.wait_ge(self.s_num, 1)
        ends = c.prefix(dve, (nt_e, self.ends_a, self.ends_b), E)
        link(dve, v.tensor_tensor(start[:, 0, :], ends[:, :, 0], nt_e[:, :, 0], ALU.subtract))
        link(dve, v.tensor_scalar(start[:], start[:], float(ST), None, ALU.mult))
        link(dve, v.tensor_tensor(self.slot[:], self.slot[:], start[:].to_broadcast([P, NT, E]), ALU.add))
        for i, is_it in enumerate((self.is1, self.is2)):
            link(dve, v.tensor_tensor(self.tmp[:], self.slot[:], is_it[:], ALU.mult))
            link(dve, v.tensor_reduce(self.mx[:], self.tmp[:], AX.X, ALU.add))
            v.tensor_copy(m.slots[:, i, :], self.mx[:, :, 0]).then_inc(self.s_k, 1)
        link(dve, v.tensor_tensor(past[:], ends[0:1, :, :].rearrange("p e a -> p a e").to_broadcast([1, ROUTED, E]),
                                  g.iota_tile[0:1], ALU.is_le))
        link(dve, v.tensor_reduce(tile_e[:], past[:], AX.X, ALU.add))
        link(dve, v.tensor_scalar(tile_e[:], tile_e[:], float(E - 1), None, ALU.min))
        v.tensor_copy(m.eid[:, L.sh_tiles:L.tiles], tile_e[:, :, 0]).then_inc(self.s_eid, 1)
        dve.wait_ge(self.s_eid, 1)


def scatter(nc, g, m, pool):
    pool.wait_ge(g.s_zeroed, 16 * ROUTED * ST // P // 2)
    for t in range(NT):
        for i in range(TOPK):
            nc.gpsimd.indirect_dma_start(
                out=g.xs, out_offset=bass.IndirectOffsetOnAxis(ap=m.slots[:, i, t:t + 1], axis=0),
                in_=m.xn[:, t, :], in_offset=None).then_inc(m.s_sc, 16)


def experts(nc, g, m, L, w, sem, router, idle):
    T = f"e{L.n}_"
    s_w1d, s_w2d, s_xl = ([sem(f"{T}{n}_loaded{q}") for q in range(2)] for n in ("w1", "w2", "x"))
    s_b1, s_b2 = sem(T + "b1_loaded"), sem(T + "b2_loaded")
    s_st = [sem(f"{T}stored{q}") for q in range(2)]
    s_w1h, s_w1l, s_w2h, s_w2l = sem(T + "w1_high"), sem(T + "w1_low"), sem(T + "w2_high"), sem(T + "w2_low")
    s_tr, s_xh, s_xlo = sem(T + "x_transposed"), sem(T + "x_high"), sem(T + "x_low")
    s_m1, s_h, s_hh, s_hl = sem(T + "first"), sem(T + "hidden"), sem(T + "hidden_high"), sem(T + "hidden_low")
    s_m2, s_ev, s_sx = sem(T + "second"), sem(T + "evacuated"), sem(T + "shared_added")
    M1, J = L.m1, L.tiles
    MG = 2 if M1 > 2 else 1
    MP = M1 // MG
    W1 = DK * L.hid
    NE = w["w1"].shape[0]
    slots_h = min(4, 2 * MP)
    with ExitStack() as ctx:
        sb = lambda name, shape, dt=FP: ctx.enter_context(nc.sbuf_tensor(T + name, shape, dt))
        pb = lambda name, shape: ctx.enter_context(nc.psum_tensor(T + name, shape, FP))
        w1s, w2s = sb("w1s", [P, 2, W1]), sb("w2s", [P, 2, W1])
        w1h, w1l = sb("w1h", [P, 2, W1], FR), sb("w1l", [P, 2, W1], FR)
        w2h, w2l = sb("w2h", [P, 2, W1], FR), sb("w2l", [P, 2, W1], FR)
        xin = sb("xin", [P, 2, ST // P, D])
        xh, xl = sb("xh", [P, 2, DK, ST], FR), sb("xl", [P, 2, DK, ST], FR)
        hf = sb("hf", [P, M1, ST])
        hh, hl = sb("hh", [P, 2, M1, ST], FR), sb("hl", [P, 2, M1, ST], FR)
        b1s, b2s = sb("b1s", [P, NE, M1]), sb("b2s", [P, NE, D])
        yo = sb("yo", [P, 2, ST // P, D])
        ps_x = pb("ps_x", [P, 2, DK, ST])
        ps_h = pb("ps_h", [P, 4, 2, ST])
        ps_o = pb("ps_o", [P, 2, ST // P, D])
        ps_c = ps_o[:, 1].rearrange("p a d -> p (a d)")[:, 0:2 * NT * E].rearrange("p (s t e) -> p s t e", s=2, t=NT)
        arrived = lambda j, q: 8 * j + (8 if q else 16)
        first = lambda a, q, k, i: a[:, q, k * L.hid + i * P:k * L.hid + (i + 1) * P]
        second = lambda a, q, i: a[:, q, i * D:(i + 1) * D]

        S = L.sh_tiles
        ROWS = ST // P

        def steps(eng, body, lo, hi, cuts=(3, J - 2)):
            for j in range(lo, cuts[0]):
                body(j, j % 2)
            for c0, c1 in zip(cuts, cuts[1:]):
                if c1 - c0 < 4:
                    for j in range(c0, c1):
                        body(j, j % 2)
                else:
                    with eng.Fori(c0, c1 - 1, 2) as i:
                        body(i, c0 % 2)
                        body(i + 1, 1 - c0 % 2)
            for j in range(cuts[-1], hi):
                body(j, j % 2)

        def expert(eng, j):
            return eng.value_load(one(m.eid[0:1, :], j), min_val=0, max_val=NE - 1)

        def low_w1(dve, j, q):
            wait(dve, s_w1h, j + 1)
            nc.vector.tensor_tensor(w1l[:, q, :], w1s[:, q, :], w1h[:, q, :], ALU.subtract).then_inc(s_w1l, 1)

        def low_w2(dve, j, q):
            wait(dve, s_w2h, j + 1)
            nc.vector.tensor_tensor(w2l[:, q, :], w2s[:, q, :], w2h[:, q, :], ALU.subtract).then_inc(s_w2l, 1)

        with nc.Block() as block:
            @block.gpsimd
            def _(pool):
                pool.wait_ge(router.s_k, TOPK)
                scatter(nc, g, m, pool)
                for h in idle:
                    pool.sem_clear(h)

            @block.sync
            def _(sp):
                def of(a, e):
                    return w[a][bass.ds(e, 1)].rearrange("a p n -> p (a n)")

                def make(shared):
                    def step(j, q):
                        static = isinstance(j, int)
                        if not static or j < J:
                            e = expert(sp, j)
                            wait(sp, s_w1l, j - 1)
                            sp.dma_start(w1s[:, q, :], of("w1", e)).then_inc(s_w1d[q], 16)
                            wait(sp, s_tr, j - 1)
                            if shared:
                                t = j * ROWS
                                rows = m.xn[:, t:t + ROWS, :] if static else m.xn[:, bass.ds(t, ROWS), :]
                            else:
                                if static and j == S:
                                    sp.wait_ge(m.s_sc, 16 * NT * TOPK)
                                rows = g.xs.rearrange("(j a p) d -> j p a d", p=P, a=ROWS)
                                rows = rows[j - S] if static else rows[bass.ds(j - S, 1)].rearrange("j p a d -> p (j a) d")
                            sp.dma_start(xin[:, q], rows).then_inc(s_xl[q], 16)
                        if not static or 1 <= j <= J:
                            e = expert(sp, j - 1)
                            wait(sp, s_w2l, j - 2)
                            sp.dma_start(w2s[:, 1 - q, :], of("w2", e)).then_inc(s_w2d[1 - q], 16)
                    return step

                make(True)(0, 0)
                sp.dma_start(b1s[:], w["b1"].rearrange("e p m -> p e m")).then_inc(s_b1, 16)
                make(True)(1, 1)
                sp.dma_start(b2s[:], w["b2"].rearrange("(a e) d -> a e d", a=1).to_broadcast([P, NE, D])).then_inc(s_b2, 16)
                steps(sp, make(True), 2, S, (3, S - 1))
                sp.wait_ge(router.s_eid, 1)
                steps(sp, make(False), S, J + 1, (S + 1, J - 2))

            @block.tensor
            def _(pe):
                def step(j, q):
                    static = isinstance(j, int)
                    if not static or j + 1 < J:
                        wait(pe, s_xl[1 - q], arrived(j + 1, 1 - q))
                        wait(pe, s_xlo, j)
                        for k in range(DK):
                            for a in range(ST // P):
                                last = nc.tensor.transpose(ps_x[:, 1 - q, k, a * P:(a + 1) * P],
                                                           xin[:, 1 - q, a, k * P:(k + 1) * P], g.ident[:])
                        last.then_inc(s_tr, 1)
                    if not static or 0 <= j < J:
                        wait(pe, s_w1l, j + 1)
                        wait(pe, s_xlo, j + 1)
                        for mp in range(MP):
                            wait(pe, s_h, j * MP + mp + 1 - slots_h)
                            for i in range(MG):
                                o = ps_h[:, (q * MP + mp) % 4, i, :]
                                for k in range(DK):
                                    last = product(nc, o, (first(w1h, q, k, MG * mp + i), first(w1l, q, k, MG * mp + i)),
                                                   (xh[:, q, k, :], xl[:, q, k, :]), k == 0, k == DK - 1)
                            last.then_inc(s_m1, 1)
                    if not static or j >= 1:
                        wait(pe, s_hl, MP * j)
                        wait(pe, s_w2l, j)
                        wait(pe, s_ev, j - 2)
                        for a in range(ST // P):
                            o = ps_o[:, 1 - q, a, :]
                            for i in range(M1):
                                ts = slice(a * P, (a + 1) * P)
                                last = product(nc, o, (hh[:, 1 - q, i, ts], hl[:, 1 - q, i, ts]),
                                               (second(w2h, 1 - q, i), second(w2l, 1 - q, i)), i == 0, i == M1 - 1)
                        last.then_inc(s_m2, 1)
                step(-1, 1)
                router.count(pe, ps_c)
                step(0, 0)
                step(1, 1)
                pe.wait_ge(router.s_num, 1)
                steps(pe, step, 2, J + 1)

            @block.scalar
            def _(act):
                def make(shared):
                    def step(j, q):
                        static = isinstance(j, int)
                        if not static or j + 1 < J:
                            wait(act, s_w1d[1 - q], arrived(j + 1, 1 - q))
                            wait(act, s_m1, MP * j)
                            nc.scalar.copy(w1h[:, 1 - q, :], w1s[:, 1 - q, :]).then_inc(s_w1h, 1)
                            wait(act, s_tr, j + 2)
                            nc.scalar.copy(xh[:, 1 - q], ps_x[:, 1 - q]).then_inc(s_xh, 1)
                        if not static or 0 <= j < J:
                            if static and j == 0:
                                act.wait_ge(s_b1, 16)
                            e = expert(act, j)
                            for mp in range(MP):
                                wait(act, s_m1, j * MP + mp + 1)
                                wait(act, s_hl, (j - 1) * MP + mp + 1)
                                for i in range(MG):
                                    c = MG * mp + i
                                    last = nc.scalar.activation(hf[:, c, :], ps_h[:, (q * MP + mp) % 4, i, :], L.func,
                                                                bias=b1s[:, bass.ds(e, 1), c:c + 1])
                                last.then_inc(s_h, 1)
                                wait(act, s_h, j * MP + mp + 1)
                                wait(act, s_m2, j - 1)
                                nc.scalar.copy(hh[:, q, MG * mp:MG * (mp + 1), :], hf[:, MG * mp:MG * (mp + 1), :]).then_inc(s_hh, 1)
                        if not shared and (not static or j - 2 >= S):
                            wait(act, s_ev, j - 1)
                            rows = g.ys.rearrange("(j a p) d -> j p a d", p=P, a=ROWS)
                            n = j - 2 - S
                            rows = rows[n] if static else rows[bass.ds(n, 1)].rearrange("j p a d -> p (j a) d")
                            act.dma_start(rows, yo[:, q]).then_inc(s_st[q], 16)
                    return step

                make(True)(-1, 1)
                router.gate(act)
                nc.scalar.preload_act_table(L.func)
                steps(act, make(True), 0, 3, (3,))
                act.wait_ge(router.s_eid, 1)
                steps(act, make(True), 3, S + 1, (3, S + 1))
                steps(act, make(False), S + 1, J + 2, (S + 3, J - 2))
                for n in (ROUTED - 2, ROUTED - 1):
                    act.wait_ge(s_st[n % 2], arrived(n, n % 2))

            @block.vector
            def _(dve):
                def make(shared):
                    def step(j, q):
                        static = isinstance(j, int)
                        if not static or j + 1 < J:
                            low_w1(dve, j + 1, 1 - q)
                            wait(dve, s_xh, j + 2)
                            nc.vector.tensor_tensor(xl[:, 1 - q], ps_x[:, 1 - q], xh[:, 1 - q], ALU.subtract).then_inc(s_xlo, 1)
                        if not static or 0 <= j < J:
                            for mp in range(MP):
                                wait(dve, s_hh, j * MP + mp + 1)
                                nc.vector.tensor_tensor(hl[:, q, MG * mp:MG * (mp + 1), :], hf[:, MG * mp:MG * (mp + 1), :],
                                                        hh[:, q, MG * mp:MG * (mp + 1), :], ALU.subtract).then_inc(s_hl, 1)
                        if not static or 1 <= j <= J:
                            wait(dve, s_m2, j)
                            if static and j == 1:
                                dve.wait_ge(s_b2, 16)
                            e = expert(dve, j - 1)
                            n = j - 3 - S
                            if not static or n >= 0:
                                if not shared:
                                    wait(dve, s_st[1 - q], arrived(n, 1 - q))
                            nc.vector.tensor_tensor(yo[:, 1 - q], ps_o[:, 1 - q], b2s[:, bass.ds(e, 1), :].to_broadcast([P, ST // P, D]),
                                                    ALU.add).then_inc(s_ev, 1)
                            if shared:
                                wait(dve, s_ev, j)
                                t = (j - 1) * ROWS
                                x = g.X[:, t:t + ROWS, :] if static else g.X[:, bass.ds(t, ROWS), :]
                                nc.vector.tensor_tensor(x, x, yo[:, 1 - q], ALU.add).then_inc(s_sx, 1)
                        if static and j == -1:
                            router.number(dve, ps_c)
                        if static and j == 0:
                            router.slots(dve)
                        if not static or j + 1 < J:
                            wait(dve, s_m2, j)
                            wait(dve, s_w2d[1 - q], arrived(j + 1, 1 - q))
                            nc.vector.tensor_copy(w2h[:, 1 - q, :], w2s[:, 1 - q, :]).then_inc(s_w2h, 1)
                            low_w2(dve, j + 1, 1 - q)
                    return step

                router.choose(dve)
                steps(dve, make(True), -1, S + 1, (3, S + 1))
                steps(dve, make(False), S + 1, J + 1, (S + 3, J - 2))


class Combine:

    NBUF = 4

    def __init__(self, nc, ctx, g, m, L, sem, out):
        self.nc, self.g, self.m, self.L, self.out = nc, g, m, L, out
        T = f"c{L.n}_"
        self.s_g = [sem(f"{T}gathered{q}") for q in range(self.NBUF)]
        self.s_f, self.s_x, self.s_bn, self.s_out = sem(T + "used"), sem(T + "x"), sem(T + "bn"), sem(T + "stored")
        self.y = ctx.enter_context(nc.sbuf_tensor(T + "y", [P, self.NBUF, TOPK, D], FP))

    def gather(self, pool):
        for t in range(NT):
            wait(pool, self.s_f, t + 1 - self.NBUF)
            for i in range(TOPK):
                self.nc.gpsimd.indirect_dma_start(
                    out=self.y[:, t % self.NBUF, i, :], out_offset=None, in_=self.g.ys,
                    in_offset=bass.IndirectOffsetOnAxis(ap=self.m.slots[:, i, t:t + 1], axis=0)).then_inc(self.s_g[t % self.NBUF], 16)

    def sync(self, sp):
        if self.out is not None:
            for t in range(NT):
                sp.wait_ge(self.s_f, t + 1)
                sp.dma_start(self.out[t * P:(t + 1) * P, :], self.g.X[:, t, :]).then_inc(self.s_out, 16)
            sp.wait_ge(self.s_out, 16 * NT)

    def add(self, dve, t):
        v, q = self.nc.vector, t % self.NBUF
        dve.wait_ge(self.s_g[q], 16 * TOPK * (t // self.NBUF + 1))
        x = self.g.X[:, t, :]
        for i in range(TOPK):
            done, n = (self.s_f, t + 1) if i == TOPK - 1 else (self.s_x, t + 1)
            v.scalar_tensor_tensor(out=x, in0=self.y[:, q, i, :], scalar=self.m.wt[:, i, t:t + 1],
                                   in1=x, op0=ALU.mult, op1=ALU.add).then_inc(done, 1)
            dve.wait_ge(done, n)
        if self.out is None:
            v.bn_stats(self.g.stats[:, t, :], x).then_inc(self.s_bn, 1)

    def statistics(self, dve):
        dve.wait_ge(self.s_bn, NT)
        for t in range(NT):
            last = self.nc.vector.bn_aggr(self.g.mv[:, t, :], self.g.stats[:, t, :])
        last.then_inc(self.s_bn, 1)
        dve.wait_ge(self.s_bn, NT + 1)


def mixture(nc, g, m, L, w, sem, handles):
    with ExitStack() as ctx:
        m.xn = ctx.enter_context(nc.sbuf_tensor(f"m{L.n}_xn", [P, NT, D], FP))
        idle = [h for h in handles if h is not g.s_zeroed]
        router = Route(nc, ctx, g, m, L, w, sem)
        router.logits()
        m.s_sc = sem(f"m{L.n}_scattered")
        experts(nc, g, m, L, w, sem, router, idle)
        for h in idle:
            nc.release_semaphore(h)


def build(nc, t, out):
    with ExitStack() as ctx:
        handles = []

        def sem(name):
            handles.append(nc.alloc_semaphore(name=name))
            return handles[-1]

        g = allocate(nc, ctx, sem)
        ms = []
        for L in LAYERS:
            sb = lambda name, shape, dt=FP: ctx.enter_context(nc.sbuf_tensor(f"m{L.n}_{name}", shape, dt))
            m = Shared()
            m.wt, m.slots = sb("weights", [P, TOPK, NT]), sb("slots", [P, TOPK, NT], I32)
            m.eid = sb("tile_expert", [1, L.tiles + 1], I32)
            ms.append(m)
        part = lambda p: {k[len(p):]: a for k, a in t.items() if k.startswith(p)}
        for L, m in zip(LAYERS, ms):
            with ExitStack() as attn:
                attention_operands(nc, attn, g, L)
                with ExitStack() as extra:
                    prepare = Prepare(nc, g, t["x"], sem) if L.n == 0 else None
                    before = Combine(nc, extra, g, ms[L.n - 1], LAYERS[L.n - 1], sem, None) if L.n else None
                    attention_setup(nc, g, L, {**part(f"a{L.n}_"), "ctx": t["ctx"]}, sem, prepare, before)
                attention(nc, g, L, sem)
            if L.shared:
                mixture(nc, g, m, L, part(f"m{L.n}_"), sem, handles)
            else:
                with ExitStack() as last:
                    dense = Dense(nc, last, g, L, part(f"m{L.n}_"), sem)
                    dense.prepare()
                    dense.run(out)


def host_layouts(inputs):
    import numpy as np
    c = np.ascontiguousarray
    f = {k: np.asarray(v) for k, v in inputs.items()}
    out = {"x": c(f["x"].reshape(TOK, D))}
    out["ctx"] = c(f["ctx_768"].transpose(2, 0, 1).reshape(CK, CP, NB, KEYS).transpose(1, 0, 2, 3))
    rows = lambda a, p: c(a.reshape(a.shape[0] // p, p, a.shape[1]).transpose(1, 0, 2))
    a0 = lambda k: f["L0_xattn_" + k]
    a1 = lambda k: f["L1_xattn_" + k]
    out.update({
        "a0_wk": rows(a0("Wk"), CP), "a0_wv": rows(a0("Wv"), CP),
        "a0_wki": rows(a0("Wk_ipa"), CP), "a0_wvi": rows(a0("Wv_ipa"), CP),
        "a0_wq": rows(a0("Wq").T, P), "a0_wo": rows(a0("Wo"), P), "a0_bo": c(a0("bo")[None, :]),
        "a0_kd": rows(a0("k_down"), CP), "a0_vd": rows(a0("v_down"), CP),
        "a0_ku": c(a0("k_up")), "a0_vu": c(a0("v_up")),
        "a0_qu": c(a0("q_up")), "a0_qd": c(a0("q_down").T),
        "a0_od": c(a0("o_down").T), "a0_ou": c(a0("o_up")),
        "a0_alphas": c(np.concatenate([a0(k + "_alpha") for k in "qkvo"])[None, :]),
        "a1_wk": rows(a1("Wk").T, CP), "a1_wv": rows(a1("Wv").T, CP),
        "a1_wq": rows(a1("Wq"), P), "a1_wo": rows(a1("Wo").T, P), "a1_bo": c(a1("bo")[None, :]),
        "a1_bq": c(a1("bq").reshape(-1, P).T), "a1_bk": c(a1("bk").reshape(-1, P).T), "a1_bv": c(a1("bv").reshape(-1, P).T),
    })

    def experts(p, w1, b1, w2, b2):
        n, _, hid = w1.shape
        out[p + "w1"] = c(w1.reshape(n, DK, P, hid).transpose(0, 2, 1, 3).reshape(n, P, -1))
        out[p + "b1"] = c(b1.reshape(n, hid // P, P).transpose(0, 2, 1))
        out[p + "w2"] = c(w2.reshape(n, hid // P, P, D).transpose(0, 2, 1, 3).reshape(n, P, -1))
        out[p + "b2"] = c(b2)

    m0 = lambda k: f["L0_ffn_" + k]
    m1 = lambda k: f["L1_ffn_" + k]
    with_shared = lambda e, s: np.concatenate([e, s[None]], axis=0)
    experts("m0_", *(with_shared(m0(e), m0(one)) for e, one in (("We1", "Ws1"), ("be1", "bs1"), ("We2", "Ws2"), ("be2", "bs2"))))
    experts("m1_", m1("w_in"), m1("b_in"), m1("w_out"), m1("b_out"))
    out.update({
        "m0_r1": rows(m0("Wr1"), P), "m0_rb1": c(m0("br1")[:, None]), "m0_r2": c(m0("Wr2")), "m0_rb2": c(m0("br2")[None, :]),
        "m1_r": rows(m1("router_w"), P),
    })
    return out


def kernel(**inputs):
    import concourse.bacc as _bacc
    from concourse.bass_utils import run_bass_kernel_spmd as _run

    nc = _bacc.Bacc("TRN2", target_bir_lowering=False, num_devices=1)
    arrays, aps = {}, {}
    for name, a in host_layouts(inputs).items():
        arrays[f"in_{name}"] = a
        aps[name] = nc.dram_tensor(f"in_{name}", a.shape, mybir.dt.from_np(a.dtype), kind="ExternalInput").ap()
    out = nc.dram_tensor("out", (TOK, D), FP, kind="ExternalOutput").ap()
    build(nc, aps, out)
    r = _run(nc, [arrays], core_ids=[0])
    return r.results[0]["out"].reshape(NB, SEQ, D)
```
